# Optimizing a Trainium2 kernel written in Bass

```python
import numpy as np
import jax
import jax.numpy as jnp

def _softmax(x, axis=-1):
    return jax.nn.softmax(x, axis=axis)

def _gelu(x):
    return jax.nn.gelu(x, approximate=True)

def _silu(x):
    return jax.nn.silu(x)

def _sigmoid(x):
    return jax.nn.sigmoid(x)

def _layernorm(x, axis=-1, eps=1e-05):
    m = jnp.mean(x, axis=axis, keepdims=True)
    v = jnp.var(x, axis=axis, keepdims=True)
    return (x - m) / jnp.sqrt(v + eps)

def _scatter_add(tgt, idx, src, axis=0):
    return tgt.at[idx].add(src)

def _segment_sum(src, seg, n):
    return jax.ops.segment_sum(src, seg, n)
kernel_name = 'mk_early_fusion_d1_tok_img1024_r4_02913f'

def setup_inputs(seed: int=0):
    np.random.seed(seed)
    _w = jnp.asarray

    def _rec_inputs():
        import jax
        import jax.numpy as jnp
        _rk = jax.random.key(seed)
        x = jax.random.uniform(jax.random.fold_in(_rk, 1), (8, 256, 256, 3), jnp.float32, 0.0, 1)
        txt = 0.49943 + 0.166574 * jax.random.normal(jax.random.fold_in(_rk, 2), (8, 128, 256), jnp.float32)
        return (x, txt)
    x, txt = _rec_inputs()

    def _L0_tok_setup():
        import jax, jax.numpy as jnp
        import numpy as np
        NPTS = 16
        NCHANS = 3
        key = jax.random.key(seed)
        k1, k2 = jax.random.split(key)
        x = jax.random.uniform(k1, (4, 256, 256, 3), dtype=jnp.float32)
        ccm = jnp.eye(NCHANS, dtype=jnp.float32) + jax.random.normal(k2, (1,), dtype=jnp.float32)[0] * 0.0001
        ccm_bias = jnp.zeros((NCHANS,), dtype=jnp.float32)
        shifts = jnp.tile(jnp.linspace(0.0, 1.0, NPTS, endpoint=False, dtype=jnp.float32)[None, :], (NCHANS, 1))
        slopes = jnp.zeros((NCHANS, NPTS), dtype=jnp.float32).at[:, 0].set(1.0)
        conv_w = jnp.full((NCHANS, 1), 1.0 / 3.0, dtype=jnp.float32)
        conv_b = jnp.zeros((1,), dtype=jnp.float32)
        return {'x': x, 'ccm': ccm, 'ccm_bias': ccm_bias, 'shifts': shifts, 'slopes': slopes, 'conv_w': conv_w, 'conv_b': conv_b}
    _L0_tok_all = _L0_tok_setup()
    _L0_tok_in = {k: v for k, v in _L0_tok_all.items() if k in ('ccm', 'ccm_bias', 'shifts', 'slopes', 'conv_w', 'conv_b')}
    del _L0_tok_all

    def _L0_attn_setup():
        import jax, jax.numpy as jnp
        import numpy as np
        DIM = 256
        N_HEADS = 16
        HEAD_DIM = DIM // N_HEADS
        D_LATENT = 64
        B, T = (1, 1024)
        key = jax.random.key(seed)
        ks = jax.random.split(key, 6)
        s = 0.02
        return {'x': jax.random.normal(ks[0], (B, T, DIM), dtype=jnp.float32), 'W_DKV': jax.random.normal(ks[1], (DIM, D_LATENT), dtype=jnp.float32) * s, 'W_UK': jax.random.normal(ks[2], (D_LATENT, DIM), dtype=jnp.float32) * s, 'W_UV': jax.random.normal(ks[3], (D_LATENT, DIM), dtype=jnp.float32) * s, 'W_UQ': jax.random.normal(ks[4], (DIM, DIM), dtype=jnp.float32) * s, 'W_O': jax.random.normal(ks[5], (DIM, DIM), dtype=jnp.float32) * s}
    _L0_attn_all = _L0_attn_setup()
    _L0_attn_in = {k: v for k, v in _L0_attn_all.items() if k in ('W_DKV', 'W_UK', 'W_UV', 'W_UQ', 'W_O')}
    del _L0_attn_all

    def _L0_ffn_setup():
        import jax, jax.numpy as jnp
        import numpy as np
        NUM_EXPERTS = 8
        TOP_K = 2
        CAPACITY_FACTOR = 1.0

        def _dispatch_compute(xf, top_expert, w1, w2, capacity):
            tokens, hs = xf.shape
            tpe = jnp.bincount(top_expert, length=NUM_EXPERTS)
            indices = jnp.argsort(top_expert)
            offsets = jnp.concatenate([jnp.zeros((1,), tpe.dtype), jnp.cumsum(tpe)[:-1]])
            slot = jnp.arange(capacity)
            pos = offsets[:, None] + slot[None, :]
            valid = slot[None, :] < tpe[:, None]
            tok_idx = indices[jnp.minimum(pos, tokens - 1)]
            xe = jnp.where(valid[..., None], xf[tok_idx], 0.0)
            h = jax.nn.gelu(jnp.einsum('ech,ehf->ecf', xe, w1), approximate=True)
            ye = jnp.einsum('ecf,efh->ech', h, w2)
            tok_safe = jnp.where(valid, tok_idx, tokens)
            out = jnp.zeros((tokens + 1, hs), xf.dtype).at[tok_safe.reshape(-1)].add(ye.reshape(-1, hs))
            return out[:tokens]
        key = jax.random.key(seed)
        k1, k2, k3, k4 = jax.random.split(key, 4)
        hs, ffn = (256, 1024)
        x = jax.random.normal(k1, (512, 2, hs), dtype=jnp.float32)
        router_w = jax.random.normal(k2, (hs, NUM_EXPERTS), dtype=jnp.float32) * hs ** (-0.5)
        w1 = jax.random.normal(k3, (NUM_EXPERTS, hs, ffn), dtype=jnp.float32) * 0.02
        w2 = jax.random.normal(k4, (NUM_EXPERTS, ffn, hs), dtype=jnp.float32) * 0.02
        bias = jnp.zeros((1, 1, hs), dtype=jnp.float32)
        return {'x': x, 'router_w': router_w, 'w1': w1, 'w2': w2, 'bias': bias}
    _L0_ffn_all = _L0_ffn_setup()
    _L0_ffn_in = {k: v for k, v in _L0_ffn_all.items() if k in ('router_w', 'w1', 'w2', 'bias')}
    del _L0_ffn_all
    return {'x': x, 'txt': txt, 'L0_tok_ccm': _L0_tok_in['ccm'], 'L0_tok_ccm_bias': _L0_tok_in['ccm_bias'], 'L0_tok_shifts': _L0_tok_in['shifts'], 'L0_tok_slopes': _L0_tok_in['slopes'], 'L0_tok_conv_w': _L0_tok_in['conv_w'], 'L0_tok_conv_b': _L0_tok_in['conv_b'], 'L0_attn_W_DKV': _L0_attn_in['W_DKV'], 'L0_attn_W_UK': _L0_attn_in['W_UK'], 'L0_attn_W_UV': _L0_attn_in['W_UV'], 'L0_attn_W_UQ': _L0_attn_in['W_UQ'], 'L0_attn_W_O': _L0_attn_in['W_O'], 'L0_ffn_router_w': _L0_ffn_in['router_w'], 'L0_ffn_w1': _L0_ffn_in['w1'], 'L0_ffn_w2': _L0_ffn_in['w2'], 'L0_ffn_bias': _L0_ffn_in['bias']}

def reference(x, txt, L0_tok_ccm, L0_tok_ccm_bias, L0_tok_shifts, L0_tok_slopes, L0_tok_conv_w, L0_tok_conv_b, L0_attn_W_DKV, L0_attn_W_UK, L0_attn_W_UV, L0_attn_W_UQ, L0_attn_W_O, L0_ffn_router_w, L0_ffn_w1, L0_ffn_w2, L0_ffn_bias):
    import jax
    import jax.numpy as jnp

    def _L0_tok_ref(x, ccm, ccm_bias, shifts, slopes, conv_w, conv_b):
        import jax, jax.numpy as jnp
        import numpy as np
        NPTS = 16
        NCHANS = 3
        g = jnp.einsum('bhwc,cd->bhwd', x, ccm) + ccm_bias
        g = jnp.sum(slopes * jax.nn.relu(g[..., None] - shifts), axis=-1)
        g = jnp.einsum('bhwc,co->bhwo', g, conv_w) + conv_b
        g = jnp.clip(g, 0.0, 1.0)
        return g[..., 0]

    def _L0_attn_ref(x, W_DKV, W_UK, W_UV, W_UQ, W_O):
        import jax, jax.numpy as jnp
        import numpy as np
        DIM = 256
        N_HEADS = 16
        HEAD_DIM = DIM // N_HEADS
        D_LATENT = 64
        B, T = (1, 1024)
        b, t, d = x.shape
        h, hd = (N_HEADS, HEAD_DIM)
        c_kv = x @ W_DKV
        k = (c_kv @ W_UK).reshape(b, t, h, hd)
        v = (c_kv @ W_UV).reshape(b, t, h, hd)
        q = (x @ W_UQ).reshape(b, t, h, hd)
        scale = 1.0 / jnp.sqrt(jnp.asarray(hd, x.dtype))
        scores = jnp.einsum('bqhd,bkhd->bhqk', q, k) * scale
        causal = jnp.tril(jnp.ones((t, t), dtype=bool))
        scores = jnp.where(causal, scores, jnp.asarray(-jnp.inf, scores.dtype))
        probs = jax.nn.softmax(scores, axis=-1)
        ctx = jnp.einsum('bhqk,bkhd->bqhd', probs, v).reshape(b, t, d)
        return ctx @ W_O

    def _L0_ffn_ref(x, router_w, w1, w2, bias):
        import jax, jax.numpy as jnp
        import numpy as np
        NUM_EXPERTS = 8
        TOP_K = 2
        CAPACITY_FACTOR = 1.0

        def _dispatch_compute(xf, top_expert, w1, w2, capacity):
            tokens, hs = xf.shape
            tpe = jnp.bincount(top_expert, length=NUM_EXPERTS)
            indices = jnp.argsort(top_expert)
            offsets = jnp.concatenate([jnp.zeros((1,), tpe.dtype), jnp.cumsum(tpe)[:-1]])
            slot = jnp.arange(capacity)
            pos = offsets[:, None] + slot[None, :]
            valid = slot[None, :] < tpe[:, None]
            tok_idx = indices[jnp.minimum(pos, tokens - 1)]
            xe = jnp.where(valid[..., None], xf[tok_idx], 0.0)
            h = jax.nn.gelu(jnp.einsum('ech,ehf->ecf', xe, w1), approximate=True)
            ye = jnp.einsum('ecf,efh->ech', h, w2)
            tok_safe = jnp.where(valid, tok_idx, tokens)
            out = jnp.zeros((tokens + 1, hs), xf.dtype).at[tok_safe.reshape(-1)].add(ye.reshape(-1, hs))
            return out[:tokens]
        sl, bs, hs = x.shape
        tokens = sl * bs
        capacity = int(CAPACITY_FACTOR * tokens / NUM_EXPERTS)
        xf = x.reshape(tokens, hs)
        scores = jax.nn.softmax(xf @ router_w, axis=-1)
        expert_weights, top_experts = jax.lax.top_k(scores, TOP_K)
        out = jnp.zeros_like(xf)
        for k in range(TOP_K):
            y = _dispatch_compute(xf, top_experts[:, k].astype(jnp.int32), w1, w2, capacity)
            out = out + y * expert_weights[:, k][:, None]
        return out.reshape(sl, bs, hs) + bias
    h = _L0_tok_ref(x, L0_tok_ccm, L0_tok_ccm_bias, L0_tok_shifts, L0_tok_slopes, L0_tok_conv_w, L0_tok_conv_b)
    h = jnp.concatenate([h, txt], axis=1)
    h = h + _L0_attn_ref(_layernorm(h, axis=-1), L0_attn_W_DKV, L0_attn_W_UK, L0_attn_W_UV, L0_attn_W_UQ, L0_attn_W_O)
    h = h + _L0_ffn_ref(_layernorm(h, axis=-1), L0_ffn_router_w, L0_ffn_w1, L0_ffn_w2, L0_ffn_bias)
    return h

_drawn_inputs = setup_inputs


def setup_inputs(seed=0):
    import zlib

    import numpy as np

    out = dict(_drawn_inputs(seed))
    spreads = {'L0_tok_ccm_bias': (0.0, 0.1),
     'L0_tok_conv_w': (0.3333333432674408, 0.2),
     'L0_ffn_bias': (0.0, 0.573)}
    factors = {'L0_attn_W_DKV': 8.0,
     'L0_attn_W_UK': 8.0,
     'L0_attn_W_UV': 8.0,
     'L0_attn_W_UQ': 8.0,
     'L0_attn_W_O': 8.0,
     'L0_ffn_router_w': 8.0,
     'L0_ffn_w1': 8.0,
     'L0_ffn_w2': 8.0}
    for name, (base, spread) in spreads.items():
        noise = np.random.default_rng([zlib.crc32(name.encode()), seed]).standard_normal(out[name].shape)
        drawn = base * np.exp(spread * noise) if base else spread * noise
        out[name] = jnp.asarray(drawn.astype(out[name].dtype))
    for name, factor in factors.items():
        out[name] = (out[name] * factor).astype(out[name].dtype)
    return out
```

```python
from contextlib import ExitStack

import numpy as np

import concourse.bass as bass
from concourse import mybir

F32 = mybir.dt.float32
F32R = mybir.dt.float32r
BF16 = mybir.dt.bfloat16
I32 = mybir.dt.int32
U32 = mybir.dt.uint32
ALU = mybir.AluOpType
ACT = mybir.ActivationFunctionType
AX_X = mybir.AxisListType.X

P = 128
B = 8
NT = 3
T = NT * P
DIM = 256
KC = DIM // P
LAT = 64
HEADS = 16
HD = DIM // HEADS
HALF = HEADS // 2
CH = 3
PTS = 16
E = 8
TOPK = 2
FFN = 1024
FC = FFN // P
TILES = B * NT
CAP = TILES * P // E
CT = CAP // P
SLOTS = TOPK * E * CAP
EPS = 1e-5
SCALE = 1.0 / np.sqrt(HD)
MASKED = -1.0e30
SROWS = 96
PARTS = 4
GH = 4
BANK_TILES = ((0, 2), (1,))
FAR = float(1 << 20)


def rows_to_all(ap, n):
    return bass.AP(tensor=ap.tensor, offset=ap.offset, ap=[[0, P], [1, n]])


def build(nc, x, txt, ccm, ccm_bias, shifts, slopes, conv_w, conv_b, w_dkv, w_uk, w_uv, w_uq, w_o,
          router_w, w1, w2, ffn_bias, out):
    qk_scratch = nc.dram_tensor("qk_scratch", [B, 2, 2, 2, P, T], F32, kind="Internal").ap()
    v_scratch = nc.dram_tensor("v_scratch", [B, NT, P, DIM], F32, kind="Internal").ap()
    max_scratch = nc.dram_tensor("max_scratch", [2, 2, 2, GH, T], F32, kind="Internal").ap()
    slot_rows = nc.dram_tensor("slot_rows", [SLOTS, DIM], F32, kind="Internal").ap()
    slot_out = nc.dram_tensor("slot_out", [SLOTS + P, DIM], F32, kind="Internal").ap()

    with ExitStack() as ctx:
        def sb(name, shape, dt=F32, where=None):
            return (where or ctx).enter_context(nc.sbuf_tensor(name, shape, dt))

        banks = [ctx.enter_context(nc.psum_tensor(f"bank{i}", [P, 512], F32)) for i in range(2)]
        s_bank = ctx.enter_context(nc.psum_tensor("s_bank", [P, 3, 512], F32))
        t_bank = ctx.enter_context(nc.psum_tensor("t_bank", [P, 3, 512], F32))

        hid = sb("hid", [P, B, NT, DIM])
        ident = sb("ident", [P, P])
        ident_b = sb("ident_b", [P, P], BF16)
        mask_q = sb("mask_q", [P, P], BF16)
        mask_k = sb("mask_k", [P, P], BF16)
        sum_rows = sb("sum_rows", [P, P])
        wo_pad = sb("wo_pad", [P, HEADS // GH, DIM])
        eps_t = sb("eps_t", [P, NT])
        neg_half = sb("neg_half", [P, NT])
        flag_i = sb("flag_i", [1, 1], I32)

        common = (hid, ident, ident_b, mask_q, mask_k, sum_rows, wo_pad, eps_t, neg_half, banks, s_bank, t_bank, sb)
        tokens(nc, common, flag_i, x, txt, ccm, ccm_bias, shifts, slopes, conv_w, conv_b,
               w_dkv, w_uk, w_uv, w_uq, w_o, qk_scratch, v_scratch, slot_rows, slot_out)
        attention(nc, common, qk_scratch, v_scratch, max_scratch)
        pos = sb("pos", [P, TILES, TOPK], I32)
        gate = sb("gate", [P, TILES, TOPK])
        routing(nc, common, router_w, slot_rows, pos, gate)
        experts(nc, common, w1, w2, ffn_bias, slot_rows, slot_out)
        combine(nc, common, slot_out, pos, gate, out)


def tokens(nc, common, flag_i, x, txt, ccm, ccm_bias, shifts, slopes, conv_w, conv_b,
           w_dkv, w_uk, w_uv, w_uq, w_o, qk_scratch, v_scratch, slot_rows, slot_out):
    hid, ident, ident_b, mask_q, mask_k, sum_rows, wo_pad, eps_t, neg_half, banks, s_bank, t_bank, sb = common
    IT = NT - 1
    W = DIM
    with ExitStack() as own:
        def buf(name, shape, dt=F32):
            return sb(name, shape, dt, own)

        def sem(name):
            return own.enter_context(nc.semaphore(name))

        prm = buf("prm", [P, 9 + 3 + 48 + 48 + 3 + 1])
        ccm_t = prm[:, 0:9]
        cbias = prm[:, 9:12]
        shift_t = prm[:, 12:60]
        slope_t = prm[:, 60:108]
        conv_t = prm[:, 108:111]
        convb_t = prm[:, 111:112]
        flag_f = buf("flag_f", [1, 2])
        curve_w = buf("curve_w", [P, CH * PTS])
        dkv = buf("dkv", [P, KC, LAT])
        uk = buf("uk", [P, DIM])
        uv = buf("uv", [P, DIM])
        uq = buf("uq", [P, KC, DIM])
        xin = buf("xin", [P, 2, IT, W * CH])
        g = buf("g", [P, CH, IT, W])
        r = buf("r", [P, CH, IT, W])
        acc = buf("acc", [P, IT, W])
        stats = buf("stats", [P, NT, 6])
        mv = buf("mv", [P, NT, 2])
        ve = buf("ve", [P, NT])
        rstd = buf("rstd", [P, NT])
        xn = buf("xn", [P, NT, DIM])
        xnT = buf("xnT", [P, KC, T])
        ckvT = buf("ckvT", [P, T])
        hi = buf("hi", [P, 2, 2, T], F32R)
        lo = buf("lo", [P, 2, 2, T], F32R)
        vals = buf("vals", [P, NT, DIM])
        zeros = buf("zeros", [P, 2048])

        consts_made = sem("consts_made")
        weights_in = sem("weights_in")
        flag_made = sem("flag_made")
        curve_made = sem("curve_made")
        text_in = sem("text_in")
        x_in = sem("x_in")
        x_free = sem("x_free")
        g_base = sem("g_base")
        g_step = sem("g_step")
        pt_step = sem("pt_step")
        g_free = sem("g_free")
        more_step = sem("more_step")
        tok_done = sem("tok_done")
        ln_step = sem("ln_step")
        var_done = sem("var_done")
        ve_done = sem("ve_done")
        rstd_done = sem("rstd_done")
        xn_done = sem("xn_done")
        xnT_ps = sem("xnT_ps")
        xnT_sb = sem("xnT_sb")
        ckv_ps = sem("ckv_ps")
        ckv_sb = sem("ckv_sb")
        qk_ps = sem("qk_ps")
        hi_done = sem("hi_done")
        lo_done = sem("lo_done")
        v_ps = sem("v_ps")
        v_sb = sem("v_sb")
        spilled = sem("spilled")
        zero_made = sem("zero_made")
        passed = sem("passed")
        zeroed = sem("zeroed")
        NW = 6 + 2 + 1 + 1 + 2

        xnT_bank = s_bank[:, 0:KC, 0:T]
        ckv_bank = s_bank[0:LAT, 2, 0:T]
        qk_bank = [[t_bank[:, 0, 0:T], t_bank[:, 1, 0:T]], [t_bank[:, 2, 0:T], banks[0][:, 0:T]]]

        block = own.enter_context(nc.Block())

        @block.gpsimd
        def _(pool):
            pool.memset(ident[:, :], 0.0).then_inc(consts_made, 1)
            pool.memset(mask_q[:, :], 0.0).then_inc(consts_made, 1)
            pool.memset(mask_k[:, :], 0.0).then_inc(consts_made, 1)
            pool.memset(sum_rows[:, :], 0.0).then_inc(consts_made, 1)
            pool.memset(wo_pad[:, :, :], 0.0).then_inc(consts_made, 1)
            pool.memset(uk[:, :], 0.0).then_inc(consts_made, 1)
            pool.memset(uv[:, :], 0.0).then_inc(consts_made, 1)
            pool.memset(ckvT[:, :], 0.0).then_inc(consts_made, 1)
            pool.memset(eps_t[:, :], EPS).then_inc(consts_made, 1)
            pool.memset(neg_half[:, :], -0.5).then_inc(consts_made, 1)
            pool.wait_ge(consts_made, 10)
            pool.affine_select(out=ident[:, :], in_=ident[:, :], compare_op=ALU.not_equal, fill=1.0, base=0,
                               pattern=[[-1, P]], channel_multiplier=1).then_inc(consts_made, 1)
            pool.affine_select(out=mask_q[:, :], in_=mask_q[:, :], compare_op=ALU.is_ge, fill=MASKED, base=0,
                               pattern=[[-1, P]], channel_multiplier=1).then_inc(consts_made, 1)
            pool.affine_select(out=mask_k[:, :], in_=mask_k[:, :], compare_op=ALU.is_ge, fill=MASKED, base=0,
                               pattern=[[1, P]], channel_multiplier=-1).then_inc(consts_made, 1)
            strips = sum_rows[:, :].rearrange("p (i c) -> p i c", i=GH)
            pool.affine_select(out=strips, in_=strips, compare_op=ALU.not_equal, fill=1.0, base=-HD,
                               pattern=[[-32, GH], [0, 32]], channel_multiplier=1).then_inc(consts_made, 1)
            pool.wait_ge(consts_made, 14)
            pool.tensor_copy(ident_b[:, :], ident[:, :]).then_inc(consts_made, 1)
            for c in range(0, 1):
                pool.memset(zeros[:, :], 0.0).then_inc(zero_made, 1)
            with pool.Fori(0, B) as b:
                pool.wait_ge(var_done, NT * b + NT)
                pool.tensor_tensor(ve[:, :], mv[:, :, 1], eps_t[:, :], ALU.add).then_inc(ve_done, 1)
                pool.wait_ge(ve_done, b + 1)
                pool.tensor_tensor(rstd[:, :], ve[:, :], neg_half[:, :], ALU.pow).then_inc(rstd_done, 1)

        @block.sync
        def _(sp):
            sp.sem_inc(spilled, 1)
            sp.wait_ge(consts_made, 10)
            for dst, src in ((ccm_t, rows_to_all(ccm, 9)), (cbias, rows_to_all(ccm_bias, 3)),
                             (shift_t, rows_to_all(shifts, 48)), (slope_t, rows_to_all(slopes, 48)),
                             (conv_t, rows_to_all(conv_w, 3)), (convb_t, rows_to_all(conv_b, 1)),
                             (dkv[:, :, :], w_dkv.rearrange("(c p) n -> p c n", p=P)),
                             (uq[:, :, :], w_uq.rearrange("(c p) n -> p c n", p=P)),
                             (uk[0:LAT, :], w_uk), (uv[0:LAT, :], w_uv)):
                sp.dma_start(dst, src).then_inc(weights_in, 16)
            sp.dma_start(hid[:, :, NT - 1, :], txt.rearrange("b p d -> p b d")).then_inc(text_in, 16)
            for i in range(GH):
                sp.dma_start(wo_pad[32 * i:32 * i + HD, :, :],
                             w_o.rearrange("(g i d) n -> i d g n", i=GH, d=HD)[i]).then_inc(text_in, 16)
            sp.wait_ge(zero_made, 1)
            flat = slot_rows.rearrange("(a p) d -> a p d", p=P * 8)
            for a in range(flat.shape[0]):
                sp.dma_start(flat[a].rearrange("(p r) d -> p (r d)", p=P), zeros[:, :]).then_inc(zeroed, 16)
            sp.dma_start(slot_out[SLOTS:SLOTS + P, :], zeros[:, 0:DIM]).then_inc(zeroed, 16)
            with sp.Fori(0, B) as b:
                for half in range(2):
                    for s in range(2):
                        k = 2 * half + s
                        sp.wait_ge(hi_done, 4 * b + k + 1)
                        sp.dma_start(qk_scratch[b, half, s, 0], hi[:, half, s, :].bitcast(F32)).then_inc(spilled, 16)
                        sp.wait_ge(lo_done, 4 * b + k + 2)
                        sp.dma_start(qk_scratch[b, half, s, 1], lo[:, half, s, :].bitcast(F32)).then_inc(spilled, 16)
                sp.wait_ge(v_sb, 2 * b + 3)
                sp.dma_start(v_scratch[b].rearrange("t p d -> p t d"), vals[:, :, :]).then_inc(spilled, 16)
            sp.wait_ge(spilled, 16 * 9 * B + 1)
            sp.wait_ge(zeroed, 16 * (flat.shape[0] + 1))
            sp.wait_ge(text_in, 16 * (1 + GH))

        @block.scalar
        def _(act):
            act.sem_inc(x_free, 2)
            act.sem_inc(v_sb, 1)
            act.wait_ge(x_free, 1)
            act.dma_start(xin[:, 0, :, :], x[0].rearrange("(j p) w c -> p j (w c)", p=P)).then_inc(x_in, 16)
            act.wait_ge(weights_in, 16 * 10)
            def batch(b, more):
                act.wait_ge(x_in, 16 * b + 16)
                act.wait_ge(g_free, b + 1)
                xv = xin[:, b % 2, :, :].rearrange("p j (w c) -> p j w c", c=CH)
                for d in range(CH):
                    act.activation(g[:, d, :, :], xv[:, :, :, 0], ACT.Identity, bias=cbias[:, d:d + 1],
                                   scale=ccm_t[:, d:d + 1]).then_inc(g_base, 1)
                if more:
                    act.wait_ge(x_free, b + 2)
                    act.wait_ge(g_base, CH * b + CH)
                    act.dma_start(xin[:, (b + 1) % 2, :, :],
                                  x[b + 1].rearrange("(j p) w c -> p j (w c)", p=P)).then_inc(x_in, 16)
                act.wait_ge(ckv_ps, b + 1)
                act.activation(ckvT[0:LAT, :], ckv_bank, ACT.Copy).then_inc(ckv_sb, 1)
                act.wait_ge(spilled, 16 * 9 * b + 1)
                for half in range(2):
                    for s in range(2):
                        act.wait_ge(qk_ps, 4 * b + 2 * half + s + 1)
                        act.activation(hi[:, half, s, :], qk_bank[half][s], ACT.Copy,
                                       scale=float(SCALE) if s == 0 else 1.0).then_inc(hi_done, 1)
                act.wait_ge(v_ps, 2 * b + 1)
                act.activation(vals[:, 0:2, :], banks[1][:, :].rearrange("p (t d) -> p t d", t=2),
                               ACT.Copy).then_inc(v_sb, 1)
                act.wait_ge(v_ps, 2 * b + 2)
                act.activation(vals[:, 2, :], s_bank[:, 2, 0:DIM], ACT.Copy).then_inc(v_sb, 1)

            with act.Fori(0, B - 1) as b:
                batch(b, True)
            batch(B - 1, False)

        @block.vector
        def _(dve):
            dve.wait_ge(weights_in, 16 * 10)
            for c in range(CH):
                dve.tensor_scalar(curve_w[:, c * PTS:(c + 1) * PTS], slope_t[:, c * PTS:(c + 1) * PTS],
                                  conv_t[:, c:c + 1], None, ALU.mult).then_inc(curve_made, 1)
            dve.tensor_reduce(flag_f[:, 0:1], slope_t[0:1, :].rearrange("p (c n) -> p c n", c=CH)[:, :, 1:PTS],
                              mybir.AxisListType.XY, ALU.max, apply_absolute_value=True).then_inc(flag_made, 1)
            dve.wait_ge(flag_made, 1)
            dve.tensor_scalar(flag_i[:, :], flag_f[:, 0:1], 0.0, None, ALU.not_equal).then_inc(flag_made, 1)
            dve.wait_ge(flag_made, 2)
            dve.wait_ge(curve_made, CH)
            more = dve.value_load(flag_i[0:1, 0:1], min_val=0, max_val=1)
            dve.wait_ge(text_in, 16 * (1 + GH))
            dve.sem_inc(g_free, 1)
            dve.sem_inc(lo_done, 1)
            with dve.Fori(0, B) as b:
                xv = xin[:, b % 2, :, :].rearrange("p j (w c) -> p j w c", c=CH)
                for c in range(1, CH):
                    for d in range(CH):
                        if c == 1:
                            dve.wait_ge(g_base, CH * b + d + 1)
                        else:
                            dve.wait_ge(g_step, 2 * CH * b + d + 1)
                        dve.scalar_tensor_tensor(out=g[:, d, :, :], in0=xv[:, :, :, c],
                                                 scalar=ccm_t[:, c * CH + d:c * CH + d + 1], in1=g[:, d, :, :],
                                                 op0=ALU.mult, op1=ALU.add).then_inc(g_step, 1)
                dve.wait_ge(g_step, 2 * CH * b + 2 * CH)
                dve.sem_inc(x_free, 1)

                for c in range(CH):
                    dve.tensor_scalar(r[:, c, :, :], g[:, c, :, :], shift_t[:, c * PTS:c * PTS + 1], 0.0,
                                      ALU.subtract, ALU.max).then_inc(pt_step, 1)
                for c in range(CH):
                    dve.wait_ge(pt_step, 6 * b + (c + 1 if c == 0 else CH + c))
                    if c == 0:
                        dve.tensor_scalar(acc[:, :, :], r[:, 0, :, :], curve_w[:, 0:1], convb_t[:, 0:1],
                                          ALU.mult, ALU.add).then_inc(pt_step, 1)
                    else:
                        dve.scalar_tensor_tensor(out=acc[:, :, :], in0=r[:, c, :, :],
                                                 scalar=curve_w[:, c * PTS:c * PTS + 1], in1=acc[:, :, :],
                                                 op0=ALU.mult, op1=ALU.add).then_inc(pt_step, 1)
                dve.wait_ge(pt_step, 6 * b + 6)
                dve.sem_inc(passed, 1)
                with dve.If(more):
                    with dve.Fori(1, PTS) as i:
                        done = 6 * (PTS - 1) * b + 6 * (i - 1)
                        for c in range(CH):
                            dve.tensor_scalar(r[:, c, :, :], g[:, c, :, :], shift_t[:, bass.ds(c * PTS + i, 1)], 0.0,
                                              ALU.subtract, ALU.max).then_inc(more_step, 1)
                        for c in range(CH):
                            dve.wait_ge(more_step, done + CH + c)
                            dve.scalar_tensor_tensor(out=acc[:, :, :], in0=r[:, c, :, :],
                                                     scalar=curve_w[:, bass.ds(c * PTS + i, 1)], in1=acc[:, :, :],
                                                     op0=ALU.mult, op1=ALU.add).then_inc(more_step, 1)
                        dve.wait_ge(more_step, done + 2 * CH)
                        dve.sem_inc(passed, 1)
                dve.sem_inc(g_free, 1)
                dve.tensor_scalar(hid[:, b, 0:IT, :], acc[:, :, :], 0.0, 1.0, ALU.max, ALU.min).then_inc(tok_done, 1)

                dve.wait_ge(tok_done, b + 1)
                dve.sem_inc(passed, 1)
                for t in range(NT):
                    dve.bn_stats(stats[:, t, :], hid[:, b, t, :]).then_inc(ln_step, 1)
                dve.wait_ge(ln_step, NT * b + NT)
                dve.sem_inc(passed, 1)
                for t in range(NT):
                    dve.bn_aggr(mv[:, t, :], stats[:, t, :]).then_inc(var_done, 1)
                dve.wait_ge(rstd_done, b + 1)
                dve.wait_ge(xnT_ps, b + 1)
                for t in range(NT):
                    dve.tensor_scalar(xn[:, t, :], hid[:, b, t, :], mv[:, t, 0:1], rstd[:, t:t + 1],
                                      ALU.subtract, ALU.mult).then_inc(xn_done, 1)
                dve.wait_ge(xnT_ps, b + 2)
                dve.tensor_copy(xnT[:, :, :], xnT_bank).then_inc(xnT_sb, 1)
                dve.wait_ge(spilled, 16 * 9 * b + 1)
                for half in range(2):
                    for s in range(2):
                        dve.wait_ge(hi_done, 4 * b + 2 * half + s + 1)
                        dve.scalar_tensor_tensor(out=lo[:, half, s, :], in0=qk_bank[half][s],
                                                 scalar=float(SCALE) if s == 0 else 1.0,
                                                 in1=hi[:, half, s, :].bitcast(F32), op0=ALU.mult,
                                                 op1=ALU.subtract).then_inc(lo_done, 1)

        @block.tensor
        def _(pe):
            pe.wait_ge(consts_made, 15)
            pe.sem_inc(xnT_ps, 1)
            pe.wait_ge(weights_in, 16 * 10)
            with pe.Fori(0, B) as b:
                pe.wait_ge(xn_done, NT * b + NT)
                for t in range(NT):
                    for c in range(KC):
                        m = pe.transpose(s_bank[:, c, t * P:(t + 1) * P], xn[:, t, c * P:(c + 1) * P], ident[:, :])
                m.then_inc(xnT_ps, 1)
                pe.wait_ge(xnT_sb, b + 1)
                pe.wait_ge(v_sb, 2 * b + 1)
                for c in range(KC):
                    m = pe.matmul(ckv_bank, dkv[:, c, :], xnT[:, c, :], start=(c == 0), stop=(c == KC - 1))
                m.then_inc(ckv_ps, 1)
                pe.wait_ge(lo_done, 4 * b + 1)
                for half in range(2):
                    cols = slice(half * P, (half + 1) * P)
                    for c in range(KC):
                        m = pe.matmul(qk_bank[half][0], uq[:, c, cols], xnT[:, c, :], start=(c == 0), stop=(c == KC - 1))
                    m.then_inc(qk_ps, 1)
                    if half == 0:
                        pe.wait_ge(ckv_sb, b + 1)
                    pe.matmul(qk_bank[half][1], uk[:, cols], ckvT[:, :], start=True, stop=True).then_inc(qk_ps, 1)
                for t in range(NT):
                    dst = banks[1][:, t * DIM:(t + 1) * DIM] if t < 2 else s_bank[:, 2, 0:DIM]
                    m = pe.matmul(dst, ckvT[:, t * P:(t + 1) * P], uv[:, :], start=True, stop=True)
                    if t:
                        m.then_inc(v_ps, 1)


def attention(nc, common, qk_scratch, v_scratch, max_scratch):
    hid, ident, ident_b, mask_q, mask_k, sum_rows, wo_pad, eps_t, neg_half, banks, s_bank, t_bank, sb = common
    misc, ctx_bank = banks[0], banks[1]
    NG = 2
    with ExitStack() as own:
        def buf(name, shape, dt=F32):
            return sb(name, shape, dt, own)

        def sem(name):
            return own.enter_context(nc.semaphore(name))

        qs = [buf(f"qs{h}", [SROWS, HALF, T], F32R) for h in range(2)]
        ks = [buf(f"ks{h}", [SROWS, HALF, T], F32R) for h in range(2)]
        vb = [buf(f"vb{h}", [P, NT, HALF, 32]) for h in range(2)]
        zrow = buf("zrow", [2, HALF * T])
        mx = buf("mx", [P, NG, NT, GH])
        ms = buf("ms", [P, NG, NT, 2, GH])
        mT = buf("mT", [2 * GH, NG, T])
        pt = buf("pt", [P, 4, 2, 2 * T])
        cx = buf("cx", [P, NG, T])
        rc = buf("rc", [P, NG, T])
        cn = buf("cn", [P, HEADS // GH, T])

        ready = sem("ready")
        stack_in = [[sem(f"stack_in{h}{q}") for q in range(2)] for h in range(2)]
        v_in = [sem(f"v_in{h}") for h in range(2)]
        s_ready = sem("s_ready")
        s_read = sem("s_read")
        m_hi = sem("m_hi")
        m_split = sem("m_split")
        mT_ps = sem("mT_ps")
        mT_sb = sem("mT_sb")
        m_out = sem("m_out")
        m_in = sem("m_in")
        t_ready = sem("t_ready")
        exp_done = sem("exp_done")
        pv_done = sem("pv_done")
        ctx_sb = sem("ctx_sb")
        sums_ps = sem("sums_ps")
        rc_done = sem("rc_done")
        cn_done = sem("cn_done")
        wo_ps = sem("wo_ps")
        hid_add = sem("hid_add")
        misc_free = sem("misc_free")
        s_used = sem("s_used")
        NL = 5

        block = own.enter_context(nc.Block())

        def program(turn, eng):
            turn(-1, 1, True, False, False)
            for half in range(2):
                turn(0, half, True, True, half == 1)
            with eng.Fori(1, B - 1) as rnd:
                for half in range(2):
                    turn(rnd, half, True, True, True)
            for half in range(2):
                turn(B - 1, half, half == 0, True, True)
            turn(B, 0, False, False, True)

        def misc_uses(rnd, half):
            if isinstance(rnd, int) and rnd < 1:
                return 0 if rnd < 0 else 1 + 3 * half
            skipped = 1 if isinstance(rnd, int) and rnd == B else 0
            return 10 * rnd - 2 + (6 if half else 0) - skipped

        @block.sync
        def _(sp):
            def load(rnd, half, grp):
                heads = slice(grp * GH, (grp + 1) * GH)
                for s, dst in ((0, qs[half]), (1, ks[half])):
                    for part in range(2):
                        src = qk_scratch[rnd, half, s, part].rearrange("(h d) t -> d h t", d=HD)[:, heads, :]
                        for rep in range(2):
                            row = (2 * part + rep if s == 0 else 2 * rep + part) * HD
                            sp.dma_start(dst[row:row + HD, heads, :].bitcast(F32), src).then_inc(stack_in[half][grp], 16)
                sp.dma_start(qs[half][4 * HD:4 * HD + 2, heads, :].bitcast(F32),
                             zrow[:, 0:GH * T].rearrange("p (h t) -> p h t", h=GH)).then_inc(stack_in[half][grp], 16)

            def load_v(rnd, half):
                src = v_scratch[rnd].rearrange("t p (h d) -> p t h d", d=HD)[:, :, half * HALF:(half + 1) * HALF, :]
                for t in range(NT):
                    sp.dma_start(vb[half][:, t, :, 0:HD], src[:, t]).then_inc(v_in[half], 16)

            def max_bounce(rnd, half, grp, n):
                G = NG * n + grp
                sp.wait_ge(mT_sb, G + 1)
                sp.dma_start(max_scratch[half, grp], mT[:, grp, :]).then_inc(m_out, 16)
                sp.wait_ge(m_out, 16 * (G + 1))
                sp.dma_start(qs[half][4 * HD:4 * HD + 2, grp * GH:(grp + 1) * GH, :].bitcast(F32),
                             max_scratch[half, grp]).then_inc(m_in, 16)
                sp.wait_ge(m_in, 16 * (G + 1))

            sp.wait_ge(ready, 7)
            for half in range(2):
                for grp in range(NG):
                    load(0, half, grp)
                load_v(0, half)

            def turn(rnd, half, nxt, cur, prev):
                n = 2 * rnd + half
                if cur:
                    max_bounce(rnd, half, 1, n)
                if nxt and half == 1:
                    max_bounce(rnd, 0, 0, n + 1)
                elif nxt:
                    max_bounce(rnd, 1, 0, n + 1)
                if cur and not (isinstance(rnd, int) and rnd == B - 1):
                    for grp in range(NG):
                        sp.wait_ge(t_ready, 2 * (4 * n + 2 * grp + 2))
                        load(rnd + 1, half, grp)
                    sp.wait_ge(pv_done, NG * n + NG + 2)
                    load_v(rnd + 1, half)

            program(turn, sp)

        @block.gpsimd
        def _(pool):
            pool.memset(zrow[:, :], 0.0).then_inc(ready, 1)
            for h in range(2):
                pool.wait_ge(ready, 1 + 3 * h)
                pool.memset(qs[h][64:96, :, :].bitcast(F32), 0.0).then_inc(ready, 1)
                pool.wait_ge(ready, 2 + 3 * h)
                pool.memset(ks[h][64:96, :, :].bitcast(F32), -1.0).then_inc(ready, 1)
                pool.wait_ge(ready, 3 + 3 * h)
                pool.memset(vb[h][:, :, :, HD:2 * HD], 1.0).then_inc(ready, 1)

            def norm_at(rnd, half, grp):
                n = 2 * rnd + half
                G = NG * n + grp
                pool.wait_ge(rc_done, G + 1)
                pool.wait_ge(wo_ps, 2 * rnd)
                pool.tensor_tensor(cn[:, NG * half + grp, :], cx[:, grp, :], rc[:, grp, :],
                                   ALU.mult).then_inc(cn_done, 1)

            def turn(rnd, half, nxt, cur, prev):
                if prev:
                    norm_at(rnd if half else rnd - 1, 1 - half, 1)
                if cur:
                    norm_at(rnd, half, 0)

            program(turn, pool)

        @block.tensor
        def _(pe):
            pe.sem_inc(pv_done, 2)

            def misc_wait(use):
                pe.wait_ge(misc_free, use)

            def score_pair(n, half, rnd, p):
                m = 4 * n + p
                if p % 2 == 0:
                    pe.wait_ge(stack_in[half][p // 2], 16 * 9 * (rnd + 1))
                for g, tiles in enumerate(BANK_TILES):
                    pe.wait_ge(s_read, 2 * m + g + 1)
                    for i in range(2):
                        h = 2 * p + i
                        for j in tiles:
                            dst, w = s_region(s_bank, j, i)
                            pe.matmul(dst, qs[half][:, h, j * P:(j + 1) * P], ks[half][:, h, 0:w], start=True, stop=False)
                            mm = pe.matmul(dst[:, j * P:(j + 1) * P], ident_b[:, :], mask_q[:, :], start=False, stop=True)
                    mm.then_inc(s_ready, 1)

            def exp_pair(n, half, p):
                m = 4 * n + p
                if p % 2 == 0:
                    pe.wait_ge(m_in, 16 * (NG * n + p // 2 + 1))
                for g, tiles in enumerate(BANK_TILES):
                    pe.wait_ge(exp_done, 2 * m + g + 1)
                    for i in range(2):
                        h = 2 * p + i
                        for j in tiles:
                            dst, w = s_region(t_bank, 2 - j, i)
                            pe.matmul(dst, ks[half][:, h, j * P:(j + 1) * P], qs[half][:, h, j * P:T], start=True, stop=False)
                            mm = pe.matmul(dst[:, 0:P], ident_b[:, :], mask_k[:, :], start=False, stop=True)
                    mm.then_inc(t_ready, 1)

            def values(n, half, rnd, grp):
                G = NG * n + grp
                pe.wait_ge(exp_done, 2 + 2 * (4 * n + 2 * grp + 2))
                pe.wait_ge(v_in[half], 16 * NT * (rnd + 1))
                pe.wait_ge(ctx_sb, G)
                for j in range(NT):
                    for i in range(GH):
                        src = pt[:, 2 * grp + i // 2, i % 2, :]
                        at = (0, T, T + 2 * P)[j]
                        mm = pe.matmul(ctx_bank[32 * i:32 * i + 32, j * P:T], vb[half][:, j, grp * GH + i, :],
                                       src[:, at:at + T - j * P], start=(j == 0), stop=(j == NT - 1))
                mm.then_inc(pv_done, 1)

            def spread_sums(n, grp, use):
                pe.wait_ge(ctx_sb, NG * n + grp + 1)
                misc_wait(use)
                pe.matmul(misc[:, 0:T], sum_rows[:, :], cx[:, grp, :], start=True, stop=True).then_inc(sums_ps, 1)

            def turn_maxima(n, grp, use):
                pe.wait_ge(m_split, NG * n + grp + 1)
                misc_wait(use)
                for j in range(NT):
                    mm = pe.transpose(misc[0:2 * GH, j * P:(j + 1) * P],
                                      ms[:, grp, j, :, :].rearrange("p a h -> p (a h)"), ident[:, :])
                mm.then_inc(mT_ps, 1)

            def project(rnd, tiles, use):
                pe.wait_ge(cn_done, 4 * (rnd + 1))
                misc_wait(use)
                for at, t in enumerate(tiles):
                    for g in range(HEADS // GH):
                        mm = pe.matmul(misc[:, at * DIM:(at + 1) * DIM], cn[:, g, t * P:(t + 1) * P],
                                       wo_pad[:, g, :], start=(g == 0), stop=(g == HEADS // GH - 1))
                mm.then_inc(wo_ps, 1)

            def turn(rnd, half, nxt, cur, prev):
                n = 2 * rnd + half
                use = misc_uses(rnd, half)
                prnd = rnd if half else rnd - 1
                for p in range(4):
                    if nxt:
                        score_pair(n + 1, 1 - half, rnd + half, p)
                    if cur and p == 0:
                        turn_maxima(n, 1, use)
                        use = use + 1
                    if nxt and p == 2:
                        turn_maxima(n + 1, 0, use)
                        use = use + 1
                    if cur:
                        exp_pair(n, half, p)
                    if prev and p == 0:
                        values(n - 1, 1 - half, prnd, 1)
                    if prev and p == 1:
                        spread_sums(n - 1, 1, use)
                        use = use + 1
                    if prev and p == 2 and half == 0:
                        project(rnd - 1, (0, 1), use)
                        use = use + 1
                    if cur and p == 2:
                        values(n, half, rnd, 0)
                    if prev and p == 2 and half == 0:
                        project(rnd - 1, (2,), use)
                        use = use + 1
                    if cur and p == 3:
                        spread_sums(n, 0, use)
                        use = use + 1

            program(turn, pe)

        @block.scalar
        def _(act):
            act.sem_inc(exp_done, 2)

            def exps(n, p):
                m = 4 * n + p
                act.wait_ge(pv_done, NG * n + p // 2 + 1)
                for g, tiles in enumerate(BANK_TILES):
                    act.wait_ge(t_ready, 2 * m + g + 1)
                    for j in tiles:
                        at = (0, T, T + 2 * P)[j]
                        ins = act.activation(pt[:, p, :, at:at + T - j * P], pair_region(t_bank, 2 - j), ACT.Exp)
                    ins.then_inc(exp_done, 1)

            def maxima_rows(n, grp):
                G = NG * n + grp
                act.wait_ge(mT_ps, G + 1)
                act.activation(mT[:, grp, :], misc[0:2 * GH, 0:T], ACT.Copy).then_inc(mT_sb, 1)
                act.wait_ge(mT_sb, G + 1)
                act.sem_inc(misc_free, 1)

            def contexts(n, grp):
                G = NG * n + grp
                act.wait_ge(pv_done, G + 3)
                act.wait_ge(cn_done, G - 1 if not isinstance(G, int) else max(G - 1, 0))
                act.activation(cx[:, grp, :], ctx_bank[:, 0:T], ACT.Copy).then_inc(ctx_sb, 1)

            def turn(rnd, half, nxt, cur, prev):
                n = 2 * rnd + half
                for p in range(4):
                    if cur and p == 0:
                        maxima_rows(n, 1)
                    if nxt and p == 2:
                        maxima_rows(n + 1, 0)
                    if cur:
                        exps(n, p)
                    if prev and p == 0:
                        contexts(n - 1, 1)
                    if cur and p == 2:
                        contexts(n, 0)

            program(turn, act)

        @block.vector
        def _(dve):
            dve.sem_inc(s_read, 2)

            def maxima(n, p):
                m = 4 * n + p
                for g, tiles in enumerate(BANK_TILES):
                    dve.wait_ge(s_ready, 2 * m + g + 1)
                    for j in tiles:
                        ins = dve.tensor_reduce(mx[:, p // 2, j, 2 * (p % 2):2 * (p % 2) + 2], pair_region(s_bank, j),
                                                AX_X, ALU.max)
                    ins.then_inc(s_read, 1)

            def split(n, grp):
                G = NG * n + grp
                dve.wait_ge(s_read, 2 + 2 * (4 * n + 2 * grp + 2))
                dve.wait_ge(mT_ps, G - 1 if not isinstance(G, int) else max(G - 1, 0))
                dve.tensor_copy(ms[:, grp, :, 0, :].bitcast(F32R), mx[:, grp, :, :]).then_inc(m_hi, 1)
                dve.wait_ge(m_hi, G + 1)
                dve.tensor_tensor(ms[:, grp, :, 1, :], mx[:, grp, :, :], ms[:, grp, :, 0, :],
                                  ALU.subtract).then_inc(m_split, 1)

            def reciprocals(n, grp):
                G = NG * n + grp
                dve.wait_ge(sums_ps, G + 1)
                dve.wait_ge(cn_done, G - 1 if not isinstance(G, int) else max(G - 1, 0))
                dve.reciprocal(rc[:, grp, :], misc[:, 0:T]).then_inc(rc_done, 1)
                dve.wait_ge(rc_done, G + 1)
                dve.sem_inc(misc_free, 1)

            def residual(rnd, k):
                dve.wait_ge(wo_ps, 2 * rnd + k + 1)
                tiles = slice(0, 2) if k == 0 else slice(2, 3)
                src = misc[:, 0:(2 - k) * DIM].rearrange("p (t d) -> p t d", d=DIM)
                dve.tensor_tensor(hid[:, rnd, tiles, :], hid[:, rnd, tiles, :], src, ALU.add).then_inc(hid_add, 1)
                dve.wait_ge(hid_add, 2 * rnd + k + 1)
                dve.sem_inc(misc_free, 1)

            def turn(rnd, half, nxt, cur, prev):
                n = 2 * rnd + half
                for p in range(4):
                    if nxt:
                        maxima(n + 1, p)
                    if nxt and p == 1:
                        split(n + 1, 0)
                    if prev and p == 1:
                        reciprocals(n - 1, 1)
                    if prev and p == 2 and half == 0:
                        residual(rnd - 1, 0)
                        residual(rnd - 1, 1)
                    if nxt and p == 3:
                        split(n + 1, 1)
                    if cur and p == 3:
                        reciprocals(n, 0)

            program(turn, dve)


def s_region(bank, j, i):
    w = (j + 1) * P
    if j == 2:
        return bank[:, i, 0:w], w
    if j == 1:
        return bank[:, 2, i * w:(i + 1) * w], w
    return bank[:, i, T:T + P], w


def pair_region(bank, j):
    w = (j + 1) * P
    if j == 2:
        return bank[:, 0:2, 0:w]
    if j == 1:
        return bank[:, 2, :].rearrange("p (i c) -> p i c", i=2)
    return bank[:, 0:2, T:T + P]


def routing(nc, common, router_w, slot_rows, pos, gate):
    hid, ident, ident_b, mask_q, mask_k, sum_rows, wo_pad, eps_t, neg_half, banks, s_bank, t_bank, sb = common
    KE = TOPK * E
    with ExitStack() as own:
        def buf(name, shape, dt=F32):
            return sb(name, shape, dt, own)

        def sem(name):
            return own.enter_context(nc.semaphore(name))

        rw = buf("rw", [P, KC, E])
        tri = buf("tri", [P, P], BF16)
        ones = buf("ones", [P, P], BF16)
        iota_i = buf("iota_i", [P, TOPK, E], I32)
        base_i = buf("base_i", [P, TOPK, E], I32)
        iota_e = buf("iota_e", [P, TOPK, E])
        base = buf("base", [P, TOPK, E])
        stats = buf("r_stats", [P, NT, 6])
        mv = buf("r_mv", [P, NT, 2])
        ve = buf("r_ve", [P, NT])
        rstd = buf("r_rstd", [P, NT])
        xn = [buf(f"r_xn{q}", [P, NT, DIM]) for q in range(2)]
        xnT = buf("r_xnT", [P, KC, T])
        logits = buf("logits", [P, NT, E])
        top = buf("top", [P, NT, 8])
        top_i = buf("top_i", [P, NT, 8], U32)
        top_f = buf("top_f", [P, NT, TOPK])
        shifted = buf("shifted", [P, NT, E])
        expd = buf("expd", [P, NT, E])
        ssum = buf("ssum", [P, NT])
        rsum = buf("rsum", [P, NT])
        etop = buf("etop", [P, NT, TOPK])
        oh = buf("oh", [P, NT, TOPK, E])
        ohb = buf("ohb", [P, NT, KE], BF16)
        seen = buf("seen", [P, NT + 1, KE], BF16)
        pick = buf("pick", [P, NT, TOPK, E])
        rank = buf("rank", [P, NT, TOPK])
        first = buf("first", [P, NT, TOPK])
        full = buf("full", [P, NT, TOPK])
        slot_f = buf("slot_f", [P, NT, TOPK])
        slot_i = [buf(f"slot_i{q}", [P, NT, TOPK], I32) for q in range(2)]

        made = sem("r_made")
        rw_in = sem("rw_in")
        step = sem("r_step")
        passed = sem("r_passed")
        var_done = sem("r_var")
        ve_done = sem("r_ve_done")
        rstd_done = sem("r_rstd_done")
        xn_done = sem("r_xn_done")
        xnT_ps = sem("r_xnT_ps")
        xnT_sb = sem("r_xnT_sb")
        log_ps = sem("log_ps")
        shift_done = sem("shift_done")
        exp_done = sem("r_exp_done")
        oh_done = sem("oh_done")
        rank_ps = sem("rank_ps")
        slot_done = sem("slot_done")
        sent = [sem(f"sent{q}") for q in range(2)]
        rows_free = sem("rows_free")
        pool_passed = sem("pool_passed")

        rank_bank = banks[1][:, 0:NT * KE].rearrange("p (t k e) -> p t k e", t=NT, k=TOPK)
        log_bank = banks[0][:, 0:NT * E].rearrange("p (t e) -> p t e", t=NT)
        block = own.enter_context(nc.Block())

        @block.sync
        def _(sp):
            sp.dma_start(rw[:, :, :], router_w.rearrange("(c p) e -> p c e", p=P)).then_inc(rw_in, 16)

        @block.gpsimd
        def _(pool):
            pool.memset(tri[:, :], 1.0).then_inc(made, 1)
            pool.memset(ones[:, :], 1.0).then_inc(made, 1)
            pool.memset(seen[:, :, :], 0.0).then_inc(made, 1)
            pool.iota(iota_i[:, :, :], pattern=[[0, TOPK], [1, E]], base=0, channel_multiplier=0).then_inc(made, 1)
            pool.iota(base_i[:, :, :], pattern=[[E * CAP, TOPK], [CAP, E]], base=0,
                      channel_multiplier=0).then_inc(made, 1)
            pool.wait_ge(made, 5)
            pool.affine_select(out=tri[:, :], in_=tri[:, :], compare_op=ALU.is_gt, fill=0.0, base=0,
                               pattern=[[1, P]], channel_multiplier=-1).then_inc(made, 1)
            pool.tensor_copy(iota_e[:, :, :], iota_i[:, :, :]).then_inc(made, 1)
            pool.tensor_copy(base[:, :, :], base_i[:, :, :]).then_inc(made, 1)
            pool.sem_inc(rows_free, 2)

            def turn(rnd, start):
                for q in range(2):
                    b = 2 * rnd + q
                    pool.wait_ge(var_done, NT * b + NT)
                    pool.tensor_tensor(ve[:, :], mv[:, :, 1], eps_t[:, :], ALU.add).then_inc(ve_done, 1)
                    pool.wait_ge(ve_done, b + 1)
                    pool.tensor_tensor(rstd[:, :], ve[:, :], neg_half[:, :], ALU.pow).then_inc(rstd_done, 1)
                    if q == 1 or not start:
                        pool.wait_ge(sent[1 - q], 16 * NT * TOPK * (rnd + q))
                        pool.sem_inc(rows_free, 1)
                    pool.wait_ge(slot_done, b + 1)
                    pool.sem_inc(pool_passed, 1)
                    for t in range(NT):
                        for k in range(TOPK):
                            pool.indirect_dma_start(
                                out=slot_rows, out_offset=bass.IndirectOffsetOnAxis(ap=slot_i[q][:, t, k:k + 1], axis=0),
                                in_=xn[q][:, t, :], in_offset=None, bounds_check=SLOTS - 1,
                                oob_is_err=False).then_inc(sent[q], 16)

            turn(0, True)
            with pool.Fori(1, B // 2) as rnd:
                turn(rnd, False)
            for q in range(2):
                pool.wait_ge(sent[q], 16 * (B // 2) * NT * TOPK)

        @block.scalar
        def _(act):
            with act.Fori(0, B) as b:
                act.wait_ge(shift_done, b + 1)
                act.activation(expd[:, :, :], shifted[:, :, :], ACT.Exp).then_inc(exp_done, 1)

        @block.vector
        def _(dve):
            dve.wait_ge(made, 8)
            per = 30

            with dve.Fori(0, B // 2) as rnd:
                for q in range(2):
                    b = 2 * rnd + q
                    k = [0]

                    def then(ins, last=True):
                        k[0] += 1
                        ins.then_inc(step, 1)
                        if last:
                            dve.wait_ge(step, per * b + k[0])

                    for t in range(NT):
                        then(dve.bn_stats(stats[:, t, :], hid[:, b, t, :]), t == NT - 1)
                    dve.sem_inc(passed, 1)
                    for t in range(NT):
                        dve.bn_aggr(mv[:, t, :], stats[:, t, :]).then_inc(var_done, 1)
                    dve.wait_ge(rstd_done, b + 1)
                    dve.wait_ge(rows_free, b + 1)
                    for t in range(NT):
                        dve.tensor_scalar(xn[q][:, t, :], hid[:, b, t, :], mv[:, t, 0:1], rstd[:, t:t + 1],
                                          ALU.subtract, ALU.mult).then_inc(xn_done, 1)
                    dve.wait_ge(xnT_ps, b + 1)
                    dve.tensor_copy(xnT[:, :, :], s_bank[:, 0:KC, 0:T]).then_inc(xnT_sb, 1)
                    dve.wait_ge(log_ps, b + 1)
                    then(dve.tensor_copy(logits[:, :, :], log_bank))
                    dve.sem_inc(passed, 1)
                    for t in range(NT):
                        then(dve.max(top[:, t, :], logits[:, t, :]), t == NT - 1)
                    dve.tensor_tensor(shifted[:, :, :], logits[:, :, :], top[:, :, 0:1].to_broadcast([P, NT, E]),
                                      ALU.subtract).then_inc(shift_done, 1)
                    for t in range(NT):
                        then(dve.max_index(top_i[:, t, :], top[:, t, :], logits[:, t, :]), t == NT - 1)
                    then(dve.tensor_copy(top_f[:, :, :], top_i[:, :, 0:TOPK]))
                    for c in range(TOPK):
                        then(dve.tensor_tensor(oh[:, :, c, :], iota_e[:, 0:1, :].to_broadcast([P, NT, E]),
                                               top_f[:, :, c:c + 1].to_broadcast([P, NT, E]), ALU.is_equal), c == 1)
                    then(dve.tensor_copy(ohb[:, :, :], oh[:, :, :, :].rearrange("p t k e -> p t (k e)")))
                    for t in range(NT):
                        ins = dve.tensor_tensor(seen[:, t + 1, :], seen[:, t, :], ohb[:, t, :], ALU.add)
                        if t < NT - 1:
                            then(ins)
                        else:
                            ins.then_inc(oh_done, 1)
                    dve.wait_ge(exp_done, b + 1)
                    then(dve.tensor_reduce(ssum[:, :], expd[:, :, :], AX_X, ALU.add))
                    then(dve.reciprocal(rsum[:, :], ssum[:, :]), False)
                    for c in range(TOPK):
                        then(dve.tensor_tensor(pick[:, :, c, :], oh[:, :, c, :], expd[:, :, :], ALU.mult), c == 1)
                    then(dve.tensor_reduce(etop[:, :, :], pick[:, :, :, :], AX_X, ALU.add))
                    then(dve.tensor_tensor(gate[:, bass.ds(NT * b, NT), :], etop[:, :, :],
                                           rsum[:, :].rearrange("p (t o) -> p t o", o=1).to_broadcast([P, NT, TOPK]),
                                           ALU.mult))
                    for t in range(NT):
                        ins = dve.tensor_tensor(pick[:, t, :, :], base[:, :, :], oh[:, t, :, :], ALU.mult)
                        if t < NT - 1:
                            ins.then_inc(passed, 1)
                        else:
                            then(ins)
                    then(dve.tensor_reduce(first[:, :, :], pick[:, :, :, :], AX_X, ALU.add))
                    dve.wait_ge(rank_ps, b + 1)
                    dve.tensor_copy(seen[:, 0, :], seen[:, NT, :]).then_inc(passed, 1)
                    then(dve.tensor_tensor(pick[:, :, :, :], rank_bank, oh[:, :, :, :], ALU.mult))
                    then(dve.tensor_reduce(rank[:, :, :], pick[:, :, :, :], AX_X, ALU.add))
                    then(dve.tensor_scalar(full[:, :, :], rank[:, :, :], float(CAP), FAR, ALU.is_ge, ALU.mult), False)
                    then(dve.tensor_tensor(slot_f[:, :, :], rank[:, :, :], first[:, :, :], ALU.add))
                    then(dve.tensor_tensor(slot_f[:, :, :], slot_f[:, :, :], full[:, :, :], ALU.add))
                    dve.tensor_copy(slot_i[q][:, :, :], slot_f[:, :, :]).then_inc(slot_done, 1)
                    then(dve.tensor_scalar(pos[:, bass.ds(NT * b, NT), :], slot_f[:, :, :], float(SLOTS), None, ALU.min))
                    assert k[0] == per, k[0]

        @block.tensor
        def _(pe):
            pe.wait_ge(rw_in, 16)
            pe.wait_ge(made, 8)
            with pe.Fori(0, B // 2) as rnd:
                for q in range(2):
                    b = 2 * rnd + q
                    pe.wait_ge(xn_done, NT * b + NT)
                    for t in range(NT):
                        for c in range(KC):
                            m = pe.transpose(s_bank[:, c, t * P:(t + 1) * P], xn[q][:, t, c * P:(c + 1) * P], ident[:, :])
                    m.then_inc(xnT_ps, 1)
                    pe.wait_ge(xnT_sb, b + 1)
                    for t in range(NT):
                        for c in range(KC):
                            m = pe.matmul(log_bank[:, t, :], xnT[:, c, t * P:(t + 1) * P], rw[:, c, :],
                                          start=(c == 0), stop=(c == KC - 1))
                    m.then_inc(log_ps, 1)
                    pe.wait_ge(oh_done, b + 1)
                    for t in range(NT):
                        dst = banks[1][:, t * KE:(t + 1) * KE]
                        pe.matmul(dst, tri[:, :], ohb[:, t, :], start=True, stop=False)
                        m = pe.matmul(dst, ones[:, :], seen[:, t, :], start=False, stop=True)
                    m.then_inc(rank_ps, 1)


def experts(nc, common, w1, w2, ffn_bias, slot_rows, slot_out):
    hid, ident, ident_b, mask_q, mask_k, sum_rows, wo_pad, eps_t, neg_half, banks, s_bank, t_bank, sb = common
    with ExitStack() as own:
        def buf(name, shape, dt=F32):
            return sb(name, shape, dt, own)

        def sem(name):
            return own.enter_context(nc.semaphore(name))

        NW = KC * FFN
        wr = [buf(f"wr{i}", [P, NW]) for i in range(2)]
        wh = [[buf(f"wh{i}{q}", [P, NW], F32R) for q in range(2)] for i in range(2)]
        wl = [[buf(f"wl{i}{q}", [P, NW], F32R) for q in range(2)] for i in range(2)]
        bias = buf("bias", [P, DIM])
        xr = [buf(f"xr{k}", [P, CT, DIM]) for k in range(TOPK)]
        xh = buf("xh", [P, KC, CAP], F32R)
        xl = buf("xl", [P, KC, CAP], F32R)
        h = buf("h", [P, 2, CAP])
        hh = buf("hh", [P, FC, CAP], F32R)
        hl = buf("hl", [P, FC, CAP], F32R)
        yo = [buf(f"yo{k}", [P, CT, DIM]) for k in range(TOPK)]

        bias_in = sem("bias_in")
        bias_added = sem("bias_added")
        w_in = [sem(f"w_in{i}") for i in range(2)]
        w_split = [sem(f"w_split{i}") for i in range(2)]
        w_used = sem("w_used")
        x_in = [sem(f"e_x_in{k}") for k in range(TOPK)]
        x_ps = sem("x_ps")
        xh_done = sem("xh_done")
        xl_done = sem("xl_done")
        h_ps = sem("h_ps")
        gelu_done = sem("gelu_done")
        hh_done = sem("hh_done")
        hl_done = sem("hl_done")
        y_ps = sem("y_ps")
        y_sb = sem("y_sb")
        y_out = [sem(f"y_out{k}") for k in range(TOPK)]
        passed = sem("e_passed")

        h_banks = [t_bank[:, 0, 0:CAP], t_bank[:, 1, 0:CAP], t_bank[:, 2, 0:CAP], s_bank[:, 2, 0:CAP]]
        NH = len(h_banks)
        y_banks = [banks[0][:, 0:DIM], banks[1][:, 0:DIM], banks[0][:, 0:DIM]]

        def program(turn, eng):
            with eng.Fori(0, E // 2 - 1) as rnd:
                for q in range(2):
                    turn(rnd, q, True, True)
            turn(E // 2 - 1, 0, True, False)
            turn(E // 2 - 1, 1, False, False)

        block = own.enter_context(nc.Block())

        def rows_of(dram, e, k):
            return dram.rearrange("(s t p) d -> s p t d", t=CT, p=P)[k * E + e]

        @block.sync
        def _(sp):
            sp.dma_start(bias[:, :], rows_to_all(ffn_bias, DIM)).then_inc(bias_in, 16)

            def load_weights(e):
                sp.wait_ge(w_split[0], 2 * e + 1)
                sp.dma_start(wr[0][:, :].rearrange("p (c f) -> p c f", c=KC),
                             w1[e].rearrange("(c p) f -> p c f", p=P)).then_inc(w_in[0], 16)
                sp.wait_ge(w_split[1], 2 * e + 1)
                sp.dma_start(wr[1][:, :].rearrange("p (c d) -> p c d", c=FC),
                             w2[e].rearrange("(c p) d -> p c d", p=P)).then_inc(w_in[1], 16)

            def load_rows(e, k):
                sp.dma_start(xr[k][:, :, :], rows_of(slot_rows, e, k)).then_inc(x_in[k], 16)

            load_weights(0)
            for k in range(TOPK):
                load_rows(0, k)

            def turn(rnd, q, more, more2):
                e = 2 * rnd + q
                if more:
                    load_weights(e + 1)
                for k in range(TOPK):
                    if more:
                        sp.wait_ge(x_ps, 2 * e + k + 1)
                        load_rows(e + 1, k)
                    sp.wait_ge(y_sb, CT * (2 * e + k + 1) + 1)
                    sp.dma_start(rows_of(slot_out[0:SLOTS, :], e, k), yo[k][:, :, :]).then_inc(y_out[k], 16)

            program(turn, sp)
            for k in range(TOPK):
                sp.wait_ge(y_out[k], 16 * E + 1)

        @block.gpsimd
        def _(pool):
            for i in range(2):
                pool.sem_inc(w_split[i], 1)

            def split(e, q):
                for i in range(2):
                    pool.wait_ge(w_in[i], 16 * (e + 1))
                    pool.wait_ge(w_used, e + 1)
                    pool.sem_inc(passed, 1)
                    pool.tensor_copy(wh[i][q][:, :], wr[i][:, :]).then_inc(w_split[i], 1)
                    pool.wait_ge(w_split[i], 2 * e + 2)
                    pool.tensor_tensor(wl[i][q][:, :], wr[i][:, :], wh[i][q][:, :].bitcast(F32),
                                       ALU.subtract).then_inc(w_split[i], 1)

            split(0, 0)

            def turn(rnd, q, more, more2):
                if more:
                    split(2 * rnd + q + 1, 1 - q)

            program(turn, pool)

        @block.scalar
        def _(act):
            act.sem_inc(gelu_done, NH)
            act.sem_inc(y_sb, 1)
            for k in range(TOPK):
                act.sem_inc(y_out[k], 1)

            def rows(u):
                act.wait_ge(x_ps, u + 1)
                act.activation(xh[:, :, :], s_bank[:, 0:KC, 0:CAP], ACT.Copy).then_inc(xh_done, 1)

            rows(0)

            def turn(rnd, q, more, more2):
                e = 2 * rnd + q
                for k in range(TOPK):
                    u = 2 * e + k
                    for f in range(FC):
                        act.wait_ge(h_ps, FC * u + f + 1)
                        act.wait_ge(hl_done, FC * u + f + 1)
                        act.activation(h[:, f % 2, :], h_banks[f % NH], ACT.Gelu_apprx_tanh).then_inc(gelu_done, 1)
                    if more or k == 0:
                        rows(u + 1)
                    act.wait_ge(y_out[k], 16 * e + 1)
                    for t in range(CT):
                        act.wait_ge(y_ps, CT * u + t + 1)
                        act.activation(yo[k][:, t, :], y_banks[t], ACT.Copy).then_inc(y_sb, 1)

            program(turn, act)

        @block.vector
        def _(dve):
            dve.sem_inc(hl_done, 2)

            def rows(u):
                dve.wait_ge(xh_done, u + 1)
                dve.tensor_tensor(xl[:, :, :], s_bank[:, 0:KC, 0:CAP], xh[:, :, :].bitcast(F32),
                                  ALU.subtract).then_inc(xl_done, 1)

            rows(0)
            dve.wait_ge(bias_in, 16)
            for b in range(B):
                for t in range(NT):
                    dve.tensor_tensor(hid[:, b, t, :], hid[:, b, t, :], bias[:, :], ALU.add).then_inc(bias_added, 1)

            def turn(rnd, q, more, more2):
                for k in range(TOPK):
                    u = 2 * (2 * rnd + q) + k
                    for f in range(FC):
                        dve.wait_ge(gelu_done, FC * u + f + 1 + NH)
                        dve.tensor_copy(hh[:, f, :], h[:, f % 2, :]).then_inc(hh_done, 1)
                        dve.wait_ge(hh_done, FC * u + f + 1)
                        dve.tensor_tensor(hl[:, f, :], h[:, f % 2, :], hh[:, f, :].bitcast(F32),
                                          ALU.subtract).then_inc(hl_done, 1)
                    if more or k == 0:
                        rows(u + 1)

            program(turn, dve)

        @block.tensor
        def _(pe):
            pe.sem_inc(w_used, 2)

            def transpose_rows(e, k, u):
                pe.wait_ge(x_in[k], 16 * (e + 1))
                for t in range(CT):
                    for c in range(KC):
                        m = pe.transpose(s_bank[:, c, t * P:(t + 1) * P], xr[k][:, t, c * P:(c + 1) * P], ident[:, :])
                m.then_inc(x_ps, 1)

            transpose_rows(0, 0, 0)

            def turn(rnd, q, more, more2):
                e = 2 * rnd + q
                w1h, w1l = (w[0][q][:, :].rearrange("p (c f) -> p c f", c=KC) for w in (wh, wl))
                w2h, w2l = (w[1][q][:, :].rearrange("p (c d) -> p c d", c=FC) for w in (wh, wl))
                for k in range(TOPK):
                    u = 2 * e + k
                    if k == 0:
                        pe.wait_ge(w_split[0], 2 * e + 3)
                    pe.wait_ge(xl_done, u + 1)
                    for f in range(FC):
                        cols = slice(f * P, (f + 1) * P)
                        pe.wait_ge(gelu_done, FC * u + f + 1)
                        steps = [(w, xx, c) for c in range(KC) for w, xx in ((w1h, xh), (w1h, xl), (w1l, xh))]
                        for i, (w, xx, c) in enumerate(steps):
                            m = pe.matmul(h_banks[f % NH], w[:, c, cols], xx[:, c, :], start=(i == 0),
                                          stop=(i == len(steps) - 1))
                        m.then_inc(h_ps, 1)
                    if k == 0:
                        transpose_rows(e, 1, u + 1)
                        pe.wait_ge(w_split[1], 2 * e + 3)
                    elif more:
                        transpose_rows(e + 1, 0, u + 1)
                    for t in range(CT):
                        rows = slice(t * P, (t + 1) * P)
                        pe.wait_ge(y_sb, CT * u + 1 if t < 2 else CT * u + 2)
                        for f in range(FC):
                            if t == 0:
                                pe.wait_ge(hl_done, FC * u + f + 3)
                            for i, (hx, w) in enumerate(((hh, w2h), (hh, w2l), (hl, w2h))):
                                m = pe.matmul(y_banks[t], hx[:, f, rows], w[:, f, :], start=(f == 0 and i == 0),
                                              stop=(f == FC - 1 and i == 2))
                        m.then_inc(y_ps, 1)
                pe.wait_ge(y_ps, CT * (2 * e + 2))
                pe.sem_inc(w_used, 1)

            program(turn, pe)


def combine(nc, common, slot_out, pos, gate, out):
    hid = common[0]
    sb = common[-1]
    with ExitStack() as own:
        def buf(name, shape, dt=F32):
            return sb(name, shape, dt, own)

        def sem(name):
            return own.enter_context(nc.semaphore(name))

        idx = [buf(f"idx{q}", [P, NT, TOPK], I32) for q in range(2)]
        ya = [buf(f"ya{q}", [P, NT, TOPK, DIM]) for q in range(2)]
        res = [buf(f"res{q}", [P, NT, DIM]) for q in range(2)]

        idx_done = sem("idx_done")
        fetched = [sem(f"fetched{q}") for q in range(2)]
        first_done = sem("first_done")
        res_done = sem("res_done")
        stored = [sem(f"stored{q}") for q in range(2)]
        pool_passed = sem("c_pool_passed")

        block = own.enter_context(nc.Block())

        @block.gpsimd
        def _(pool):
            pool.sem_inc(res_done, 2 * NT)
            with pool.Fori(0, B // 2) as rnd:
                for q in range(2):
                    b = 2 * rnd + q
                    pool.wait_ge(idx_done, b + 1)
                    pool.wait_ge(res_done, NT * b + NT)
                    pool.sem_inc(pool_passed, 1)
                    for t in range(NT):
                        for k in range(TOPK):
                            pool.indirect_dma_start(
                                out=ya[q][:, t, k, :], out_offset=None, in_=slot_out,
                                in_offset=bass.IndirectOffsetOnAxis(ap=idx[q][:, t, k:k + 1], axis=0),
                                bounds_check=SLOTS, oob_is_err=False).then_inc(fetched[q], 16)

        @block.vector
        def _(dve):
            for q in range(2):
                dve.sem_inc(stored[q], 1)
                dve.tensor_copy(idx[q][:, :, :], pos[:, NT * q:NT * q + NT, :]).then_inc(idx_done, 1)

            def turn(rnd, q, more):
                b = 2 * rnd + q
                dve.wait_ge(fetched[q], 16 * NT * TOPK * (rnd + 1))
                if more:
                    dve.tensor_copy(idx[q][:, :, :], pos[:, bass.ds(NT * (b + 2), NT), :]).then_inc(idx_done, 1)
                dve.wait_ge(stored[q], 16 * rnd + 1)
                for t in range(NT):
                    g = gate[:, bass.ds(NT * b + t, 1), :].rearrange("p o k -> p (o k)")
                    dve.scalar_tensor_tensor(out=res[q][:, t, :], in0=ya[q][:, t, 0, :], scalar=g[:, 0:1],
                                             in1=hid[:, b, t, :], op0=ALU.mult, op1=ALU.add).then_inc(first_done, 1)
                for t in range(NT):
                    g = gate[:, bass.ds(NT * b + t, 1), :].rearrange("p o k -> p (o k)")
                    dve.wait_ge(first_done, NT * b + t + 1)
                    dve.scalar_tensor_tensor(out=res[q][:, t, :], in0=ya[q][:, t, 1, :], scalar=g[:, 1:2],
                                             in1=res[q][:, t, :], op0=ALU.mult, op1=ALU.add).then_inc(res_done, 1)

            with dve.Fori(0, B // 2 - 1) as rnd:
                for q in range(2):
                    turn(rnd, q, True)
            for q in range(2):
                turn(B // 2 - 1, q, False)

        @block.sync
        def _(sp):
            with sp.Fori(0, B // 2) as rnd:
                for q in range(2):
                    b = 2 * rnd + q
                    sp.wait_ge(res_done, NT * (b + 3))
                    sp.dma_start(out[b].rearrange("(t p) d -> p t d", p=P), res[q][:, :, :]).then_inc(stored[q], 16)
            for q in range(2):
                sp.wait_ge(stored[q], 16 * (B // 2) + 1)


_INS = ["x", "txt", "L0_tok_ccm", "L0_tok_ccm_bias", "L0_tok_shifts", "L0_tok_slopes", "L0_tok_conv_w",
        "L0_tok_conv_b", "L0_attn_W_DKV", "L0_attn_W_UK", "L0_attn_W_UV", "L0_attn_W_UQ", "L0_attn_W_O",
        "L0_ffn_router_w", "L0_ffn_w1", "L0_ffn_w2", "L0_ffn_bias"]


def kernel(**inputs):
    import concourse.bacc as _bacc
    from concourse.bass_utils import run_bass_kernel_spmd as _run

    nc = _bacc.Bacc("TRN2", target_bir_lowering=False, num_devices=1)
    arrays, args = {}, []
    for name in _INS:
        a = np.ascontiguousarray(inputs[name])
        arrays[f"in_{name}"] = a
        args.append(nc.dram_tensor(f"in_{name}", a.shape, mybir.dt.from_np(a.dtype), kind="ExternalInput").ap())
    out = nc.dram_tensor("out", (B, T, DIM), F32, kind="ExternalOutput").ap()
    build(nc, *args, out)
    return _run(nc, [arrays], core_ids=[0]).results[0]["out"]
```

```python
from contextlib import ExitStack

import numpy as np

import concourse.bass as bass
from concourse import mybir

F32 = mybir.dt.float32
F32R = mybir.dt.float32r
BF16 = mybir.dt.bfloat16
I32 = mybir.dt.int32
U32 = mybir.dt.uint32
ALU = mybir.AluOpType
ACT = mybir.ActivationFunctionType
AX_X = mybir.AxisListType.X

P = 128
B = 8
NT = 3
T = NT * P
DIM = 256
KC = DIM // P
LAT = 64
HEADS = 16
HD = DIM // HEADS
HALF = HEADS // 2
CH = 3
PTS = 16
E = 8
TOPK = 2
FFN = 1024
FC = FFN // P
TILES = B * NT
CAP = TILES * P // E
CT = CAP // P
SLOTS = TOPK * E * CAP
EPS = 1e-5
SCALE = 1.0 / np.sqrt(HD)
MASKED = -1.0e30
Q_PARTS = (0, 0, 0, 1, 1, 2)
K_PARTS = (0, 1, 2, 0, 1, 0)
MROW = len(Q_PARTS) * HD
MPARTS = 2
SROWS = MROW + MPARTS
GH = 4
BANK_TILES = ((0, 2), (1,))
FAR = float(1 << 20)


def rows_to_all(ap, n):
    return bass.AP(tensor=ap.tensor, offset=ap.offset, ap=[[0, P], [1, n]])


def build(nc, x, txt, ccm, ccm_bias, shifts, slopes, conv_w, conv_b, w_dkv, w_uk, w_uv, w_uq, w_o,
          router_w, w1, w2, ffn_bias, out):
    qk_scratch = nc.dram_tensor("qk_scratch", [B, 2, 2, 3, P, T], BF16, kind="Internal").ap()
    v_scratch = nc.dram_tensor("v_scratch", [B, NT, P, DIM], F32, kind="Internal").ap()
    slot_rows = nc.dram_tensor("slot_rows", [SLOTS, DIM], F32, kind="Internal").ap()
    slot_out = nc.dram_tensor("slot_out", [SLOTS + P, DIM], F32, kind="Internal").ap()

    with ExitStack() as ctx:
        def sb(name, shape, dt=F32, where=None):
            return (where or ctx).enter_context(nc.sbuf_tensor(name, shape, dt))

        banks = [ctx.enter_context(nc.psum_tensor(f"bank{i}", [P, 512], F32)) for i in range(2)]
        s_bank = ctx.enter_context(nc.psum_tensor("s_bank", [P, 3, 512], F32))
        t_bank = ctx.enter_context(nc.psum_tensor("t_bank", [P, 3, 512], F32))

        hid = sb("hid", [P, B, NT, DIM])
        ident = sb("ident", [P, P])
        ident_b = sb("ident_b", [P, P], BF16)
        mask_q = sb("mask_q", [P, P], BF16)
        mask_k = sb("mask_k", [P, P], BF16)
        sum_rows = sb("sum_rows", [P, P])
        wo_pad = sb("wo_pad", [P, HEADS // GH, DIM])
        eps_t = sb("eps_t", [P, NT])
        neg_half = sb("neg_half", [P, NT])
        flag_i = sb("flag_i", [1, 1], I32)

        common = (hid, ident, ident_b, mask_q, mask_k, sum_rows, wo_pad, eps_t, neg_half, banks, s_bank, t_bank, sb)
        tokens(nc, common, flag_i, x, txt, ccm, ccm_bias, shifts, slopes, conv_w, conv_b,
               w_dkv, w_uk, w_uv, w_uq, w_o, qk_scratch, v_scratch, slot_rows, slot_out)
        attention(nc, common, qk_scratch, v_scratch)
        pos = sb("pos", [P, TILES, TOPK], I32)
        gate = sb("gate", [P, TILES, TOPK])
        routing(nc, common, router_w, slot_rows, pos, gate)
        experts(nc, common, w1, w2, ffn_bias, slot_rows, slot_out)
        combine(nc, common, slot_out, pos, gate, out)


def tokens(nc, common, flag_i, x, txt, ccm, ccm_bias, shifts, slopes, conv_w, conv_b,
           w_dkv, w_uk, w_uv, w_uq, w_o, qk_scratch, v_scratch, slot_rows, slot_out):
    hid, ident, ident_b, mask_q, mask_k, sum_rows, wo_pad, eps_t, neg_half, banks, s_bank, t_bank, sb = common
    IT = NT - 1
    W = DIM
    with ExitStack() as own:
        def buf(name, shape, dt=F32):
            return sb(name, shape, dt, own)

        def sem(name):
            return own.enter_context(nc.semaphore(name))

        prm = buf("prm", [P, 9 + 3 + 48 + 48 + 3 + 1])
        ccm_t = prm[:, 0:9]
        cbias = prm[:, 9:12]
        shift_t = prm[:, 12:60]
        slope_t = prm[:, 60:108]
        conv_t = prm[:, 108:111]
        convb_t = prm[:, 111:112]
        flag_f = buf("flag_f", [1, 2])
        curve_w = buf("curve_w", [P, CH * PTS])
        dkv = buf("dkv", [P, KC, LAT])
        uk = buf("uk", [P, DIM])
        uv = buf("uv", [P, DIM])
        uq = buf("uq", [P, KC, DIM])
        xin = buf("xin", [P, 2, IT, W * CH])
        g = buf("g", [P, CH, IT, W])
        r = buf("r", [P, CH, IT, W])
        acc = buf("acc", [P, IT, W])
        stats = buf("stats", [P, NT, 6])
        mv = buf("mv", [P, NT, 2])
        ve = buf("ve", [P, NT])
        rstd = buf("rstd", [P, NT])
        xn = buf("xn", [P, NT, DIM])
        xnT = buf("xnT", [P, KC, T])
        ckvT = buf("ckvT", [P, T])
        high = buf("high", [P, 2, 2, T], BF16)
        rest = buf("rest", [P, 2, 2, T])
        mid = buf("mid", [P, 2, 2, T], BF16)
        low = buf("low", [P, 2, 2, T], BF16)
        vals = buf("vals", [P, NT, DIM])
        zeros = buf("zeros", [P, 2048])

        consts_made = sem("consts_made")
        weights_in = sem("weights_in")
        flag_made = sem("flag_made")
        curve_made = sem("curve_made")
        text_in = sem("text_in")
        x_in = sem("x_in")
        x_free = sem("x_free")
        g_base = sem("g_base")
        g_step = sem("g_step")
        pt_step = sem("pt_step")
        g_free = sem("g_free")
        more_step = sem("more_step")
        tok_done = sem("tok_done")
        ln_step = sem("ln_step")
        var_done = sem("var_done")
        ve_done = sem("ve_done")
        rstd_done = sem("rstd_done")
        xn_done = sem("xn_done")
        xnT_ps = sem("xnT_ps")
        xnT_sb = sem("xnT_sb")
        ckv_ps = sem("ckv_ps")
        ckv_sb = sem("ckv_sb")
        qk_ps = sem("qk_ps")
        high_done = sem("high_done")
        rest_done = sem("rest_done")
        mid_done = sem("mid_done")
        low_done = sem("low_done")
        v_ps = sem("v_ps")
        v_sb = sem("v_sb")
        spilled = sem("spilled")
        zero_made = sem("zero_made")
        passed = sem("passed")
        zeroed = sem("zeroed")
        pool_passed = sem("t_pool_passed")
        NSPILL = 13

        xnT_bank = s_bank[:, 0:KC, 0:T]
        ckv_bank = s_bank[0:LAT, 2, 0:T]
        qk_bank = [[t_bank[:, 0, 0:T], t_bank[:, 1, 0:T]], [t_bank[:, 2, 0:T], banks[0][:, 0:T]]]

        block = own.enter_context(nc.Block())

        @block.gpsimd
        def _(pool):
            pool.memset(ident[:, :], 0.0).then_inc(consts_made, 1)
            pool.memset(mask_q[:, :], 0.0).then_inc(consts_made, 1)
            pool.memset(mask_k[:, :], 0.0).then_inc(consts_made, 1)
            pool.memset(sum_rows[:, :], 0.0).then_inc(consts_made, 1)
            pool.memset(wo_pad[:, :, :], 0.0).then_inc(consts_made, 1)
            pool.memset(uk[:, :], 0.0).then_inc(consts_made, 1)
            pool.memset(uv[:, :], 0.0).then_inc(consts_made, 1)
            pool.memset(ckvT[:, :], 0.0).then_inc(consts_made, 1)
            pool.memset(eps_t[:, :], EPS).then_inc(consts_made, 1)
            pool.memset(neg_half[:, :], -0.5).then_inc(consts_made, 1)
            pool.wait_ge(consts_made, 10)
            pool.affine_select(out=ident[:, :], in_=ident[:, :], compare_op=ALU.not_equal, fill=1.0, base=0,
                               pattern=[[-1, P]], channel_multiplier=1).then_inc(consts_made, 1)
            pool.affine_select(out=mask_q[:, :], in_=mask_q[:, :], compare_op=ALU.is_ge, fill=MASKED, base=0,
                               pattern=[[-1, P]], channel_multiplier=1).then_inc(consts_made, 1)
            pool.affine_select(out=mask_k[:, :], in_=mask_k[:, :], compare_op=ALU.is_ge, fill=MASKED, base=0,
                               pattern=[[1, P]], channel_multiplier=-1).then_inc(consts_made, 1)
            strips = sum_rows[:, :].rearrange("p (i c) -> p i c", i=GH)
            pool.affine_select(out=strips, in_=strips, compare_op=ALU.not_equal, fill=1.0, base=-HD,
                               pattern=[[-32, GH], [0, 32]], channel_multiplier=1).then_inc(consts_made, 1)
            pool.wait_ge(consts_made, 14)
            pool.tensor_copy(ident_b[:, :], ident[:, :]).then_inc(consts_made, 1)
            pool.memset(zeros[:, :], 0.0).then_inc(zero_made, 1)

            def rstds(b):
                pool.wait_ge(var_done, NT * b + NT)
                pool.tensor_tensor(ve[:, :], mv[:, :, 1], eps_t[:, :], ALU.add).then_inc(ve_done, 1)
                pool.wait_ge(ve_done, b + 1)
                pool.tensor_tensor(rstd[:, :], ve[:, :], neg_half[:, :], ALU.pow).then_inc(rstd_done, 1)

            def splits(b):
                pool.wait_ge(spilled, 16 * NSPILL * b + 1)
                for k in range(4):
                    half, s = k // 2, k % 2
                    pool.wait_ge(rest_done, 4 * b + k + 2)
                    pool.sem_inc(pool_passed, 1)
                    pool.tensor_copy(mid[:, half, s, :], rest[:, half, s, :]).then_inc(mid_done, 1)
                    pool.wait_ge(mid_done, 4 * b + k + 1)
                    pool.tensor_tensor(low[:, half, s, :], rest[:, half, s, :], mid[:, half, s, :],
                                       ALU.subtract).then_inc(low_done, 1)

            rstds(0)
            with pool.Fori(0, B - 1) as b:
                rstds(b + 1)
                splits(b)
            splits(B - 1)

        @block.sync
        def _(sp):
            sp.sem_inc(spilled, 1)
            sp.wait_ge(consts_made, 10)
            for dst, src in ((ccm_t, rows_to_all(ccm, 9)), (cbias, rows_to_all(ccm_bias, 3)),
                             (shift_t, rows_to_all(shifts, 48)), (slope_t, rows_to_all(slopes, 48)),
                             (conv_t, rows_to_all(conv_w, 3)), (convb_t, rows_to_all(conv_b, 1)),
                             (dkv[:, :, :], w_dkv.rearrange("(c p) n -> p c n", p=P)),
                             (uq[:, :, :], w_uq.rearrange("(c p) n -> p c n", p=P)),
                             (uk[0:LAT, :], w_uk), (uv[0:LAT, :], w_uv)):
                sp.dma_start(dst, src).then_inc(weights_in, 16)
            sp.dma_start(hid[:, :, NT - 1, :], txt.rearrange("b p d -> p b d")).then_inc(text_in, 16)
            for i in range(GH):
                sp.dma_start(wo_pad[32 * i:32 * i + HD, :, :],
                             w_o.rearrange("(g i d) n -> i d g n", i=GH, d=HD)[i]).then_inc(text_in, 16)
            sp.wait_ge(zero_made, 1)
            flat = slot_rows.rearrange("(a p) d -> a p d", p=P * 8)
            for a in range(flat.shape[0]):
                sp.dma_start(flat[a].rearrange("(p r) d -> p (r d)", p=P), zeros[:, :]).then_inc(zeroed, 16)
            sp.dma_start(slot_out[SLOTS:SLOTS + P, :], zeros[:, 0:DIM]).then_inc(zeroed, 16)
            with sp.Fori(0, B) as b:
                for k in range(4):
                    half, s = k // 2, k % 2
                    for part, (src, made, start) in enumerate(((high, high_done, 0), (mid, mid_done, 0),
                                                               (low, low_done, 1))):
                        sp.wait_ge(made, start + 4 * b + k + 1)
                        sp.dma_start(qk_scratch[b, half, s, part], src[:, half, s, :]).then_inc(spilled, 16)
                sp.wait_ge(v_sb, 2 * b + 3)
                sp.dma_start(v_scratch[b].rearrange("t p d -> p t d"), vals[:, :, :]).then_inc(spilled, 16)
            sp.wait_ge(spilled, 16 * NSPILL * B + 1)
            sp.wait_ge(zeroed, 16 * (flat.shape[0] + 1))
            sp.wait_ge(text_in, 16 * (1 + GH))

        @block.scalar
        def _(act):
            act.sem_inc(x_free, 2)
            act.sem_inc(v_sb, 1)
            act.wait_ge(x_free, 1)
            act.dma_start(xin[:, 0, :, :], x[0].rearrange("(j p) w c -> p j (w c)", p=P)).then_inc(x_in, 16)
            act.wait_ge(weights_in, 16 * 10)
            def colours(b, more):
                act.wait_ge(x_in, 16 * b + 16)
                act.wait_ge(g_free, b + 1)
                xv = xin[:, b % 2, :, :].rearrange("p j (w c) -> p j w c", c=CH)
                for d in range(CH):
                    act.activation(g[:, d, :, :], xv[:, :, :, 0], ACT.Identity, bias=cbias[:, d:d + 1],
                                   scale=ccm_t[:, d:d + 1]).then_inc(g_base, 1)
                if more:
                    act.wait_ge(x_free, b + 2)
                    act.wait_ge(g_base, CH * b + CH)
                    act.dma_start(xin[:, (b + 1) % 2, :, :],
                                  x[b + 1].rearrange("(j p) w c -> p j (w c)", p=P)).then_inc(x_in, 16)

            def products(b):
                act.wait_ge(xnT_ps, b + 2)
                act.activation(xnT[:, :, :], xnT_bank, ACT.Copy).then_inc(xnT_sb, 1)
                act.wait_ge(ckv_ps, b + 1)
                act.activation(ckvT[0:LAT, :], ckv_bank, ACT.Copy).then_inc(ckv_sb, 1)
                act.wait_ge(spilled, 16 * NSPILL * b + 1)
                for k in range(4):
                    half, s = k // 2, k % 2
                    act.wait_ge(qk_ps, 4 * b + k + 1)
                    act.activation(high[:, half, s, :], qk_bank[half][s], ACT.Copy,
                                   scale=float(SCALE) if s == 0 else 1.0).then_inc(high_done, 1)
                act.wait_ge(v_ps, 2 * b + 1)
                act.activation(vals[:, 0:2, :], banks[1][:, :].rearrange("p (t d) -> p t d", t=2),
                               ACT.Copy).then_inc(v_sb, 1)
                act.wait_ge(v_ps, 2 * b + 2)
                act.activation(vals[:, 2, :], s_bank[:, 2, 0:DIM], ACT.Copy).then_inc(v_sb, 1)

            colours(0, True)
            with act.Fori(0, B - 2) as b:
                colours(b + 1, True)
                products(b)
            colours(B - 1, False)
            products(B - 2)
            products(B - 1)

        @block.vector
        def _(dve):
            dve.wait_ge(weights_in, 16 * 10)
            for c in range(CH):
                dve.tensor_scalar(curve_w[:, c * PTS:(c + 1) * PTS], slope_t[:, c * PTS:(c + 1) * PTS],
                                  conv_t[:, c:c + 1], None, ALU.mult).then_inc(curve_made, 1)
            dve.tensor_reduce(flag_f[:, 0:1], slope_t[0:1, :].rearrange("p (c n) -> p c n", c=CH)[:, :, 1:PTS],
                              mybir.AxisListType.XY, ALU.max, apply_absolute_value=True).then_inc(flag_made, 1)
            dve.wait_ge(flag_made, 1)
            dve.tensor_scalar(flag_i[:, :], flag_f[:, 0:1], 0.0, None, ALU.not_equal).then_inc(flag_made, 1)
            dve.wait_ge(flag_made, 2)
            dve.wait_ge(curve_made, CH)
            more_points = dve.value_load(flag_i[0:1, 0:1], min_val=0, max_val=1)
            dve.wait_ge(text_in, 16 * (1 + GH))
            dve.sem_inc(g_free, 1)
            dve.sem_inc(rest_done, 1)

            def colours(b):
                xv = xin[:, b % 2, :, :].rearrange("p j (w c) -> p j w c", c=CH)
                for c in range(1, CH):
                    for d in range(CH):
                        if c == 1:
                            dve.wait_ge(g_base, CH * b + d + 1)
                        else:
                            dve.wait_ge(g_step, 2 * CH * b + d + 1)
                        dve.scalar_tensor_tensor(out=g[:, d, :, :], in0=xv[:, :, :, c],
                                                 scalar=ccm_t[:, c * CH + d:c * CH + d + 1], in1=g[:, d, :, :],
                                                 op0=ALU.mult, op1=ALU.add).then_inc(g_step, 1)
                dve.wait_ge(g_step, 2 * CH * b + 2 * CH)
                dve.sem_inc(x_free, 1)

            def curve(b):
                for c in range(CH):
                    dve.tensor_scalar(r[:, c, :, :], g[:, c, :, :], shift_t[:, c * PTS:c * PTS + 1], 0.0,
                                      ALU.subtract, ALU.max).then_inc(pt_step, 1)
                for c in range(CH):
                    dve.wait_ge(pt_step, 6 * b + (c + 1 if c == 0 else CH + c))
                    if c == 0:
                        dve.tensor_scalar(acc[:, :, :], r[:, 0, :, :], curve_w[:, 0:1], convb_t[:, 0:1],
                                          ALU.mult, ALU.add).then_inc(pt_step, 1)
                    else:
                        dve.scalar_tensor_tensor(out=acc[:, :, :], in0=r[:, c, :, :],
                                                 scalar=curve_w[:, c * PTS:c * PTS + 1], in1=acc[:, :, :],
                                                 op0=ALU.mult, op1=ALU.add).then_inc(pt_step, 1)
                dve.wait_ge(pt_step, 6 * b + 6)
                dve.sem_inc(passed, 1)
                with dve.If(more_points):
                    with dve.Fori(1, PTS) as i:
                        done = 6 * (PTS - 1) * b + 6 * (i - 1)
                        for c in range(CH):
                            dve.tensor_scalar(r[:, c, :, :], g[:, c, :, :], shift_t[:, bass.ds(c * PTS + i, 1)], 0.0,
                                              ALU.subtract, ALU.max).then_inc(more_step, 1)
                        for c in range(CH):
                            dve.wait_ge(more_step, done + CH + c)
                            dve.scalar_tensor_tensor(out=acc[:, :, :], in0=r[:, c, :, :],
                                                     scalar=curve_w[:, bass.ds(c * PTS + i, 1)], in1=acc[:, :, :],
                                                     op0=ALU.mult, op1=ALU.add).then_inc(more_step, 1)
                        dve.wait_ge(more_step, done + 2 * CH)
                        dve.sem_inc(passed, 1)
                dve.sem_inc(g_free, 1)
                dve.tensor_scalar(hid[:, b, 0:IT, :], acc[:, :, :], 0.0, 1.0, ALU.max, ALU.min).then_inc(tok_done, 1)

            def rests(b):
                dve.wait_ge(low_done, 4 * b + 1)
                for k in range(4):
                    half, s = k // 2, k % 2
                    dve.wait_ge(high_done, 4 * b + k + 1)
                    dve.scalar_tensor_tensor(out=rest[:, half, s, :], in0=qk_bank[half][s],
                                             scalar=float(SCALE) if s == 0 else 1.0,
                                             in1=high[:, half, s, :], op0=ALU.mult,
                                             op1=ALU.subtract).then_inc(rest_done, 1)

            def norms(b):
                dve.wait_ge(tok_done, b + 1)
                dve.sem_inc(passed, 1)
                for t in range(NT):
                    dve.bn_stats(stats[:, t, :], hid[:, b, t, :]).then_inc(ln_step, 1)
                dve.wait_ge(ln_step, NT * b + NT)
                dve.sem_inc(passed, 1)
                for t in range(NT):
                    dve.bn_aggr(mv[:, t, :], stats[:, t, :]).then_inc(var_done, 1)

            def scaled(b):
                dve.wait_ge(rstd_done, b + 1)
                dve.wait_ge(xnT_ps, b + 1)
                for t in range(NT):
                    dve.tensor_scalar(xn[:, t, :], hid[:, b, t, :], mv[:, t, 0:1], rstd[:, t:t + 1],
                                      ALU.subtract, ALU.mult).then_inc(xn_done, 1)

            dve.sem_inc(low_done, 1)
            colours(0)
            curve(0)
            norms(0)
            scaled(0)
            with dve.Fori(0, B - 1) as b:
                colours(b + 1)
                curve(b + 1)
                norms(b + 1)
                rests(b)
                scaled(b + 1)
            rests(B - 1)

        @block.tensor
        def _(pe):
            pe.wait_ge(consts_made, 15)
            pe.sem_inc(xnT_ps, 1)
            pe.wait_ge(weights_in, 16 * 10)
            with pe.Fori(0, B) as b:
                pe.wait_ge(xn_done, NT * b + NT)
                for t in range(NT):
                    for c in range(KC):
                        m = pe.transpose(s_bank[:, c, t * P:(t + 1) * P], xn[:, t, c * P:(c + 1) * P], ident[:, :])
                m.then_inc(xnT_ps, 1)
                pe.wait_ge(xnT_sb, b + 1)
                pe.wait_ge(v_sb, 2 * b + 1)
                for c in range(KC):
                    m = pe.matmul(ckv_bank, dkv[:, c, :], xnT[:, c, :], start=(c == 0), stop=(c == KC - 1))
                m.then_inc(ckv_ps, 1)
                pe.wait_ge(rest_done, 4 * b + 1)
                for half in range(2):
                    cols = slice(half * P, (half + 1) * P)
                    for c in range(KC):
                        m = pe.matmul(qk_bank[half][0], uq[:, c, cols], xnT[:, c, :], start=(c == 0), stop=(c == KC - 1))
                    m.then_inc(qk_ps, 1)
                    if half == 0:
                        pe.wait_ge(ckv_sb, b + 1)
                    pe.matmul(qk_bank[half][1], uk[:, cols], ckvT[:, :], start=True, stop=True).then_inc(qk_ps, 1)
                for t in range(NT):
                    dst = banks[1][:, t * DIM:(t + 1) * DIM] if t < 2 else s_bank[:, 2, 0:DIM]
                    m = pe.matmul(dst, ckvT[:, t * P:(t + 1) * P], uv[:, :], start=True, stop=True)
                    if t:
                        m.then_inc(v_ps, 1)


def attention(nc, common, qk_scratch, v_scratch):
    hid, ident, ident_b, mask_q, mask_k, sum_rows, wo_pad, eps_t, neg_half, banks, s_bank, t_bank, sb = common
    misc, ctx_bank = banks[0], banks[1]
    misc_b = misc[:, :].bitcast(BF16)
    NG = 2
    with ExitStack() as own:
        def buf(name, shape, dt=F32):
            return sb(name, shape, dt, own)

        def sem(name):
            return own.enter_context(nc.semaphore(name))

        qs = [buf(f"qs{h}", [SROWS, HALF, T], BF16) for h in range(2)]
        ks = [buf(f"ks{h}", [SROWS, HALF, T], BF16) for h in range(2)]
        vb = [buf(f"vb{h}", [P, NT, HALF, 32]) for h in range(2)]
        zrow = buf("zrow", [MPARTS, GH * T], BF16)
        mx = buf("mx", [P, NG, NT, GH])
        ms = buf("ms", [P, NG, NT, MPARTS, GH], BF16)
        mT = buf("mT", [MPARTS * GH, NG, T], BF16)
        pt = buf("pt", [P, 4, 2, 2 * T])
        cx = buf("cx", [P, NG, T])
        rs = buf("rs", [P, NG, NT, GH])
        wide = buf("wide", [P, NG, NT, GH, 32])
        cn = buf("cn", [P, HEADS // GH, T])

        ready = sem("ready")
        stack_in = [[sem(f"stack_in{h}{q}") for q in range(2)] for h in range(2)]
        v_in = [sem(f"v_in{h}") for h in range(2)]
        s_ready = sem("s_ready")
        s_read = sem("s_read")
        m_part = sem("m_part")
        mT_ps = sem("mT_ps")
        mT_sb = sem("mT_sb")
        m_in = [sem(f"m_in{g}") for g in range(NG)]
        t_ready = sem("t_ready")
        exp_done = sem("exp_done")
        pv_done = sem("pv_done")
        ctx_sb = sem("ctx_sb")
        sums_ps = sem("sums_ps")
        rs_done = sem("rs_done")
        spread_ps = sem("spread_ps")
        wide_done = sem("wide_done")
        pool_passed = sem("a_pool_passed")
        cn_done = sem("cn_done")
        wo_ps = sem("wo_ps")
        hid_add = sem("hid_add")
        misc_free = sem("misc_free")
        s_used = sem("s_used")
        NL = len(Q_PARTS) + len(K_PARTS) + 1

        block = own.enter_context(nc.Block())

        def program(turn, eng):
            turn(-1, 1, True, False, False)
            for half in range(2):
                turn(0, half, True, True, half == 1)
            with eng.Fori(1, B - 1) as rnd:
                for half in range(2):
                    turn(rnd, half, True, True, True)
            for half in range(2):
                turn(B - 1, half, half == 0, True, True)
            turn(B, 0, False, False, True)

        def misc_uses(rnd, half):
            if isinstance(rnd, int) and rnd < 1:
                return 0 if rnd < 0 else 1 + 4 * half
            skipped = 1 if isinstance(rnd, int) and rnd == B else 0
            return 14 * rnd - 3 + (8 if half else 0) - skipped

        @block.sync
        def _(sp):
            def load(rnd, half, grp):
                heads = slice(grp * GH, (grp + 1) * GH)
                for s, dst, parts in ((0, qs[half], Q_PARTS), (1, ks[half], K_PARTS)):
                    for at, part in enumerate(parts):
                        src = qk_scratch[rnd, half, s, part].rearrange("(h d) t -> d h t", d=HD)[:, heads, :]
                        sp.dma_start(dst[at * HD:(at + 1) * HD, heads, :], src).then_inc(stack_in[half][grp], 16)
                sp.dma_start(qs[half][MROW:SROWS, heads, :],
                             zrow[:, :].rearrange("p (h t) -> p h t", h=GH)).then_inc(stack_in[half][grp], 16)

            def load_v(rnd, half):
                src = v_scratch[rnd].rearrange("t p (h d) -> p t h d", d=HD)[:, :, half * HALF:(half + 1) * HALF, :]
                for t in range(NT):
                    sp.dma_start(vb[half][:, t, :, 0:HD], src[:, t]).then_inc(v_in[half], 16)

            def max_rows(half, grp, n):
                G = NG * n + grp
                sp.wait_ge(mT_sb, G + 1)
                for a in range(MPARTS):
                    sp.dma_start(qs[half][MROW + a:MROW + a + 1, grp * GH:(grp + 1) * GH, :],
                                 mT[a * GH:(a + 1) * GH, grp, :]).then_inc(m_in[grp], 16)

            sp.wait_ge(ready, 5)
            for half in range(2):
                for grp in range(NG):
                    load(0, half, grp)
                load_v(0, half)

            def turn(rnd, half, nxt, cur, prev):
                n = 2 * rnd + half
                if cur:
                    max_rows(half, 1, n)
                if nxt:
                    max_rows(1 - half, 0, n + 1)
                if cur and not (isinstance(rnd, int) and rnd == B - 1):
                    for grp in range(NG):
                        sp.wait_ge(t_ready, 2 * (4 * n + 2 * grp + 2))
                        load(rnd + 1, half, grp)
                    sp.wait_ge(pv_done, NG * n + NG + 2)
                    load_v(rnd + 1, half)

            program(turn, sp)

        @block.gpsimd
        def _(pool):
            pool.memset(zrow[:, :], 0.0).then_inc(ready, 1)
            for h in range(2):
                pool.wait_ge(ready, 1 + 2 * h)
                pool.memset(ks[h][MROW:SROWS, :, :], -1.0).then_inc(ready, 1)
                pool.wait_ge(ready, 2 + 2 * h)
                pool.memset(vb[h][:, :, :, HD:2 * HD], 1.0).then_inc(ready, 1)

            def widen(n, grp):
                pool.wait_ge(rs_done, NG * n + grp + 1)
                pool.sem_inc(pool_passed, 1)
                src = rs[:, grp, :, :].rearrange("p j (h o) -> p j h o", o=1).to_broadcast([P, NT, GH, 32])
                pool.tensor_copy(wide[:, grp, :, :, :], src).then_inc(wide_done, 1)

            def turn(rnd, half, nxt, cur, prev):
                n = 2 * rnd + half
                if prev:
                    widen(n - 1, 1)
                if cur:
                    widen(n, 0)

            program(turn, pool)

        @block.tensor
        def _(pe):
            pe.sem_inc(pv_done, 2)

            def misc_wait(use):
                pe.wait_ge(misc_free, use)

            def score_pair(n, half, rnd, p):
                m = 4 * n + p
                if p % 2 == 0:
                    pe.wait_ge(stack_in[half][p // 2], 16 * NL * (rnd + 1))
                for g, tiles in enumerate(BANK_TILES):
                    pe.wait_ge(s_read, 2 * m + g + 1)
                    for i in range(2):
                        h = 2 * p + i
                        for j in tiles:
                            dst, w = s_region(s_bank, j, i)
                            pe.matmul(dst, qs[half][:, h, j * P:(j + 1) * P], ks[half][:, h, 0:w], start=True, stop=False)
                            mm = pe.matmul(dst[:, j * P:(j + 1) * P], ident_b[:, :], mask_q[:, :], start=False, stop=True)
                    mm.then_inc(s_ready, 1)

            def exp_pair(n, half, p):
                m = 4 * n + p
                if p % 2 == 0:
                    pe.wait_ge(m_in[p // 2], 16 * MPARTS * (n + 1))
                for g, tiles in enumerate(BANK_TILES):
                    pe.wait_ge(exp_done, 2 * m + g + 1)
                    for i in range(2):
                        h = 2 * p + i
                        for j in tiles:
                            dst, w = s_region(t_bank, 2 - j, i)
                            pe.matmul(dst, ks[half][:, h, j * P:(j + 1) * P], qs[half][:, h, j * P:T], start=True, stop=False)
                            mm = pe.matmul(dst[:, 0:P], ident_b[:, :], mask_k[:, :], start=False, stop=True)
                    mm.then_inc(t_ready, 1)

            def values(n, half, rnd, grp):
                G = NG * n + grp
                pe.wait_ge(exp_done, 2 + 2 * (4 * n + 2 * grp + 2))
                pe.wait_ge(v_in[half], 16 * NT * (rnd + 1))
                pe.wait_ge(ctx_sb, G)
                for j in range(NT):
                    for i in range(GH):
                        src = pt[:, 2 * grp + i // 2, i % 2, :]
                        at = (0, T, T + 2 * P)[j]
                        mm = pe.matmul(ctx_bank[32 * i:32 * i + 32, j * P:T], vb[half][:, j, grp * GH + i, :],
                                       src[:, at:at + T - j * P], start=(j == 0), stop=(j == NT - 1))
                mm.then_inc(pv_done, 1)

            def turn_sums(n, grp, use):
                pe.wait_ge(ctx_sb, NG * n + grp + 1)
                misc_wait(use)
                for j in range(NT):
                    mm = pe.transpose(misc[:, j * P:(j + 1) * P], cx[:, grp, j * P:(j + 1) * P], ident[:, :])
                mm.then_inc(sums_ps, 1)

            def spread(n, grp, use):
                pe.wait_ge(wide_done, NG * n + grp + 1)
                misc_wait(use)
                for j in range(NT):
                    mm = pe.transpose(misc[:, j * P:(j + 1) * P], wide[:, grp, j, :, :].rearrange("p h c -> p (h c)"),
                                      ident[:, :])
                mm.then_inc(spread_ps, 1)

            def turn_maxima(n, grp, use):
                pe.wait_ge(m_part, MPARTS * (NG * n + grp + 1))
                misc_wait(use)
                for j in range(NT):
                    mm = pe.transpose(misc_b[0:MPARTS * GH, j * P:(j + 1) * P],
                                      ms[:, grp, j, :, :].rearrange("p a h -> p (a h)"), ident_b[:, :])
                mm.then_inc(mT_ps, 1)

            def project(rnd, tiles, use):
                pe.wait_ge(cn_done, 4 * (rnd + 1))
                misc_wait(use)
                for at, t in enumerate(tiles):
                    for g in range(HEADS // GH):
                        mm = pe.matmul(misc[:, at * DIM:(at + 1) * DIM], cn[:, g, t * P:(t + 1) * P],
                                       wo_pad[:, g, :], start=(g == 0), stop=(g == HEADS // GH - 1))
                mm.then_inc(wo_ps, 1)

            def turn(rnd, half, nxt, cur, prev):
                n = 2 * rnd + half
                use = misc_uses(rnd, half)
                prnd = rnd if half else rnd - 1
                for p in range(4):
                    if nxt:
                        score_pair(n + 1, 1 - half, rnd + half, p)
                    if cur:
                        exp_pair(n, half, p)
                    if cur and p == 0:
                        turn_maxima(n, 1, use)
                        use = use + 1
                    if nxt and p == 2:
                        turn_maxima(n + 1, 0, use)
                        use = use + 1
                    if prev and p == 0:
                        values(n - 1, 1 - half, prnd, 1)
                    if prev and p == 1:
                        turn_sums(n - 1, 1, use)
                        use = use + 1
                    if prev and p == 2:
                        spread(n - 1, 1, use)
                        use = use + 1
                    if cur and p == 2:
                        values(n, half, rnd, 0)
                    if cur and p == 3:
                        turn_sums(n, 0, use)
                        use = use + 1
                    if prev and p == 3 and half == 0:
                        for tiles in ((0, 1), (2,)):
                            project(rnd - 1, tiles, use)
                            use = use + 1
                    if cur and p == 3:
                        spread(n, 0, use)
                        use = use + 1

            program(turn, pe)

        @block.scalar
        def _(act):
            act.sem_inc(exp_done, 2)

            def exps(n, p):
                m = 4 * n + p
                act.wait_ge(pv_done, NG * n + p // 2 + 1)
                for g, tiles in enumerate(BANK_TILES):
                    act.wait_ge(t_ready, 2 * m + g + 1)
                    for j in tiles:
                        at = (0, T, T + 2 * P)[j]
                        ins = act.activation(pt[:, p, :, at:at + T - j * P], pair_region(t_bank, 2 - j), ACT.Exp)
                    ins.then_inc(exp_done, 1)

            def maxima_rows(n, grp):
                G = NG * n + grp
                act.wait_ge(mT_ps, G + 1)
                if not isinstance(n, int) or n > 0:
                    act.wait_ge(m_in[grp], 16 * MPARTS * n)
                act.activation(mT[:, grp, :], misc_b[0:MPARTS * GH, 0:T], ACT.Copy).then_inc(mT_sb, 1)
                act.wait_ge(mT_sb, G + 1)
                act.sem_inc(misc_free, 1)

            def contexts(n, grp):
                G = NG * n + grp
                act.wait_ge(pv_done, G + 3)
                act.wait_ge(cn_done, G - 1 if not isinstance(G, int) else max(G - 1, 0))
                act.activation(cx[:, grp, :], ctx_bank[:, 0:T], ACT.Copy).then_inc(ctx_sb, 1)

            def turn(rnd, half, nxt, cur, prev):
                n = 2 * rnd + half
                for p in range(4):
                    if cur:
                        exps(n, p)
                    if cur and p == 0:
                        maxima_rows(n, 1)
                    if nxt and p == 2:
                        maxima_rows(n + 1, 0)
                    if prev and p == 0:
                        contexts(n - 1, 1)
                    if cur and p == 2:
                        contexts(n, 0)

            program(turn, act)

        @block.vector
        def _(dve):
            dve.sem_inc(s_read, 2)

            def maxima(n, p):
                m = 4 * n + p
                for g, tiles in enumerate(BANK_TILES):
                    dve.wait_ge(s_ready, 2 * m + g + 1)
                    for j in tiles:
                        ins = dve.tensor_reduce(mx[:, p // 2, j, 2 * (p % 2):2 * (p % 2) + 2], pair_region(s_bank, j),
                                                AX_X, ALU.max)
                    ins.then_inc(s_read, 1)

            def split(n, grp):
                G = NG * n + grp
                dve.wait_ge(s_read, 2 + 2 * (4 * n + 2 * grp + 2))
                dve.wait_ge(mT_ps, G - 1 if not isinstance(G, int) else max(G - 1, 0))
                dve.tensor_copy(ms[:, grp, :, 0, :], mx[:, grp, :, :]).then_inc(m_part, 1)
                dve.wait_ge(m_part, MPARTS * G + 1)
                dve.tensor_tensor(ms[:, grp, :, 1, :], mx[:, grp, :, :], ms[:, grp, :, 0, :],
                                  ALU.subtract).then_inc(m_part, 1)

            def reciprocals(n, grp):
                G = NG * n + grp
                dve.wait_ge(sums_ps, G + 1)
                sums = misc[:, 0:T].rearrange("p (j h c) -> p j h c", j=NT, h=GH)[:, :, :, HD]
                dve.reciprocal(rs[:, grp, :, :], sums).then_inc(rs_done, 1)
                dve.wait_ge(rs_done, G + 1)
                dve.sem_inc(misc_free, 1)

            def normalise(rnd, half, grp):
                G = NG * (2 * rnd + half) + grp
                dve.wait_ge(spread_ps, G + 1)
                dve.wait_ge(wo_ps, 2 * rnd)
                dve.tensor_tensor(cn[:, NG * half + grp, :], misc[:, 0:T], cx[:, grp, :],
                                  ALU.mult).then_inc(cn_done, 1)
                dve.wait_ge(cn_done, G + 1)
                dve.sem_inc(misc_free, 1)

            def residual(rnd, k):
                dve.wait_ge(wo_ps, 2 * rnd + k + 1)
                tiles = slice(0, 2) if k == 0 else slice(2, 3)
                src = misc[:, 0:(2 - k) * DIM].rearrange("p (t d) -> p t d", d=DIM)
                dve.tensor_tensor(hid[:, rnd, tiles, :], hid[:, rnd, tiles, :], src, ALU.add).then_inc(hid_add, 1)
                dve.wait_ge(hid_add, 2 * rnd + k + 1)
                dve.sem_inc(misc_free, 1)

            def turn(rnd, half, nxt, cur, prev):
                n = 2 * rnd + half
                for p in range(4):
                    if nxt:
                        maxima(n + 1, p)
                    if nxt and p == 1:
                        split(n + 1, 0)
                    if prev and p == 1:
                        reciprocals(n - 1, 1)
                    if prev and p == 2:
                        normalise(rnd if half else rnd - 1, 1 - half, 1)
                    if nxt and p == 3:
                        split(n + 1, 1)
                    if cur and p == 3:
                        reciprocals(n, 0)
                    if prev and p == 3 and half == 0:
                        residual(rnd - 1, 0)
                        residual(rnd - 1, 1)
                    if cur and p == 3:
                        normalise(rnd, half, 0)

            program(turn, dve)


def s_region(bank, j, i):
    w = (j + 1) * P
    if j == 2:
        return bank[:, i, 0:w], w
    if j == 1:
        return bank[:, 2, i * w:(i + 1) * w], w
    return bank[:, i, T:T + P], w


def pair_region(bank, j):
    w = (j + 1) * P
    if j == 2:
        return bank[:, 0:2, 0:w]
    if j == 1:
        return bank[:, 2, :].rearrange("p (i c) -> p i c", i=2)
    return bank[:, 0:2, T:T + P]


def routing(nc, common, router_w, slot_rows, pos, gate):
    hid, ident, ident_b, mask_q, mask_k, sum_rows, wo_pad, eps_t, neg_half, banks, s_bank, t_bank, sb = common
    KE = TOPK * E
    with ExitStack() as own:
        def buf(name, shape, dt=F32):
            return sb(name, shape, dt, own)

        def sem(name):
            return own.enter_context(nc.semaphore(name))

        rw = buf("rw", [P, KC, E])
        tri = buf("tri", [P, P], BF16)
        ones = buf("ones", [P, P], BF16)
        iota_i = buf("iota_i", [P, TOPK, E], I32)
        base_i = buf("base_i", [P, TOPK, E], I32)
        iota_e = buf("iota_e", [P, TOPK, E])
        base = buf("base", [P, TOPK, E])
        stats = buf("r_stats", [P, NT, 6])
        mv = buf("r_mv", [P, NT, 2])
        ve = buf("r_ve", [P, NT])
        rstd = buf("r_rstd", [P, NT])
        xn = [buf(f"r_xn{q}", [P, NT, DIM]) for q in range(2)]
        xnT = buf("r_xnT", [P, KC, T])
        logits = buf("logits", [P, NT, E])
        top = buf("top", [P, NT, 8])
        top_i = buf("top_i", [P, NT, 8], U32)
        top_f = buf("top_f", [P, NT, TOPK])
        shifted = buf("shifted", [P, NT, E])
        expd = buf("expd", [P, NT, E])
        ssum = buf("ssum", [P, NT])
        rsum = buf("rsum", [P, NT])
        etop = buf("etop", [P, NT, TOPK])
        oh = buf("oh", [P, NT, TOPK, E])
        ohb = buf("ohb", [P, NT, KE], BF16)
        seen = buf("seen", [P, NT + 1, KE], BF16)
        pick = buf("pick", [P, NT, TOPK, E])
        rank = buf("rank", [P, NT, TOPK])
        first = buf("first", [P, NT, TOPK])
        full = buf("full", [P, NT, TOPK])
        slot_f = buf("slot_f", [P, NT, TOPK])
        slot_i = [buf(f"slot_i{q}", [P, NT, TOPK], I32) for q in range(2)]

        made = sem("r_made")
        rw_in = sem("rw_in")
        step = sem("r_step")
        passed = sem("r_passed")
        var_done = sem("r_var")
        ve_done = sem("r_ve_done")
        rstd_done = sem("r_rstd_done")
        xn_done = sem("r_xn_done")
        xnT_ps = sem("r_xnT_ps")
        xnT_sb = sem("r_xnT_sb")
        log_ps = sem("log_ps")
        shift_done = sem("shift_done")
        exp_done = sem("r_exp_done")
        oh_done = sem("oh_done")
        rank_ps = sem("rank_ps")
        slot_done = sem("slot_done")
        sent = [sem(f"sent{q}") for q in range(2)]
        rows_free = sem("rows_free")
        pool_passed = sem("pool_passed")

        rank_bank = banks[1][:, 0:NT * KE].rearrange("p (t k e) -> p t k e", t=NT, k=TOPK)
        log_bank = banks[0][:, 0:NT * E].rearrange("p (t e) -> p t e", t=NT)
        block = own.enter_context(nc.Block())

        @block.sync
        def _(sp):
            sp.dma_start(rw[:, :, :], router_w.rearrange("(c p) e -> p c e", p=P)).then_inc(rw_in, 16)

        @block.gpsimd
        def _(pool):
            pool.memset(tri[:, :], 1.0).then_inc(made, 1)
            pool.memset(ones[:, :], 1.0).then_inc(made, 1)
            pool.memset(seen[:, :, :], 0.0).then_inc(made, 1)
            pool.iota(iota_i[:, :, :], pattern=[[0, TOPK], [1, E]], base=0, channel_multiplier=0).then_inc(made, 1)
            pool.iota(base_i[:, :, :], pattern=[[E * CAP, TOPK], [CAP, E]], base=0,
                      channel_multiplier=0).then_inc(made, 1)
            pool.wait_ge(made, 5)
            pool.affine_select(out=tri[:, :], in_=tri[:, :], compare_op=ALU.is_gt, fill=0.0, base=0,
                               pattern=[[1, P]], channel_multiplier=-1).then_inc(made, 1)
            pool.tensor_copy(iota_e[:, :, :], iota_i[:, :, :]).then_inc(made, 1)
            pool.tensor_copy(base[:, :, :], base_i[:, :, :]).then_inc(made, 1)
            pool.sem_inc(rows_free, 2)

            def turn(rnd, start):
                for q in range(2):
                    b = 2 * rnd + q
                    pool.wait_ge(var_done, NT * b + NT)
                    pool.tensor_tensor(ve[:, :], mv[:, :, 1], eps_t[:, :], ALU.add).then_inc(ve_done, 1)
                    pool.wait_ge(ve_done, b + 1)
                    pool.tensor_tensor(rstd[:, :], ve[:, :], neg_half[:, :], ALU.pow).then_inc(rstd_done, 1)
                    if q == 1 or not start:
                        pool.wait_ge(sent[1 - q], 16 * NT * TOPK * (rnd + q))
                        pool.sem_inc(rows_free, 1)
                    pool.wait_ge(slot_done, b + 1)
                    pool.sem_inc(pool_passed, 1)
                    for t in range(NT):
                        for k in range(TOPK):
                            pool.indirect_dma_start(
                                out=slot_rows, out_offset=bass.IndirectOffsetOnAxis(ap=slot_i[q][:, t, k:k + 1], axis=0),
                                in_=xn[q][:, t, :], in_offset=None, bounds_check=SLOTS - 1,
                                oob_is_err=False).then_inc(sent[q], 16)

            turn(0, True)
            with pool.Fori(1, B // 2) as rnd:
                turn(rnd, False)
            for q in range(2):
                pool.wait_ge(sent[q], 16 * (B // 2) * NT * TOPK)

        @block.scalar
        def _(act):
            with act.Fori(0, B) as b:
                act.wait_ge(shift_done, b + 1)
                act.activation(expd[:, :, :], shifted[:, :, :], ACT.Exp).then_inc(exp_done, 1)

        @block.vector
        def _(dve):
            dve.wait_ge(made, 8)
            per = 30

            with dve.Fori(0, B // 2) as rnd:
                for q in range(2):
                    b = 2 * rnd + q
                    k = [0]

                    def then(ins, last=True):
                        k[0] += 1
                        ins.then_inc(step, 1)
                        if last:
                            dve.wait_ge(step, per * b + k[0])

                    for t in range(NT):
                        then(dve.bn_stats(stats[:, t, :], hid[:, b, t, :]), t == NT - 1)
                    dve.sem_inc(passed, 1)
                    for t in range(NT):
                        dve.bn_aggr(mv[:, t, :], stats[:, t, :]).then_inc(var_done, 1)
                    dve.wait_ge(rstd_done, b + 1)
                    dve.wait_ge(rows_free, b + 1)
                    for t in range(NT):
                        dve.tensor_scalar(xn[q][:, t, :], hid[:, b, t, :], mv[:, t, 0:1], rstd[:, t:t + 1],
                                          ALU.subtract, ALU.mult).then_inc(xn_done, 1)
                    dve.wait_ge(xnT_ps, b + 1)
                    dve.tensor_copy(xnT[:, :, :], s_bank[:, 0:KC, 0:T]).then_inc(xnT_sb, 1)
                    dve.wait_ge(log_ps, b + 1)
                    then(dve.tensor_copy(logits[:, :, :], log_bank))
                    dve.sem_inc(passed, 1)
                    for t in range(NT):
                        then(dve.max(top[:, t, :], logits[:, t, :]), t == NT - 1)
                    dve.tensor_tensor(shifted[:, :, :], logits[:, :, :], top[:, :, 0:1].to_broadcast([P, NT, E]),
                                      ALU.subtract).then_inc(shift_done, 1)
                    for t in range(NT):
                        then(dve.max_index(top_i[:, t, :], top[:, t, :], logits[:, t, :]), t == NT - 1)
                    then(dve.tensor_copy(top_f[:, :, :], top_i[:, :, 0:TOPK]))
                    for c in range(TOPK):
                        then(dve.tensor_tensor(oh[:, :, c, :], iota_e[:, 0:1, :].to_broadcast([P, NT, E]),
                                               top_f[:, :, c:c + 1].to_broadcast([P, NT, E]), ALU.is_equal), c == 1)
                    then(dve.tensor_copy(ohb[:, :, :], oh[:, :, :, :].rearrange("p t k e -> p t (k e)")))
                    for t in range(NT):
                        ins = dve.tensor_tensor(seen[:, t + 1, :], seen[:, t, :], ohb[:, t, :], ALU.add)
                        if t < NT - 1:
                            then(ins)
                        else:
                            ins.then_inc(oh_done, 1)
                    dve.wait_ge(exp_done, b + 1)
                    then(dve.tensor_reduce(ssum[:, :], expd[:, :, :], AX_X, ALU.add))
                    then(dve.reciprocal(rsum[:, :], ssum[:, :]), False)
                    for c in range(TOPK):
                        then(dve.tensor_tensor(pick[:, :, c, :], oh[:, :, c, :], expd[:, :, :], ALU.mult), c == 1)
                    then(dve.tensor_reduce(etop[:, :, :], pick[:, :, :, :], AX_X, ALU.add))
                    then(dve.tensor_tensor(gate[:, bass.ds(NT * b, NT), :], etop[:, :, :],
                                           rsum[:, :].rearrange("p (t o) -> p t o", o=1).to_broadcast([P, NT, TOPK]),
                                           ALU.mult))
                    for t in range(NT):
                        ins = dve.tensor_tensor(pick[:, t, :, :], base[:, :, :], oh[:, t, :, :], ALU.mult)
                        if t < NT - 1:
                            ins.then_inc(passed, 1)
                        else:
                            then(ins)
                    then(dve.tensor_reduce(first[:, :, :], pick[:, :, :, :], AX_X, ALU.add))
                    dve.wait_ge(rank_ps, b + 1)
                    dve.tensor_copy(seen[:, 0, :], seen[:, NT, :]).then_inc(passed, 1)
                    then(dve.tensor_tensor(pick[:, :, :, :], rank_bank, oh[:, :, :, :], ALU.mult))
                    then(dve.tensor_reduce(rank[:, :, :], pick[:, :, :, :], AX_X, ALU.add))
                    then(dve.tensor_scalar(full[:, :, :], rank[:, :, :], float(CAP), FAR, ALU.is_ge, ALU.mult), False)
                    then(dve.tensor_tensor(slot_f[:, :, :], rank[:, :, :], first[:, :, :], ALU.add))
                    then(dve.tensor_tensor(slot_f[:, :, :], slot_f[:, :, :], full[:, :, :], ALU.add))
                    dve.tensor_copy(slot_i[q][:, :, :], slot_f[:, :, :]).then_inc(slot_done, 1)
                    then(dve.tensor_scalar(pos[:, bass.ds(NT * b, NT), :], slot_f[:, :, :], float(SLOTS), None, ALU.min))
                    assert k[0] == per, k[0]

        @block.tensor
        def _(pe):
            pe.wait_ge(rw_in, 16)
            pe.wait_ge(made, 8)
            with pe.Fori(0, B // 2) as rnd:
                for q in range(2):
                    b = 2 * rnd + q
                    pe.wait_ge(xn_done, NT * b + NT)
                    for t in range(NT):
                        for c in range(KC):
                            m = pe.transpose(s_bank[:, c, t * P:(t + 1) * P], xn[q][:, t, c * P:(c + 1) * P], ident[:, :])
                    m.then_inc(xnT_ps, 1)
                    pe.wait_ge(xnT_sb, b + 1)
                    for t in range(NT):
                        for c in range(KC):
                            m = pe.matmul(log_bank[:, t, :], xnT[:, c, t * P:(t + 1) * P], rw[:, c, :],
                                          start=(c == 0), stop=(c == KC - 1))
                    m.then_inc(log_ps, 1)
                    pe.wait_ge(oh_done, b + 1)
                    for t in range(NT):
                        dst = banks[1][:, t * KE:(t + 1) * KE]
                        pe.matmul(dst, tri[:, :], ohb[:, t, :], start=True, stop=False)
                        m = pe.matmul(dst, ones[:, :], seen[:, t, :], start=False, stop=True)
                    m.then_inc(rank_ps, 1)


def experts(nc, common, w1, w2, ffn_bias, slot_rows, slot_out):
    hid, ident, ident_b, mask_q, mask_k, sum_rows, wo_pad, eps_t, neg_half, banks, s_bank, t_bank, sb = common
    with ExitStack() as own:
        def buf(name, shape, dt=F32):
            return sb(name, shape, dt, own)

        def sem(name):
            return own.enter_context(nc.semaphore(name))

        NW = KC * FFN
        wr = [buf(f"wr{i}", [P, NW]) for i in range(2)]
        wh = [[buf(f"wh{i}{q}", [P, NW], F32R) for q in range(2)] for i in range(2)]
        wl = [[buf(f"wl{i}{q}", [P, NW], F32R) for q in range(2)] for i in range(2)]
        bias = buf("bias", [P, DIM])
        xr = [buf(f"xr{k}", [P, CT, DIM]) for k in range(TOPK)]
        xh = buf("xh", [P, KC, CAP], F32R)
        xl = buf("xl", [P, KC, CAP], F32R)
        h = buf("h", [P, 2, CAP])
        hh = buf("hh", [P, FC, CAP], F32R)
        hl = buf("hl", [P, FC, CAP], F32R)
        yo = [buf(f"yo{k}", [P, CT, DIM]) for k in range(TOPK)]

        bias_in = sem("bias_in")
        bias_added = sem("bias_added")
        w_in = [sem(f"w_in{i}") for i in range(2)]
        w_split = [sem(f"w_split{i}") for i in range(2)]
        w_used = sem("w_used")
        x_in = [sem(f"e_x_in{k}") for k in range(TOPK)]
        x_ps = sem("x_ps")
        xh_done = sem("xh_done")
        xl_done = sem("xl_done")
        h_ps = sem("h_ps")
        gelu_done = sem("gelu_done")
        hh_done = sem("hh_done")
        hl_done = sem("hl_done")
        y_ps = sem("y_ps")
        y_sb = sem("y_sb")
        y_out = [sem(f"y_out{k}") for k in range(TOPK)]
        passed = sem("e_passed")

        h_banks = [t_bank[:, 0, 0:CAP], t_bank[:, 1, 0:CAP], t_bank[:, 2, 0:CAP], s_bank[:, 2, 0:CAP]]
        NH = len(h_banks)
        y_banks = [banks[0][:, 0:DIM], banks[1][:, 0:DIM], banks[0][:, 0:DIM]]

        def program(turn, eng):
            with eng.Fori(0, E // 2 - 1) as rnd:
                for q in range(2):
                    turn(rnd, q, True, True)
            turn(E // 2 - 1, 0, True, False)
            turn(E // 2 - 1, 1, False, False)

        block = own.enter_context(nc.Block())

        def rows_of(dram, e, k):
            return dram.rearrange("(s t p) d -> s p t d", t=CT, p=P)[k * E + e]

        @block.sync
        def _(sp):
            sp.dma_start(bias[:, :], rows_to_all(ffn_bias, DIM)).then_inc(bias_in, 16)

            def load_weights(e):
                sp.wait_ge(w_split[0], 2 * e + 1)
                sp.dma_start(wr[0][:, :].rearrange("p (c f) -> p c f", c=KC),
                             w1[e].rearrange("(c p) f -> p c f", p=P)).then_inc(w_in[0], 16)
                sp.wait_ge(w_split[1], 2 * e + 1)
                sp.dma_start(wr[1][:, :].rearrange("p (c d) -> p c d", c=FC),
                             w2[e].rearrange("(c p) d -> p c d", p=P)).then_inc(w_in[1], 16)

            def load_rows(e, k):
                sp.dma_start(xr[k][:, :, :], rows_of(slot_rows, e, k)).then_inc(x_in[k], 16)

            load_weights(0)
            for k in range(TOPK):
                load_rows(0, k)

            def turn(rnd, q, more, more2):
                e = 2 * rnd + q
                if more:
                    load_weights(e + 1)
                for k in range(TOPK):
                    if more:
                        sp.wait_ge(x_ps, 2 * e + k + 1)
                        load_rows(e + 1, k)
                    sp.wait_ge(y_sb, CT * (2 * e + k + 1) + 1)
                    sp.dma_start(rows_of(slot_out[0:SLOTS, :], e, k), yo[k][:, :, :]).then_inc(y_out[k], 16)

            program(turn, sp)
            for k in range(TOPK):
                sp.wait_ge(y_out[k], 16 * E + 1)

        @block.gpsimd
        def _(pool):
            for i in range(2):
                pool.sem_inc(w_split[i], 1)

            def split(e, q):
                for i in range(2):
                    pool.wait_ge(w_in[i], 16 * (e + 1))
                    pool.wait_ge(w_used, e + 1)
                    pool.sem_inc(passed, 1)
                    pool.tensor_copy(wh[i][q][:, :], wr[i][:, :]).then_inc(w_split[i], 1)
                    pool.wait_ge(w_split[i], 2 * e + 2)
                    pool.tensor_tensor(wl[i][q][:, :], wr[i][:, :], wh[i][q][:, :].bitcast(F32),
                                       ALU.subtract).then_inc(w_split[i], 1)

            split(0, 0)

            def turn(rnd, q, more, more2):
                if more:
                    split(2 * rnd + q + 1, 1 - q)

            program(turn, pool)

        @block.scalar
        def _(act):
            act.sem_inc(gelu_done, NH)
            act.sem_inc(y_sb, 1)
            for k in range(TOPK):
                act.sem_inc(y_out[k], 1)

            def rows(u):
                act.wait_ge(x_ps, u + 1)
                act.activation(xh[:, :, :], s_bank[:, 0:KC, 0:CAP], ACT.Copy).then_inc(xh_done, 1)

            rows(0)

            def turn(rnd, q, more, more2):
                e = 2 * rnd + q
                for k in range(TOPK):
                    u = 2 * e + k
                    for f in range(FC):
                        act.wait_ge(h_ps, FC * u + f + 1)
                        act.wait_ge(hl_done, FC * u + f + 1)
                        act.activation(h[:, f % 2, :], h_banks[f % NH], ACT.Gelu_apprx_tanh).then_inc(gelu_done, 1)
                    if more or k == 0:
                        rows(u + 1)
                    act.wait_ge(y_out[k], 16 * e + 1)
                    for t in range(CT):
                        act.wait_ge(y_ps, CT * u + t + 1)
                        act.activation(yo[k][:, t, :], y_banks[t], ACT.Copy).then_inc(y_sb, 1)

            program(turn, act)

        @block.vector
        def _(dve):
            dve.sem_inc(hl_done, 2)

            def rows(u):
                dve.wait_ge(xh_done, u + 1)
                dve.tensor_tensor(xl[:, :, :], s_bank[:, 0:KC, 0:CAP], xh[:, :, :].bitcast(F32),
                                  ALU.subtract).then_inc(xl_done, 1)

            rows(0)
            dve.wait_ge(bias_in, 16)
            for b in range(B):
                for t in range(NT):
                    dve.tensor_tensor(hid[:, b, t, :], hid[:, b, t, :], bias[:, :], ALU.add).then_inc(bias_added, 1)

            def turn(rnd, q, more, more2):
                for k in range(TOPK):
                    u = 2 * (2 * rnd + q) + k
                    for f in range(FC):
                        dve.wait_ge(gelu_done, FC * u + f + 1 + NH)
                        dve.tensor_copy(hh[:, f, :], h[:, f % 2, :]).then_inc(hh_done, 1)
                        dve.wait_ge(hh_done, FC * u + f + 1)
                        dve.tensor_tensor(hl[:, f, :], h[:, f % 2, :], hh[:, f, :].bitcast(F32),
                                          ALU.subtract).then_inc(hl_done, 1)
                    if more or k == 0:
                        rows(u + 1)

            program(turn, dve)

        @block.tensor
        def _(pe):
            pe.sem_inc(w_used, 2)

            def transpose_rows(e, k, u):
                pe.wait_ge(x_in[k], 16 * (e + 1))
                for t in range(CT):
                    for c in range(KC):
                        m = pe.transpose(s_bank[:, c, t * P:(t + 1) * P], xr[k][:, t, c * P:(c + 1) * P], ident[:, :])
                m.then_inc(x_ps, 1)

            transpose_rows(0, 0, 0)

            def turn(rnd, q, more, more2):
                e = 2 * rnd + q
                w1h, w1l = (w[0][q][:, :].rearrange("p (c f) -> p c f", c=KC) for w in (wh, wl))
                w2h, w2l = (w[1][q][:, :].rearrange("p (c d) -> p c d", c=FC) for w in (wh, wl))
                for k in range(TOPK):
                    u = 2 * e + k
                    if k == 0:
                        pe.wait_ge(w_split[0], 2 * e + 3)
                    pe.wait_ge(xl_done, u + 1)
                    for f in range(FC):
                        cols = slice(f * P, (f + 1) * P)
                        pe.wait_ge(gelu_done, FC * u + f + 1)
                        steps = [(w, xx, c) for c in range(KC) for w, xx in ((w1h, xh), (w1h, xl), (w1l, xh))]
                        for i, (w, xx, c) in enumerate(steps):
                            m = pe.matmul(h_banks[f % NH], w[:, c, cols], xx[:, c, :], start=(i == 0),
                                          stop=(i == len(steps) - 1))
                        m.then_inc(h_ps, 1)
                    if k == 0:
                        transpose_rows(e, 1, u + 1)
                        pe.wait_ge(w_split[1], 2 * e + 3)
                    elif more:
                        transpose_rows(e + 1, 0, u + 1)
                    for t in range(CT):
                        rows = slice(t * P, (t + 1) * P)
                        pe.wait_ge(y_sb, CT * u + 1 if t < 2 else CT * u + 2)
                        for f in range(FC):
                            if t == 0:
                                pe.wait_ge(hl_done, FC * u + f + 3)
                            for i, (hx, w) in enumerate(((hh, w2h), (hh, w2l), (hl, w2h))):
                                m = pe.matmul(y_banks[t], hx[:, f, rows], w[:, f, :], start=(f == 0 and i == 0),
                                              stop=(f == FC - 1 and i == 2))
                        m.then_inc(y_ps, 1)
                pe.wait_ge(y_ps, CT * (2 * e + 2))
                pe.sem_inc(w_used, 1)

            program(turn, pe)


def combine(nc, common, slot_out, pos, gate, out):
    hid = common[0]
    sb = common[-1]
    with ExitStack() as own:
        def buf(name, shape, dt=F32):
            return sb(name, shape, dt, own)

        def sem(name):
            return own.enter_context(nc.semaphore(name))

        idx = [buf(f"idx{q}", [P, NT, TOPK], I32) for q in range(2)]
        ya = [buf(f"ya{q}", [P, NT, TOPK, DIM]) for q in range(2)]
        res = [buf(f"res{q}", [P, NT, DIM]) for q in range(2)]

        idx_done = sem("idx_done")
        fetched = [sem(f"fetched{q}") for q in range(2)]
        first_done = sem("first_done")
        res_done = sem("res_done")
        stored = [sem(f"stored{q}") for q in range(2)]
        pool_passed = sem("c_pool_passed")

        block = own.enter_context(nc.Block())

        @block.gpsimd
        def _(pool):
            pool.sem_inc(res_done, 2 * NT)
            with pool.Fori(0, B // 2) as rnd:
                for q in range(2):
                    b = 2 * rnd + q
                    pool.wait_ge(idx_done, b + 1)
                    pool.wait_ge(res_done, NT * b + NT)
                    pool.sem_inc(pool_passed, 1)
                    for t in range(NT):
                        for k in range(TOPK):
                            pool.indirect_dma_start(
                                out=ya[q][:, t, k, :], out_offset=None, in_=slot_out,
                                in_offset=bass.IndirectOffsetOnAxis(ap=idx[q][:, t, k:k + 1], axis=0),
                                bounds_check=SLOTS, oob_is_err=False).then_inc(fetched[q], 16)

        @block.vector
        def _(dve):
            for q in range(2):
                dve.sem_inc(stored[q], 1)
                dve.tensor_copy(idx[q][:, :, :], pos[:, NT * q:NT * q + NT, :]).then_inc(idx_done, 1)

            def turn(rnd, q, more):
                b = 2 * rnd + q
                dve.wait_ge(fetched[q], 16 * NT * TOPK * (rnd + 1))
                if more:
                    dve.tensor_copy(idx[q][:, :, :], pos[:, bass.ds(NT * (b + 2), NT), :]).then_inc(idx_done, 1)
                dve.wait_ge(stored[q], 16 * rnd + 1)
                for t in range(NT):
                    g = gate[:, bass.ds(NT * b + t, 1), :].rearrange("p o k -> p (o k)")
                    dve.scalar_tensor_tensor(out=res[q][:, t, :], in0=ya[q][:, t, 0, :], scalar=g[:, 0:1],
                                             in1=hid[:, b, t, :], op0=ALU.mult, op1=ALU.add).then_inc(first_done, 1)
                for t in range(NT):
                    g = gate[:, bass.ds(NT * b + t, 1), :].rearrange("p o k -> p (o k)")
                    dve.wait_ge(first_done, NT * b + t + 1)
                    dve.scalar_tensor_tensor(out=res[q][:, t, :], in0=ya[q][:, t, 1, :], scalar=g[:, 1:2],
                                             in1=res[q][:, t, :], op0=ALU.mult, op1=ALU.add).then_inc(res_done, 1)

            with dve.Fori(0, B // 2 - 1) as rnd:
                for q in range(2):
                    turn(rnd, q, True)
            for q in range(2):
                turn(B // 2 - 1, q, False)

        @block.sync
        def _(sp):
            with sp.Fori(0, B // 2) as rnd:
                for q in range(2):
                    b = 2 * rnd + q
                    sp.wait_ge(res_done, NT * (b + 3))
                    sp.dma_start(out[b].rearrange("(t p) d -> p t d", p=P), res[q][:, :, :]).then_inc(stored[q], 16)
            for q in range(2):
                sp.wait_ge(stored[q], 16 * (B // 2) + 1)


_INS = ["x", "txt", "L0_tok_ccm", "L0_tok_ccm_bias", "L0_tok_shifts", "L0_tok_slopes", "L0_tok_conv_w",
        "L0_tok_conv_b", "L0_attn_W_DKV", "L0_attn_W_UK", "L0_attn_W_UV", "L0_attn_W_UQ", "L0_attn_W_O",
        "L0_ffn_router_w", "L0_ffn_w1", "L0_ffn_w2", "L0_ffn_bias"]


def kernel(**inputs):
    import concourse.bacc as _bacc
    from concourse.bass_utils import run_bass_kernel_spmd as _run

    nc = _bacc.Bacc("TRN2", target_bir_lowering=False, num_devices=1)
    arrays, args = {}, []
    for name in _INS:
        a = np.ascontiguousarray(inputs[name])
        arrays[f"in_{name}"] = a
        args.append(nc.dram_tensor(f"in_{name}", a.shape, mybir.dt.from_np(a.dtype), kind="ExternalInput").ap())
    out = nc.dram_tensor("out", (B, T, DIM), F32, kind="ExternalOutput").ap()
    build(nc, *args, out)
    return _run(nc, [arrays], core_ids=[0]).results[0]["out"]
```

```python
from contextlib import ExitStack

import numpy as np

import concourse.bass as bass
from concourse import mybir

F32 = mybir.dt.float32
F32R = mybir.dt.float32r
BF16 = mybir.dt.bfloat16
I32 = mybir.dt.int32
U32 = mybir.dt.uint32
ALU = mybir.AluOpType
ACT = mybir.ActivationFunctionType
AX_X = mybir.AxisListType.X

P = 128
B = 8
NT = 3
T = NT * P
DIM = 256
KC = DIM // P
LAT = 64
HEADS = 16
HD = DIM // HEADS
HALF = HEADS // 2
CH = 3
PTS = 16
E = 8
TOPK = 2
FFN = 1024
FC = FFN // P
TILES = B * NT
CAP = TILES * P // E
CT = CAP // P
SLOTS = TOPK * E * CAP
EPS = 1e-5
SCALE = 1.0 / np.sqrt(HD)
MASKED = -1.0e30
Q_PARTS = (0, 0, 0, 1, 1, 2)
K_PARTS = (0, 1, 2, 0, 1, 0)
MROW = len(Q_PARTS) * HD
MPARTS = 2
SROWS = MROW + MPARTS
PROWS = 3 * HD + MPARTS
GH = 4
BANK_TILES = ((0, 2), (1,))
NW = KC * FFN
FAR = float(1 << 20)


def rows_to_all(ap, n):
    return bass.AP(tensor=ap.tensor, offset=ap.offset, ap=[[0, P], [1, n]])


def build(nc, x, txt, ccm, ccm_bias, shifts, slopes, conv_w, conv_b, w_dkv, w_uk, w_uv, w_uq, w_o,
          router_w, w1, w2, ffn_bias, out):
    qk_scratch = nc.dram_tensor("qk_scratch", [B, 2, 2, PROWS, HALF, T], BF16, kind="Internal").ap()
    slot_rows = nc.dram_tensor("slot_rows", [SLOTS, DIM], F32, kind="Internal").ap()
    slot_out = nc.dram_tensor("slot_out", [SLOTS + P, DIM], F32, kind="Internal").ap()

    with ExitStack() as ctx:
        def sb(name, shape, dt=F32, where=None):
            return (where or ctx).enter_context(nc.sbuf_tensor(name, shape, dt))

        banks = [ctx.enter_context(nc.psum_tensor(f"bank{i}", [P, 512], F32)) for i in range(2)]
        s_bank = ctx.enter_context(nc.psum_tensor("s_bank", [P, 3, 512], F32))
        t_bank = ctx.enter_context(nc.psum_tensor("t_bank", [P, 3, 512], F32))

        hid = sb("hid", [P, B, NT, DIM])
        ident = sb("ident", [P, P])
        ident_b = sb("ident_b", [P, P], BF16)
        mask_q = sb("mask_q", [P, P], BF16)
        mask_k = sb("mask_k", [P, P], BF16)
        sum_rows = sb("sum_rows", [P, P])
        wo_pad = sb("wo_pad", [P, HEADS // GH, DIM])
        eps_t = sb("eps_t", [P, NT])
        neg_half = sb("neg_half", [P, NT])
        flag_i = sb("flag_i", [1, 1], I32)

        common = (hid, ident, ident_b, mask_q, mask_k, sum_rows, wo_pad, eps_t, neg_half, banks, s_bank, t_bank, sb)
        with ExitStack() as shared:
            v_all = sb("v_all", [P, B, NT, DIM], F32, shared)
            tokens(nc, common, flag_i, x, txt, ccm, ccm_bias, shifts, slopes, conv_w, conv_b,
                   w_dkv, w_uk, w_uv, w_uq, w_o, qk_scratch, v_all, slot_rows, slot_out)
            attention(nc, common, qk_scratch, v_all)
        pos = sb("pos", [P, TILES, TOPK], I32)
        gate = sb("gate", [P, TILES, TOPK])
        with ExitStack() as shared:
            wr = [sb(f"wr{i}", [P, NW], F32, shared) for i in range(2)]
            wh = [[sb(f"wh{i}{q}", [P, NW], F32R, shared) for q in range(2)] for i in range(2)]
            wl = [[sb(f"wl{i}{q}", [P, NW], F32R, shared) for q in range(2)] for i in range(2)]
            w_in = [shared.enter_context(nc.semaphore(f"w_in{i}")) for i in range(2)]
            w_split = [shared.enter_context(nc.semaphore(f"w_split{i}")) for i in range(2)]
            weights = (wr, wh, wl, w_in, w_split)
            routing(nc, common, router_w, slot_rows, pos, gate, weights, w1, w2)
            experts(nc, common, weights, w1, w2, ffn_bias, slot_rows, slot_out)
        combine(nc, common, slot_out, pos, gate, out)


def tokens(nc, common, flag_i, x, txt, ccm, ccm_bias, shifts, slopes, conv_w, conv_b,
           w_dkv, w_uk, w_uv, w_uq, w_o, qk_scratch, v_all, slot_rows, slot_out):
    hid, ident, ident_b, mask_q, mask_k, sum_rows, wo_pad, eps_t, neg_half, banks, s_bank, t_bank, sb = common
    IT = NT - 1
    W = DIM
    with ExitStack() as own:
        def buf(name, shape, dt=F32):
            return sb(name, shape, dt, own)

        def sem(name):
            return own.enter_context(nc.semaphore(name))

        prm = buf("prm", [P, 9 + 3 + 48 + 48 + 3 + 1])
        ccm_t = prm[:, 0:9]
        cbias = prm[:, 9:12]
        shift_t = prm[:, 12:60]
        slope_t = prm[:, 60:108]
        conv_t = prm[:, 108:111]
        convb_t = prm[:, 111:112]
        flag_f = buf("flag_f", [1, 2])
        curve_w = buf("curve_w", [P, CH * PTS])
        dkv = buf("dkv", [P, KC, LAT])
        uk = buf("uk", [P, DIM])
        uv = buf("uv", [P, DIM])
        uq = buf("uq", [P, KC, DIM])
        xin = buf("xin", [P, 2, IT, W * CH])
        g = buf("g", [P, CH, IT, W])
        r = buf("r", [P, CH, IT, W])
        acc = buf("acc", [P, IT, W])
        stats = buf("stats", [P, NT, 6])
        mv = buf("mv", [P, NT, 2])
        ve = buf("ve", [P, NT])
        rstd = buf("rstd", [P, NT])
        xn = buf("xn", [P, NT, DIM])
        xnT = buf("xnT", [P, KC, T])
        ckvT = buf("ckvT", [P, T])
        high = buf("high", [P, 2, 2, T], BF16)
        rest = buf("rest", [P, 2, 2, T])
        mid = buf("mid", [P, 2, 2, T], BF16)
        low = buf("low", [P, 2, 2, T], BF16)
        zeros = buf("zeros", [P, 2048])

        consts_made = sem("consts_made")
        weights_in = sem("weights_in")
        flag_made = sem("flag_made")
        curve_made = sem("curve_made")
        text_in = sem("text_in")
        x_in = sem("x_in")
        x_free = sem("x_free")
        g_base = sem("g_base")
        g_step = sem("g_step")
        pt_step = sem("pt_step")
        g_free = sem("g_free")
        more_step = sem("more_step")
        tok_done = sem("tok_done")
        ln_step = sem("ln_step")
        var_done = sem("var_done")
        ve_done = sem("ve_done")
        rstd_done = sem("rstd_done")
        xn_done = sem("xn_done")
        xnT_ps = sem("xnT_ps")
        xnT_sb = sem("xnT_sb")
        ckv_ps = sem("ckv_ps")
        ckv_sb = sem("ckv_sb")
        qk_ps = sem("qk_ps")
        high_done = sem("high_done")
        rest_done = sem("rest_done")
        mid_done = sem("mid_done")
        low_done = sem("low_done")
        v_ps = sem("v_ps")
        v_sb = sem("v_sb")
        spilled = sem("spilled")
        zero_made = sem("zero_made")
        passed = sem("passed")
        zeroed = sem("zeroed")
        pool_passed = sem("t_pool_passed")
        NSPILL = 12

        xnT_bank = s_bank[:, 0:KC, 0:T]
        ckv_bank = s_bank[0:LAT, 2, 0:T]
        qk_bank = [[t_bank[:, 0, 0:T], t_bank[:, 1, 0:T]], [t_bank[:, 2, 0:T], banks[0][:, 0:T]]]

        block = own.enter_context(nc.Block())

        @block.gpsimd
        def _(pool):
            pool.memset(ident[:, :], 0.0).then_inc(consts_made, 1)
            pool.memset(mask_q[:, :], 0.0).then_inc(consts_made, 1)
            pool.memset(mask_k[:, :], 0.0).then_inc(consts_made, 1)
            pool.memset(sum_rows[:, :], 0.0).then_inc(consts_made, 1)
            pool.memset(wo_pad[:, :, :], 0.0).then_inc(consts_made, 1)
            pool.memset(uk[:, :], 0.0).then_inc(consts_made, 1)
            pool.memset(uv[:, :], 0.0).then_inc(consts_made, 1)
            pool.memset(ckvT[:, :], 0.0).then_inc(consts_made, 1)
            pool.memset(eps_t[:, :], EPS).then_inc(consts_made, 1)
            pool.memset(neg_half[:, :], -0.5).then_inc(consts_made, 1)
            pool.wait_ge(consts_made, 10)
            pool.affine_select(out=ident[:, :], in_=ident[:, :], compare_op=ALU.not_equal, fill=1.0, base=0,
                               pattern=[[-1, P]], channel_multiplier=1).then_inc(consts_made, 1)
            pool.affine_select(out=mask_q[:, :], in_=mask_q[:, :], compare_op=ALU.is_ge, fill=MASKED, base=0,
                               pattern=[[-1, P]], channel_multiplier=1).then_inc(consts_made, 1)
            pool.affine_select(out=mask_k[:, :], in_=mask_k[:, :], compare_op=ALU.is_ge, fill=MASKED, base=0,
                               pattern=[[1, P]], channel_multiplier=-1).then_inc(consts_made, 1)
            strips = sum_rows[:, :].rearrange("p (i c) -> p i c", i=GH)
            pool.affine_select(out=strips, in_=strips, compare_op=ALU.not_equal, fill=1.0, base=-HD,
                               pattern=[[-32, GH], [0, 32]], channel_multiplier=1).then_inc(consts_made, 1)
            pool.wait_ge(consts_made, 14)
            pool.tensor_copy(ident_b[:, :], ident[:, :]).then_inc(consts_made, 1)
            pool.memset(zeros[:, :], 0.0).then_inc(zero_made, 1)

            def rstds(b):
                pool.wait_ge(var_done, NT * b + NT)
                pool.tensor_tensor(ve[:, :], mv[:, :, 1], eps_t[:, :], ALU.add).then_inc(ve_done, 1)
                pool.wait_ge(ve_done, b + 1)
                pool.tensor_tensor(rstd[:, :], ve[:, :], neg_half[:, :], ALU.pow).then_inc(rstd_done, 1)

            def splits(b):
                pool.wait_ge(spilled, 16 * NSPILL * b + 1)
                for k in range(4):
                    half, s = k // 2, k % 2
                    pool.wait_ge(rest_done, 4 * b + k + 2)
                    pool.sem_inc(pool_passed, 1)
                    pool.tensor_copy(mid[:, half, s, :], rest[:, half, s, :]).then_inc(mid_done, 1)
                    pool.wait_ge(mid_done, 4 * b + k + 1)
                    pool.tensor_tensor(low[:, half, s, :], rest[:, half, s, :], mid[:, half, s, :],
                                       ALU.subtract).then_inc(low_done, 1)

            rstds(0)
            with pool.Fori(0, B - 1) as b:
                rstds(b + 1)
                splits(b)
            splits(B - 1)

        @block.sync
        def _(sp):
            sp.sem_inc(spilled, 1)
            sp.wait_ge(consts_made, 10)
            for dst, src in ((ccm_t, rows_to_all(ccm, 9)), (cbias, rows_to_all(ccm_bias, 3)),
                             (shift_t, rows_to_all(shifts, 48)), (slope_t, rows_to_all(slopes, 48)),
                             (conv_t, rows_to_all(conv_w, 3)), (convb_t, rows_to_all(conv_b, 1)),
                             (dkv[:, :, :], w_dkv.rearrange("(c p) n -> p c n", p=P)),
                             (uq[:, :, :], w_uq.rearrange("(c p) n -> p c n", p=P)),
                             (uk[0:LAT, :], w_uk), (uv[0:LAT, :], w_uv)):
                sp.dma_start(dst, src).then_inc(weights_in, 16)
            sp.dma_start(hid[:, :, NT - 1, :], txt.rearrange("b p d -> p b d")).then_inc(text_in, 16)
            for i in range(GH):
                sp.dma_start(wo_pad[32 * i:32 * i + HD, :, :],
                             w_o.rearrange("(g i d) n -> i d g n", i=GH, d=HD)[i]).then_inc(text_in, 16)
            sp.wait_ge(zero_made, 1)
            flat = slot_rows.rearrange("(a p) d -> a p d", p=P * 8)
            for a in range(flat.shape[0]):
                sp.dma_start(flat[a].rearrange("(p r) d -> p (r d)", p=P), zeros[:, :]).then_inc(zeroed, 16)
            sp.dma_start(slot_out[SLOTS:SLOTS + P, :], zeros[:, 0:DIM]).then_inc(zeroed, 16)
            for a in range(MPARTS):
                sp.dma_start(qk_scratch[:, :, 0, 3 * HD + a].rearrange("b s h t -> (b s) (h t)"),
                             zeros[0:2 * B, 0:HALF * T // 2].bitcast(BF16)).then_inc(zeroed, 16)
            with sp.Fori(0, B) as b:
                for k in range(4):
                    half, s = k // 2, k % 2
                    for part, (src, made, start) in enumerate(((high, high_done, 0), (mid, mid_done, 0),
                                                               (low, low_done, 1))):
                        sp.wait_ge(made, start + 4 * b + k + 1)
                        rows = qk_scratch[b, half, s, part * HD:(part + 1) * HD]
                        sp.dma_start(rows.rearrange("d h t -> h d t"), src[:, half, s, :]).then_inc(spilled, 16)
            sp.wait_ge(spilled, 16 * NSPILL * B + 1)
            sp.wait_ge(zeroed, 16 * (flat.shape[0] + 1 + MPARTS))
            sp.wait_ge(text_in, 16 * (1 + GH))

        @block.scalar
        def _(act):
            act.sem_inc(x_free, 2)
            act.sem_inc(v_sb, 1)
            act.wait_ge(x_free, 1)
            act.dma_start(xin[:, 0, :, :], x[0].rearrange("(j p) w c -> p j (w c)", p=P)).then_inc(x_in, 16)
            act.wait_ge(weights_in, 16 * 10)
            def colours(b, more):
                act.wait_ge(x_in, 16 * b + 16)
                act.wait_ge(g_free, b + 1)
                xv = xin[:, b % 2, :, :].rearrange("p j (w c) -> p j w c", c=CH)
                for d in range(CH):
                    act.activation(g[:, d, :, :], xv[:, :, :, 0], ACT.Identity, bias=cbias[:, d:d + 1],
                                   scale=ccm_t[:, d:d + 1]).then_inc(g_base, 1)
                if more:
                    act.wait_ge(x_free, b + 2)
                    act.wait_ge(g_base, CH * b + CH)
                    act.dma_start(xin[:, (b + 1) % 2, :, :],
                                  x[b + 1].rearrange("(j p) w c -> p j (w c)", p=P)).then_inc(x_in, 16)

            def products(b):
                act.wait_ge(xnT_ps, b + 2)
                act.activation(xnT[:, :, :], xnT_bank, ACT.Copy).then_inc(xnT_sb, 1)
                act.wait_ge(ckv_ps, b + 1)
                act.activation(ckvT[0:LAT, :], ckv_bank, ACT.Copy).then_inc(ckv_sb, 1)
                act.wait_ge(spilled, 16 * NSPILL * b + 1)
                for k in range(4):
                    half, s = k // 2, k % 2
                    act.wait_ge(qk_ps, 4 * b + k + 1)
                    act.activation(high[:, half, s, :], qk_bank[half][s], ACT.Copy,
                                   scale=float(SCALE) if s == 0 else 1.0).then_inc(high_done, 1)
                act.wait_ge(v_ps, 2 * b + 1)
                act.activation(v_all[:, b, 0:2, :], banks[1][:, :].rearrange("p (t d) -> p t d", t=2),
                               ACT.Copy).then_inc(v_sb, 1)
                act.wait_ge(v_ps, 2 * b + 2)
                act.activation(v_all[:, b, 2, :], s_bank[:, 2, 0:DIM], ACT.Copy).then_inc(v_sb, 1)

            colours(0, True)
            with act.Fori(0, B - 2) as b:
                colours(b + 1, True)
                products(b)
            colours(B - 1, False)
            products(B - 2)
            products(B - 1)

        @block.vector
        def _(dve):
            dve.wait_ge(weights_in, 16 * 10)
            for c in range(CH):
                dve.tensor_scalar(curve_w[:, c * PTS:(c + 1) * PTS], slope_t[:, c * PTS:(c + 1) * PTS],
                                  conv_t[:, c:c + 1], None, ALU.mult).then_inc(curve_made, 1)
            dve.tensor_reduce(flag_f[:, 0:1], slope_t[0:1, :].rearrange("p (c n) -> p c n", c=CH)[:, :, 1:PTS],
                              mybir.AxisListType.XY, ALU.max, apply_absolute_value=True).then_inc(flag_made, 1)
            dve.wait_ge(flag_made, 1)
            dve.tensor_scalar(flag_i[:, :], flag_f[:, 0:1], 0.0, None, ALU.not_equal).then_inc(flag_made, 1)
            dve.wait_ge(flag_made, 2)
            dve.wait_ge(curve_made, CH)
            more_points = dve.value_load(flag_i[0:1, 0:1], min_val=0, max_val=1)
            dve.wait_ge(text_in, 16 * (1 + GH))
            dve.sem_inc(g_free, 1)
            dve.sem_inc(rest_done, 1)

            def colours(b):
                xv = xin[:, b % 2, :, :].rearrange("p j (w c) -> p j w c", c=CH)
                for c in range(1, CH):
                    for d in range(CH):
                        if c == 1:
                            dve.wait_ge(g_base, CH * b + d + 1)
                        else:
                            dve.wait_ge(g_step, 2 * CH * b + d + 1)
                        dve.scalar_tensor_tensor(out=g[:, d, :, :], in0=xv[:, :, :, c],
                                                 scalar=ccm_t[:, c * CH + d:c * CH + d + 1], in1=g[:, d, :, :],
                                                 op0=ALU.mult, op1=ALU.add).then_inc(g_step, 1)
                dve.wait_ge(g_step, 2 * CH * b + 2 * CH)
                dve.sem_inc(x_free, 1)

            def curve(b):
                for c in range(CH):
                    dve.tensor_scalar(r[:, c, :, :], g[:, c, :, :], shift_t[:, c * PTS:c * PTS + 1], 0.0,
                                      ALU.subtract, ALU.max).then_inc(pt_step, 1)
                for c in range(CH):
                    dve.wait_ge(pt_step, 6 * b + (c + 1 if c == 0 else CH + c))
                    if c == 0:
                        dve.tensor_scalar(acc[:, :, :], r[:, 0, :, :], curve_w[:, 0:1], convb_t[:, 0:1],
                                          ALU.mult, ALU.add).then_inc(pt_step, 1)
                    else:
                        dve.scalar_tensor_tensor(out=acc[:, :, :], in0=r[:, c, :, :],
                                                 scalar=curve_w[:, c * PTS:c * PTS + 1], in1=acc[:, :, :],
                                                 op0=ALU.mult, op1=ALU.add).then_inc(pt_step, 1)
                dve.wait_ge(pt_step, 6 * b + 6)
                dve.sem_inc(passed, 1)
                with dve.If(more_points):
                    with dve.Fori(1, PTS) as i:
                        done = 6 * (PTS - 1) * b + 6 * (i - 1)
                        for c in range(CH):
                            dve.tensor_scalar(r[:, c, :, :], g[:, c, :, :], shift_t[:, bass.ds(c * PTS + i, 1)], 0.0,
                                              ALU.subtract, ALU.max).then_inc(more_step, 1)
                        for c in range(CH):
                            dve.wait_ge(more_step, done + CH + c)
                            dve.scalar_tensor_tensor(out=acc[:, :, :], in0=r[:, c, :, :],
                                                     scalar=curve_w[:, bass.ds(c * PTS + i, 1)], in1=acc[:, :, :],
                                                     op0=ALU.mult, op1=ALU.add).then_inc(more_step, 1)
                        dve.wait_ge(more_step, done + 2 * CH)
                        dve.sem_inc(passed, 1)
                dve.sem_inc(g_free, 1)
                dve.tensor_scalar(hid[:, b, 0:IT, :], acc[:, :, :], 0.0, 1.0, ALU.max, ALU.min).then_inc(tok_done, 1)

            def rests(b):
                dve.wait_ge(low_done, 4 * b + 1)
                for k in range(4):
                    half, s = k // 2, k % 2
                    dve.wait_ge(high_done, 4 * b + k + 1)
                    dve.scalar_tensor_tensor(out=rest[:, half, s, :], in0=qk_bank[half][s],
                                             scalar=float(SCALE) if s == 0 else 1.0,
                                             in1=high[:, half, s, :], op0=ALU.mult,
                                             op1=ALU.subtract).then_inc(rest_done, 1)

            def norms(b):
                dve.wait_ge(tok_done, b + 1)
                dve.sem_inc(passed, 1)
                for t in range(NT):
                    dve.bn_stats(stats[:, t, :], hid[:, b, t, :]).then_inc(ln_step, 1)
                dve.wait_ge(ln_step, NT * b + NT)
                dve.sem_inc(passed, 1)
                for t in range(NT):
                    dve.bn_aggr(mv[:, t, :], stats[:, t, :]).then_inc(var_done, 1)

            def scaled(b):
                dve.wait_ge(rstd_done, b + 1)
                dve.wait_ge(xnT_ps, b + 1)
                for t in range(NT):
                    dve.tensor_scalar(xn[:, t, :], hid[:, b, t, :], mv[:, t, 0:1], rstd[:, t:t + 1],
                                      ALU.subtract, ALU.mult).then_inc(xn_done, 1)

            dve.sem_inc(low_done, 1)
            colours(0)
            curve(0)
            norms(0)
            scaled(0)
            with dve.Fori(0, B - 1) as b:
                colours(b + 1)
                curve(b + 1)
                norms(b + 1)
                rests(b)
                scaled(b + 1)
            rests(B - 1)

        @block.tensor
        def _(pe):
            pe.wait_ge(consts_made, 15)
            pe.sem_inc(xnT_ps, 1)
            pe.wait_ge(weights_in, 16 * 10)
            with pe.Fori(0, B) as b:
                pe.wait_ge(xn_done, NT * b + NT)
                for t in range(NT):
                    for c in range(KC):
                        m = pe.transpose(s_bank[:, c, t * P:(t + 1) * P], xn[:, t, c * P:(c + 1) * P], ident[:, :])
                m.then_inc(xnT_ps, 1)
                pe.wait_ge(xnT_sb, b + 1)
                pe.wait_ge(v_sb, 2 * b + 1)
                for c in range(KC):
                    m = pe.matmul(ckv_bank, dkv[:, c, :], xnT[:, c, :], start=(c == 0), stop=(c == KC - 1))
                m.then_inc(ckv_ps, 1)
                pe.wait_ge(rest_done, 4 * b + 1)
                for half in range(2):
                    cols = slice(half * P, (half + 1) * P)
                    for c in range(KC):
                        m = pe.matmul(qk_bank[half][0], uq[:, c, cols], xnT[:, c, :], start=(c == 0), stop=(c == KC - 1))
                    m.then_inc(qk_ps, 1)
                    if half == 0:
                        pe.wait_ge(ckv_sb, b + 1)
                    pe.matmul(qk_bank[half][1], uk[:, cols], ckvT[:, :], start=True, stop=True).then_inc(qk_ps, 1)
                for t in range(NT):
                    dst = banks[1][:, t * DIM:(t + 1) * DIM] if t < 2 else s_bank[:, 2, 0:DIM]
                    m = pe.matmul(dst, ckvT[:, t * P:(t + 1) * P], uv[:, :], start=True, stop=True)
                    if t:
                        m.then_inc(v_ps, 1)


def attention(nc, common, qk_scratch, v_all):
    hid, ident, ident_b, mask_q, mask_k, sum_rows, wo_pad, eps_t, neg_half, banks, s_bank, t_bank, sb = common
    misc, ctx_bank = banks[0], banks[1]
    misc_b = misc[:, :].bitcast(BF16)
    NG = 2
    with ExitStack() as own:
        def buf(name, shape, dt=F32):
            return sb(name, shape, dt, own)

        def sem(name):
            return own.enter_context(nc.semaphore(name))

        qs = [[buf(f"qs{r}{h}", [SROWS, HALF, T], BF16) for h in range(2)] for r in range(2)]
        ks = [[buf(f"ks{r}{h}", [SROWS, HALF, T], BF16) for h in range(2)] for r in range(2)]
        vb = [buf(f"vb{h}", [P, NT, HALF, 32]) for h in range(2)]
        mx = buf("mx", [P, NG, NT, GH])
        ms = buf("ms", [P, NG, NT, MPARTS, GH], BF16)
        mT = buf("mT", [MPARTS * GH, NG, T], BF16)
        pt = buf("pt", [P, 4, 2, 2 * T])
        cx = buf("cx", [P, NG, T])
        rs = buf("rs", [P, NG, NT, GH])
        wide = buf("wide", [P, NG, NT, GH, 32])
        cn = buf("cn", [P, HEADS // GH, T])

        ready = sem("ready")
        ready0 = sem("ready0")
        stack_in = [sem(f"stack_in{h}") for h in range(2)]
        v_ready = sem("v_ready")
        s_ready = sem("s_ready")
        s_read = sem("s_read")
        m_part = sem("m_part")
        mT_ps = sem("mT_ps")
        mT_sb = sem("mT_sb")
        m_in = [sem(f"m_in{g}") for g in range(NG)]
        t_ready = sem("t_ready")
        exp_done = sem("exp_done")
        pv_done = sem("pv_done")
        ctx_sb = sem("ctx_sb")
        sums_ps = sem("sums_ps")
        rs_done = sem("rs_done")
        spread_ps = sem("spread_ps")
        wide_done = sem("wide_done")
        pool_passed = sem("a_pool_passed")
        cn_done = sem("cn_done")
        wo_ps = sem("wo_ps")
        hid_add = sem("hid_add")
        misc_free = sem("misc_free")
        Q_RUNS = ((0, 0, 1, 3), (3, 1, 1, 2), (5, 2, 1, 1))
        K_RUNS = ((0, 0, 3, 1), (3, 0, 2, 1), (5, 0, 1, 1))
        NL = len(Q_RUNS) + len(K_RUNS)

        block = own.enter_context(nc.Block())

        def program(turn, eng):
            turn(-1, 1, 1, True, False, False, False)
            for half in range(2):
                turn(0, 0, half, True, True, half == 1, False)
            with eng.Fori(0, (B - 2) // 2) as pair:
                for r in range(2):
                    for half in range(2):
                        turn(2 * pair + 1 + r, 1 - r, half, True, True, True, half == 1)
            for half in range(2):
                turn(B - 1, (B - 1) % 2, half, half == 0, True, True, half == 1)
            turn(B, B % 2, 0, False, False, True, False)
            turn(B, B % 2, 1, False, False, False, True)

        def misc_uses(rnd, half):
            if isinstance(rnd, int) and rnd < 1:
                return 0 if rnd < 0 else 1 + 3 * half
            if isinstance(rnd, int) and rnd == B:
                return 14 * B - 5 + 3 * half
            return 14 * rnd - 4 + 6 * half

        @block.sync
        def _(sp):
            def load(rnd, par, half):
                for s, dst, runs in ((0, qs[par][half], Q_RUNS), (1, ks[par][half], K_RUNS)):
                    scratch = qk_scratch[rnd, half, s]
                    for i, (at, part, parts, times) in enumerate(runs):
                        rows = parts * HD + (MPARTS if s == 0 and i == len(runs) - 1 else 0)
                        src = scratch[part * HD:part * HD + rows].rearrange("r h t -> r (h t)")
                        if times > 1:
                            src = bass.AP(tensor=src.tensor, offset=src.offset,
                                          ap=[[0, times]] + [list(d) for d in src.ap])
                        to = dst[at * HD:at * HD + times * rows].rearrange("r h t -> r (h t)")
                        sp.dma_start(to, src).then_inc(stack_in[half], 16)

            def max_rows(par, half, grp, n):
                G = NG * n + grp
                sp.wait_ge(mT_sb, G + 1)
                for a in range(MPARTS):
                    sp.dma_start(qs[par][half][MROW + a:MROW + a + 1, grp * GH:(grp + 1) * GH, :],
                                 mT[a * GH:(a + 1) * GH, grp, :]).then_inc(m_in[grp], 16)

            for rnd in range(2):
                for half in range(2):
                    if rnd:
                        sp.wait_ge(stack_in[half], 16 * NL)
                    load(rnd, rnd, half)

            def turn(rnd, par, half, nxt, cur, prev, proj):
                n = 2 * rnd + half
                if cur:
                    max_rows(par, half, 1, n)
                if cur and (not isinstance(rnd, int) or 0 < rnd < B - 1):
                    sp.wait_ge(t_ready, 8 * (n - 1))
                    sp.wait_ge(stack_in[half], 16 * NL * (rnd + 1))
                    load(rnd + 1, 1 - par, half)
                if nxt:
                    max_rows(par if half == 0 else 1 - par, 1 - half, 0, n + 1)

            program(turn, sp)

        @block.gpsimd
        def _(pool):
            for h in range(2):
                pool.memset(vb[h][:, :, :, HD:2 * HD], 1.0).then_inc(ready, 1)
            pool.wait_ge(ready, 2)
            for h in range(2):
                pool.memset(ks[1][h][MROW:SROWS, :, :], -1.0).then_inc(ready, 1)
            pool.wait_ge(ready, 4)

            def widen(n, grp):
                pool.wait_ge(rs_done, NG * n + grp + 1)
                pool.sem_inc(pool_passed, 1)
                src = rs[:, grp, :, :].rearrange("p j (h o) -> p j h o", o=1).to_broadcast([P, NT, GH, 32])
                pool.tensor_copy(wide[:, grp, :, :, :], src).then_inc(wide_done, 1)

            def values_of(rnd, half, n):
                if not isinstance(n, int) or n > 1:
                    pool.wait_ge(pv_done, 2 * n)
                    pool.sem_inc(pool_passed, 1)
                src = v_all[:, rnd, :, half * DIM // 2:(half + 1) * DIM // 2]
                pool.tensor_copy(vb[half][:, :, :, 0:HD],
                                 src.rearrange("p t (h d) -> p t h d", d=HD)).then_inc(v_ready, 1)

            def turn(rnd, par, half, nxt, cur, prev, proj):
                n = 2 * rnd + half
                if prev:
                    widen(n - 1, 0)
                if nxt:
                    values_of(rnd + half, 1 - half, n + 1)
                if prev:
                    widen(n - 1, 1)

            program(turn, pool)

        @block.tensor
        def _(pe):
            pe.sem_inc(pv_done, 2)
            pe.wait_ge(ready, 4)
            pe.wait_ge(ready0, 2)

            def misc_wait(use):
                pe.wait_ge(misc_free, use)

            def score_pair(n, par, half, rnd, p):
                m = 4 * n + p
                if p == 0:
                    pe.wait_ge(stack_in[half], 16 * NL * (rnd + 1))
                for g, tiles in enumerate(BANK_TILES):
                    pe.wait_ge(s_read, 2 * m + g + 1)
                    for i in range(2):
                        h = 2 * p + i
                        for j in tiles:
                            dst, w = s_region(s_bank, j, i)
                            pe.matmul(dst, qs[par][half][:, h, j * P:(j + 1) * P], ks[par][half][:, h, 0:w],
                                      start=True, stop=False)
                            mm = pe.matmul(dst[:, j * P:(j + 1) * P], ident_b[:, :], mask_q[:, :], start=False, stop=True)
                    mm.then_inc(s_ready, 1)

            def exp_pair(n, par, half, p):
                m = 4 * n + p
                if p % 2 == 0:
                    pe.wait_ge(m_in[p // 2], 16 * MPARTS * (n + 1))
                for g, tiles in enumerate(BANK_TILES):
                    pe.wait_ge(exp_done, 2 * m + g + 1)
                    for i in range(2):
                        h = 2 * p + i
                        for j in tiles:
                            dst, w = s_region(t_bank, 2 - j, i)
                            pe.matmul(dst, ks[par][half][:, h, j * P:(j + 1) * P], qs[par][half][:, h, j * P:T],
                                      start=True, stop=False)
                            mm = pe.matmul(dst[:, 0:P], ident_b[:, :], mask_k[:, :], start=False, stop=True)
                    mm.then_inc(t_ready, 1)

            def values(n, half, grp):
                G = NG * n + grp
                pe.wait_ge(exp_done, 2 + 2 * (4 * n + 2 * grp + 2))
                pe.wait_ge(v_ready, n + 1)
                pe.wait_ge(ctx_sb, G)
                for j in range(NT):
                    for i in range(GH):
                        src = pt[:, 2 * grp + i // 2, i % 2, :]
                        at = (0, T, T + 2 * P)[j]
                        mm = pe.matmul(ctx_bank[32 * i:32 * i + 32, j * P:T], vb[half][:, j, grp * GH + i, :],
                                       src[:, at:at + T - j * P], start=(j == 0), stop=(j == NT - 1))
                mm.then_inc(pv_done, 1)

            def turn_sums(n, grp, use):
                pe.wait_ge(ctx_sb, NG * n + grp + 1)
                misc_wait(use)
                for j in range(NT):
                    mm = pe.transpose(misc[:, j * P:(j + 1) * P], cx[:, grp, j * P:(j + 1) * P], ident[:, :])
                mm.then_inc(sums_ps, 1)

            def spread(n, grp, use):
                pe.wait_ge(wide_done, NG * n + grp + 1)
                misc_wait(use)
                for j in range(NT):
                    mm = pe.transpose(misc[:, j * P:(j + 1) * P], wide[:, grp, j, :, :].rearrange("p h c -> p (h c)"),
                                      ident[:, :])
                mm.then_inc(spread_ps, 1)

            def turn_maxima(n, grp, use):
                pe.wait_ge(m_part, MPARTS * (NG * n + grp + 1))
                misc_wait(use)
                for j in range(NT):
                    mm = pe.transpose(misc_b[0:MPARTS * GH, j * P:(j + 1) * P],
                                      ms[:, grp, j, :, :].rearrange("p a h -> p (a h)"), ident_b[:, :])
                mm.then_inc(mT_ps, 1)

            def project(rnd, tiles, use):
                pe.wait_ge(cn_done, 4 * (rnd + 1))
                misc_wait(use)
                for at, t in enumerate(tiles):
                    for g in range(HEADS // GH):
                        mm = pe.matmul(misc[:, at * DIM:(at + 1) * DIM], cn[:, g, t * P:(t + 1) * P],
                                       wo_pad[:, g, :], start=(g == 0), stop=(g == HEADS // GH - 1))
                mm.then_inc(wo_ps, 1)

            def turn(rnd, par, half, nxt, cur, prev, proj):
                n = 2 * rnd + half
                use = misc_uses(rnd, half)

                def scores(p):
                    if nxt:
                        score_pair(n + 1, par if half == 0 else 1 - par, 1 - half, rnd + half, p)

                def exps(p):
                    if cur:
                        exp_pair(n, par, half, p)

                scores(0)
                if cur:
                    turn_maxima(n, 1, use)
                    use = use + 1
                exps(0)
                if proj:
                    project(rnd - 1, (0, 1), use)
                    use = use + 1
                if prev:
                    values(n - 1, 1 - half, 1)
                if proj:
                    project(rnd - 1, (2,), use)
                    use = use + 1
                if prev:
                    spread(n - 1, 0, use)
                    use = use + 1
                scores(1)
                exps(1)
                if prev:
                    turn_sums(n - 1, 1, use)
                    use = use + 1
                scores(2)
                if nxt:
                    turn_maxima(n + 1, 0, use)
                    use = use + 1
                exps(2)
                if cur:
                    values(n, half, 0)
                if prev:
                    spread(n - 1, 1, use)
                    use = use + 1
                scores(3)
                exps(3)
                if cur:
                    turn_sums(n, 0, use)
                    use = use + 1

            program(turn, pe)

        @block.scalar
        def _(act):
            act.sem_inc(exp_done, 2)

            def exps(n, p):
                m = 4 * n + p
                act.wait_ge(pv_done, NG * n + p // 2 + 1)
                for g, tiles in enumerate(BANK_TILES):
                    act.wait_ge(t_ready, 2 * m + g + 1)
                    for j in tiles:
                        at = (0, T, T + 2 * P)[j]
                        ins = act.activation(pt[:, p, :, at:at + T - j * P], pair_region(t_bank, 2 - j), ACT.Exp)
                    ins.then_inc(exp_done, 1)

            def maxima_rows(n, grp):
                G = NG * n + grp
                act.wait_ge(mT_ps, G + 1)
                if not isinstance(n, int) or n > 0:
                    act.wait_ge(m_in[grp], 16 * MPARTS * n)
                act.activation(mT[:, grp, :], misc_b[0:MPARTS * GH, 0:T], ACT.Copy).then_inc(mT_sb, 1)
                act.wait_ge(mT_sb, G + 1)
                act.sem_inc(misc_free, 1)

            def contexts(n, grp):
                G = NG * n + grp
                act.wait_ge(pv_done, G + 3)
                act.wait_ge(cn_done, G - 1 if not isinstance(G, int) else max(G - 1, 0))
                act.activation(cx[:, grp, :], ctx_bank[:, 0:T], ACT.Copy).then_inc(ctx_sb, 1)

            def turn(rnd, par, half, nxt, cur, prev, proj):
                n = 2 * rnd + half
                for p in range(4):
                    if cur and p == 0:
                        maxima_rows(n, 1)
                    if nxt and p == 2:
                        maxima_rows(n + 1, 0)
                    if cur:
                        exps(n, p)
                    if prev and p == 0:
                        contexts(n - 1, 1)
                    if cur and p == 2:
                        contexts(n, 0)

            program(turn, act)

        @block.vector
        def _(dve):
            dve.sem_inc(s_read, 2)
            for h in range(2):
                dve.memset(ks[0][h][MROW:SROWS, :, :], -1.0).then_inc(ready0, 1)

            def maxima(n, p):
                m = 4 * n + p
                for g, tiles in enumerate(BANK_TILES):
                    dve.wait_ge(s_ready, 2 * m + g + 1)
                    for j in tiles:
                        ins = dve.tensor_reduce(mx[:, p // 2, j, 2 * (p % 2):2 * (p % 2) + 2], pair_region(s_bank, j),
                                                AX_X, ALU.max)
                    ins.then_inc(s_read, 1)

            def split(n, grp):
                G = NG * n + grp
                dve.wait_ge(s_read, 2 + 2 * (4 * n + 2 * grp + 2))
                dve.wait_ge(mT_ps, G - 1 if not isinstance(G, int) else max(G - 1, 0))
                dve.tensor_copy(ms[:, grp, :, 0, :], mx[:, grp, :, :]).then_inc(m_part, 1)
                dve.wait_ge(m_part, MPARTS * G + 1)
                dve.tensor_tensor(ms[:, grp, :, 1, :], mx[:, grp, :, :], ms[:, grp, :, 0, :],
                                  ALU.subtract).then_inc(m_part, 1)

            def reciprocals(n, grp):
                G = NG * n + grp
                dve.wait_ge(sums_ps, G + 1)
                sums = misc[:, 0:T].rearrange("p (j h c) -> p j h c", j=NT, h=GH)[:, :, :, HD]
                dve.reciprocal(rs[:, grp, :, :], sums).then_inc(rs_done, 1)
                dve.wait_ge(rs_done, G + 1)
                dve.sem_inc(misc_free, 1)

            def normalise(rnd, half, grp):
                G = NG * (2 * rnd + half) + grp
                dve.wait_ge(spread_ps, G + 1)
                dve.wait_ge(wo_ps, 2 * rnd)
                dve.tensor_tensor(cn[:, NG * half + grp, :], misc[:, 0:T], cx[:, grp, :],
                                  ALU.mult).then_inc(cn_done, 1)
                dve.wait_ge(cn_done, G + 1)
                dve.sem_inc(misc_free, 1)

            def residual(rnd, k):
                dve.wait_ge(wo_ps, 2 * rnd + k + 1)
                tiles = slice(0, 2) if k == 0 else slice(2, 3)
                src = misc[:, 0:(2 - k) * DIM].rearrange("p (t d) -> p t d", d=DIM)
                dve.tensor_tensor(hid[:, rnd, tiles, :], hid[:, rnd, tiles, :], src, ALU.add).then_inc(hid_add, 1)
                dve.wait_ge(hid_add, 2 * rnd + k + 1)
                dve.sem_inc(misc_free, 1)

            def turn(rnd, par, half, nxt, cur, prev, proj):
                n = 2 * rnd + half
                for p in range(4):
                    if nxt:
                        maxima(n + 1, p)
                    if proj and p == 0:
                        residual(rnd - 1, 0)
                        residual(rnd - 1, 1)
                    if prev and p in (0, 2):
                        normalise(rnd if half else rnd - 1, 1 - half, p // 2)
                    if nxt and p in (1, 3):
                        split(n + 1, p // 2)
                    if prev and p == 1:
                        reciprocals(n - 1, 1)
                    if cur and p == 3:
                        reciprocals(n, 0)

            program(turn, dve)


def s_region(bank, j, i):
    w = (j + 1) * P
    if j == 2:
        return bank[:, i, 0:w], w
    if j == 1:
        return bank[:, 2, i * w:(i + 1) * w], w
    return bank[:, i, T:T + P], w


def pair_region(bank, j):
    w = (j + 1) * P
    if j == 2:
        return bank[:, 0:2, 0:w]
    if j == 1:
        return bank[:, 2, :].rearrange("p (i c) -> p i c", i=2)
    return bank[:, 0:2, T:T + P]


def weight_layouts(w1, w2, e):
    return w1[e].rearrange("(c p) f -> p c f", p=P), w2[e].rearrange("(c p) d -> p c d", p=P)


def routing(nc, common, router_w, slot_rows, pos, gate, weights, w1, w2):
    wr, wh, wl, w_in, w_split = weights
    hid, ident, ident_b, mask_q, mask_k, sum_rows, wo_pad, eps_t, neg_half, banks, s_bank, t_bank, sb = common
    KE = TOPK * E
    with ExitStack() as own:
        def buf(name, shape, dt=F32):
            return sb(name, shape, dt, own)

        def sem(name):
            return own.enter_context(nc.semaphore(name))

        rw = buf("rw", [P, KC, E])
        tri = buf("tri", [P, P], BF16)
        ones = buf("ones", [P, P], BF16)
        iota_i = buf("iota_i", [P, TOPK, E], I32)
        base_i = buf("base_i", [P, TOPK, E], I32)
        iota_e = buf("iota_e", [P, TOPK, E])
        base = buf("base", [P, TOPK, E])
        stats = buf("r_stats", [P, NT, 6])
        mv = buf("r_mv", [P, NT, 2])
        ve = buf("r_ve", [P, NT])
        rstd = buf("r_rstd", [P, NT])
        xn = [buf(f"r_xn{q}", [P, NT, DIM]) for q in range(2)]
        xnT = buf("r_xnT", [P, KC, T])
        logits = buf("logits", [P, NT, E])
        top = buf("top", [P, NT, 8])
        top_i = buf("top_i", [P, NT, 8], U32)
        top_f = buf("top_f", [P, NT, TOPK])
        shifted = buf("shifted", [P, NT, E])
        expd = buf("expd", [P, NT, E])
        ssum = buf("ssum", [P, NT])
        rsum = buf("rsum", [P, NT])
        etop = buf("etop", [P, NT, TOPK])
        oh = buf("oh", [P, NT, TOPK, E])
        ohb = buf("ohb", [P, NT, KE], BF16)
        seen = buf("seen", [P, NT + 1, KE], BF16)
        pick = buf("pick", [P, NT, TOPK, E])
        rank = buf("rank", [P, NT, TOPK])
        first = buf("first", [P, NT, TOPK])
        full = buf("full", [P, NT, TOPK])
        slot_f = buf("slot_f", [P, NT, TOPK])
        slot_i = [buf(f"slot_i{q}", [P, NT, TOPK], I32) for q in range(2)]

        made = sem("r_made")
        rw_in = sem("rw_in")
        step = sem("r_step")
        passed = sem("r_passed")
        ln_step = sem("r_ln_step")
        var_done = sem("r_var")
        ve_done = sem("r_ve_done")
        rstd_done = sem("r_rstd_done")
        xn_done = sem("r_xn_done")
        xnT_ps = sem("r_xnT_ps")
        xnT_sb = sem("r_xnT_sb")
        log_ps = sem("log_ps")
        shift_done = sem("shift_done")
        exp_done = sem("r_exp_done")
        oh_done = sem("oh_done")
        rank_ps = sem("rank_ps")
        slot_done = sem("slot_done")
        sent = [sem(f"sent{q}") for q in range(2)]
        rows_free = sem("rows_free")
        pool_passed = sem("pool_passed")

        rank_bank = banks[1][:, 0:NT * KE].rearrange("p (t k e) -> p t k e", t=NT, k=TOPK)
        log_bank = banks[0][:, 0:NT * E].rearrange("p (t e) -> p t e", t=NT)
        block = own.enter_context(nc.Block())

        @block.sync
        def _(sp):
            sp.dma_start(rw[:, :, :], router_w.rearrange("(c p) e -> p c e", p=P)).then_inc(rw_in, 16)
            for i, w in enumerate(weight_layouts(w1, w2, 0)):
                sp.dma_start(wr[i][:, :].rearrange("p (c f) -> p c f", f=w.shape[2]), w).then_inc(w_in[i], 16)
            for i in range(2):
                sp.wait_ge(w_in[i], 16)

        @block.gpsimd
        def _(pool):
            pool.memset(tri[:, :], 1.0).then_inc(made, 1)
            pool.memset(ones[:, :], 1.0).then_inc(made, 1)
            pool.memset(seen[:, :, :], 0.0).then_inc(made, 1)
            pool.iota(iota_i[:, :, :], pattern=[[0, TOPK], [1, E]], base=0, channel_multiplier=0).then_inc(made, 1)
            pool.iota(base_i[:, :, :], pattern=[[E * CAP, TOPK], [CAP, E]], base=0,
                      channel_multiplier=0).then_inc(made, 1)
            pool.wait_ge(made, 5)
            pool.affine_select(out=tri[:, :], in_=tri[:, :], compare_op=ALU.is_gt, fill=0.0, base=0,
                               pattern=[[1, P]], channel_multiplier=-1).then_inc(made, 1)
            pool.tensor_copy(iota_e[:, :, :], iota_i[:, :, :]).then_inc(made, 1)
            pool.tensor_copy(base[:, :, :], base_i[:, :, :]).then_inc(made, 1)
            pool.sem_inc(rows_free, 2)

            def rstds(b):
                pool.wait_ge(var_done, NT * b + NT)
                pool.tensor_tensor(ve[:, :], mv[:, :, 1], eps_t[:, :], ALU.add).then_inc(ve_done, 1)
                pool.wait_ge(ve_done, b + 1)
                pool.tensor_tensor(rstd[:, :], ve[:, :], neg_half[:, :], ALU.pow).then_inc(rstd_done, 1)

            def turn(rnd, q, start, more):
                b = 2 * rnd + q
                if more:
                    rstds(b + 1)
                if not start:
                    pool.wait_ge(sent[1 - q], 16 * NT * TOPK * (rnd + q))
                    pool.sem_inc(rows_free, 1)
                pool.wait_ge(slot_done, b + 1)
                pool.sem_inc(pool_passed, 1)
                for t in range(NT):
                    for k in range(TOPK):
                        pool.indirect_dma_start(
                            out=slot_rows, out_offset=bass.IndirectOffsetOnAxis(ap=slot_i[q][:, t, k:k + 1], axis=0),
                            in_=xn[q][:, t, :], in_offset=None, bounds_check=SLOTS - 1,
                            oob_is_err=False).then_inc(sent[q], 16)

            rstds(0)
            for q in range(2):
                turn(0, q, q == 0, True)
                pool.wait_ge(w_split[q], 1)
                pool.tensor_tensor(wl[q][0][:, :], wr[q][:, :], wh[q][0][:, :].bitcast(F32),
                                   ALU.subtract).then_inc(w_split[q], 1)
            with pool.Fori(1, B // 2 - 1) as rnd:
                for q in range(2):
                    turn(rnd, q, False, True)
            for q in range(2):
                turn(B // 2 - 1, q, False, q == 0)
            for q in range(2):
                pool.wait_ge(sent[q], 16 * (B // 2) * NT * TOPK)

        @block.scalar
        def _(act):
            def transposed(b):
                act.wait_ge(xnT_ps, b + 1)
                act.activation(xnT[:, :, :], s_bank[:, 0:KC, 0:T], ACT.Copy).then_inc(xnT_sb, 1)

            def exps(b):
                act.wait_ge(shift_done, b + 1)
                act.activation(expd[:, :, :], shifted[:, :, :], ACT.Exp).then_inc(exp_done, 1)

            transposed(0)
            for b in range(2):
                exps(b)
                transposed(b + 1)
                act.wait_ge(w_in[b], 16)
                act.activation(wh[b][0][:, :], wr[b][:, :], ACT.Copy).then_inc(w_split[b], 1)
            with act.Fori(2, B - 1) as b:
                exps(b)
                transposed(b + 1)
            exps(B - 1)

        @block.vector
        def _(dve):
            dve.wait_ge(made, 8)
            per = 27

            def norms(b):
                for t in range(NT):
                    dve.bn_stats(stats[:, t, :], hid[:, b, t, :]).then_inc(ln_step, 1)
                dve.wait_ge(ln_step, NT * b + NT)
                dve.sem_inc(passed, 1)
                for t in range(NT):
                    dve.bn_aggr(mv[:, t, :], stats[:, t, :]).then_inc(var_done, 1)

            def scaled(b, q):
                dve.wait_ge(rstd_done, b + 1)
                dve.wait_ge(rows_free, b + 1)
                for t in range(NT):
                    dve.tensor_scalar(xn[q][:, t, :], hid[:, b, t, :], mv[:, t, 0:1], rstd[:, t:t + 1],
                                      ALU.subtract, ALU.mult).then_inc(xn_done, 1)

            def turn(rnd, q, more):
                b = 2 * rnd + q
                k = [0]

                def then(ins, last=True):
                    k[0] += 1
                    ins.then_inc(step, 1)
                    if last:
                        dve.wait_ge(step, per * b + k[0])

                dve.wait_ge(log_ps, b + 1)
                then(dve.tensor_copy(logits[:, :, :], log_bank))
                if more:
                    norms(b + 1)
                dve.sem_inc(passed, 1)
                for t in range(NT):
                    then(dve.max(top[:, t, :], logits[:, t, :]), t == NT - 1)
                dve.tensor_tensor(shifted[:, :, :], logits[:, :, :], top[:, :, 0:1].to_broadcast([P, NT, E]),
                                  ALU.subtract).then_inc(shift_done, 1)
                for t in range(NT):
                    then(dve.max_index(top_i[:, t, :], top[:, t, :], logits[:, t, :]), t == NT - 1)
                then(dve.tensor_copy(top_f[:, :, :], top_i[:, :, 0:TOPK]))
                for c in range(TOPK):
                    then(dve.tensor_tensor(oh[:, :, c, :], iota_e[:, 0:1, :].to_broadcast([P, NT, E]),
                                           top_f[:, :, c:c + 1].to_broadcast([P, NT, E]), ALU.is_equal), c == 1)
                then(dve.tensor_copy(ohb[:, :, :], oh[:, :, :, :].rearrange("p t k e -> p t (k e)")))
                for t in range(NT):
                    ins = dve.tensor_tensor(seen[:, t + 1, :], seen[:, t, :], ohb[:, t, :], ALU.add)
                    if t < NT - 1:
                        then(ins)
                    else:
                        ins.then_inc(oh_done, 1)
                dve.wait_ge(exp_done, b + 1)
                then(dve.tensor_reduce(ssum[:, :], expd[:, :, :], AX_X, ALU.add))
                then(dve.reciprocal(rsum[:, :], ssum[:, :]), False)
                for c in range(TOPK):
                    then(dve.tensor_tensor(pick[:, :, c, :], oh[:, :, c, :], expd[:, :, :], ALU.mult), c == 1)
                then(dve.tensor_reduce(etop[:, :, :], pick[:, :, :, :], AX_X, ALU.add))
                then(dve.tensor_tensor(gate[:, bass.ds(NT * b, NT), :], etop[:, :, :],
                                       rsum[:, :].rearrange("p (t o) -> p t o", o=1).to_broadcast([P, NT, TOPK]),
                                       ALU.mult))
                if more:
                    scaled(b + 1, 1 - q)
                for t in range(NT):
                    ins = dve.tensor_tensor(pick[:, t, :, :], base[:, :, :], oh[:, t, :, :], ALU.mult)
                    if t < NT - 1:
                        ins.then_inc(passed, 1)
                    else:
                        then(ins)
                then(dve.tensor_reduce(first[:, :, :], pick[:, :, :, :], AX_X, ALU.add))
                dve.wait_ge(rank_ps, b + 1)
                dve.tensor_copy(seen[:, 0, :], seen[:, NT, :]).then_inc(passed, 1)
                then(dve.tensor_tensor(pick[:, :, :, :], rank_bank, oh[:, :, :, :], ALU.mult))
                then(dve.tensor_reduce(rank[:, :, :], pick[:, :, :, :], AX_X, ALU.add))
                then(dve.tensor_scalar(full[:, :, :], rank[:, :, :], float(CAP), FAR, ALU.is_ge, ALU.mult), False)
                then(dve.tensor_tensor(slot_f[:, :, :], rank[:, :, :], first[:, :, :], ALU.add))
                then(dve.tensor_tensor(slot_f[:, :, :], slot_f[:, :, :], full[:, :, :], ALU.add))
                dve.tensor_copy(slot_i[q][:, :, :], slot_f[:, :, :]).then_inc(slot_done, 1)
                then(dve.tensor_scalar(pos[:, bass.ds(NT * b, NT), :], slot_f[:, :, :], float(SLOTS), None, ALU.min))
                assert k[0] == per, k[0]

            norms(0)
            scaled(0, 0)
            with dve.Fori(0, B // 2 - 1) as rnd:
                for q in range(2):
                    turn(rnd, q, True)
            for q in range(2):
                turn(B // 2 - 1, q, q == 0)

        @block.tensor
        def _(pe):
            pe.wait_ge(rw_in, 16)
            pe.wait_ge(made, 8)

            def router(b, q):
                pe.wait_ge(xn_done, NT * b + NT)
                for t in range(NT):
                    for c in range(KC):
                        m = pe.transpose(s_bank[:, c, t * P:(t + 1) * P], xn[q][:, t, c * P:(c + 1) * P], ident[:, :])
                m.then_inc(xnT_ps, 1)
                pe.wait_ge(xnT_sb, b + 1)
                for t in range(NT):
                    for c in range(KC):
                        m = pe.matmul(log_bank[:, t, :], xnT[:, c, t * P:(t + 1) * P], rw[:, c, :],
                                      start=(c == 0), stop=(c == KC - 1))
                m.then_inc(log_ps, 1)

            def ranks(b):
                pe.wait_ge(oh_done, b + 1)
                for t in range(NT):
                    dst = banks[1][:, t * KE:(t + 1) * KE]
                    pe.matmul(dst, tri[:, :], ohb[:, t, :], start=True, stop=False)
                    m = pe.matmul(dst, ones[:, :], seen[:, t, :], start=False, stop=True)
                m.then_inc(rank_ps, 1)

            router(0, 0)
            with pe.Fori(0, B // 2 - 1) as rnd:
                for q in range(2):
                    ranks(2 * rnd + q)
                    router(2 * rnd + q + 1, 1 - q)
            ranks(B - 2)
            router(B - 1, 1)
            ranks(B - 1)


def experts(nc, common, weights, w1, w2, ffn_bias, slot_rows, slot_out):
    wr, wh, wl, w_in, w_split = weights
    hid, ident, ident_b, mask_q, mask_k, sum_rows, wo_pad, eps_t, neg_half, banks, s_bank, t_bank, sb = common
    with ExitStack() as own:
        def buf(name, shape, dt=F32):
            return sb(name, shape, dt, own)

        def sem(name):
            return own.enter_context(nc.semaphore(name))

        bias = buf("bias", [P, DIM])
        xr = [buf(f"xr{k}", [P, CT, DIM]) for k in range(TOPK)]
        xh = buf("xh", [P, KC, CAP], F32R)
        xl = buf("xl", [P, KC, CAP], F32R)
        h = buf("h", [P, 2, CAP])
        hh = buf("hh", [P, FC, CAP], F32R)
        hl = buf("hl", [P, FC, CAP], F32R)
        yo = [buf(f"yo{k}", [P, CT, DIM]) for k in range(TOPK)]

        bias_in = sem("bias_in")
        bias_added = sem("bias_added")
        w_used = sem("w_used")
        x_in = [sem(f"e_x_in{k}") for k in range(TOPK)]
        x_ps = sem("x_ps")
        xh_done = sem("xh_done")
        xl_done = sem("xl_done")
        h_ps = sem("h_ps")
        gelu_done = sem("gelu_done")
        hh_done = sem("hh_done")
        hl_done = sem("hl_done")
        y_ps = sem("y_ps")
        y_sb = sem("y_sb")
        y_out = [sem(f"y_out{k}") for k in range(TOPK)]
        passed = sem("e_passed")

        h_banks = [t_bank[:, 0, 0:CAP], t_bank[:, 1, 0:CAP], t_bank[:, 2, 0:CAP], s_bank[:, 2, 0:CAP]]
        NH = len(h_banks)
        y_banks = [banks[0][:, 0:DIM], banks[1][:, 0:DIM], banks[0][:, 0:DIM]]

        def program(turn, eng):
            with eng.Fori(0, E // 2 - 1) as rnd:
                for q in range(2):
                    turn(rnd, q, True, True)
            turn(E // 2 - 1, 0, True, False)
            turn(E // 2 - 1, 1, False, False)

        block = own.enter_context(nc.Block())

        def rows_of(dram, e, k):
            return dram.rearrange("(s t p) d -> s p t d", t=CT, p=P)[k * E + e]

        @block.sync
        def _(sp):
            sp.dma_start(bias[:, :], rows_to_all(ffn_bias, DIM)).then_inc(bias_in, 16)

            def load_weights(e):
                for i, w in enumerate(weight_layouts(w1, w2, e)):
                    sp.wait_ge(w_split[i], 2 * e)
                    sp.dma_start(wr[i][:, :].rearrange("p (c f) -> p c f", f=w.shape[2]), w).then_inc(w_in[i], 16)

            def load_rows(e, k):
                sp.dma_start(xr[k][:, :, :], rows_of(slot_rows, e, k)).then_inc(x_in[k], 16)

            for k in range(TOPK):
                load_rows(0, k)

            def turn(rnd, q, more, more2):
                e = 2 * rnd + q
                if more:
                    load_weights(e + 1)
                for k in range(TOPK):
                    if more:
                        sp.wait_ge(x_ps, 2 * e + k + 1)
                        load_rows(e + 1, k)
                    sp.wait_ge(y_sb, CT * (2 * e + k + 1) + 1)
                    sp.dma_start(rows_of(slot_out[0:SLOTS, :], e, k), yo[k][:, :, :]).then_inc(y_out[k], 16)

            program(turn, sp)
            for k in range(TOPK):
                sp.wait_ge(y_out[k], 16 * E + 1)

        @block.gpsimd
        def _(pool):
            def split(e, q):
                for i in range(2):
                    pool.wait_ge(w_in[i], 16 * (e + 1))
                    pool.wait_ge(w_used, e + 1)
                    pool.sem_inc(passed, 1)
                    pool.tensor_copy(wh[i][q][:, :], wr[i][:, :]).then_inc(w_split[i], 1)
                    pool.wait_ge(w_split[i], 2 * e + 1)
                    pool.tensor_tensor(wl[i][q][:, :], wr[i][:, :], wh[i][q][:, :].bitcast(F32),
                                       ALU.subtract).then_inc(w_split[i], 1)

            def turn(rnd, q, more, more2):
                if more:
                    split(2 * rnd + q + 1, 1 - q)

            program(turn, pool)

        @block.scalar
        def _(act):
            act.sem_inc(gelu_done, NH)
            act.sem_inc(y_sb, 1)
            for k in range(TOPK):
                act.sem_inc(y_out[k], 1)

            def rows(u):
                act.wait_ge(x_ps, u + 1)
                act.activation(xh[:, :, :], s_bank[:, 0:KC, 0:CAP], ACT.Copy).then_inc(xh_done, 1)

            rows(0)

            def turn(rnd, q, more, more2):
                e = 2 * rnd + q
                for k in range(TOPK):
                    u = 2 * e + k
                    for f in range(FC):
                        act.wait_ge(h_ps, FC * u + f + 1)
                        act.wait_ge(hl_done, FC * u + f + 1)
                        act.activation(h[:, f % 2, :], h_banks[f % NH], ACT.Gelu_apprx_tanh).then_inc(gelu_done, 1)
                    if more or k == 0:
                        rows(u + 1)
                    act.wait_ge(y_out[k], 16 * e + 1)
                    for t in range(CT):
                        act.wait_ge(y_ps, CT * u + t + 1)
                        act.activation(yo[k][:, t, :], y_banks[t], ACT.Copy).then_inc(y_sb, 1)

            program(turn, act)

        @block.vector
        def _(dve):
            dve.sem_inc(hl_done, 2)

            def rows(u):
                dve.wait_ge(xh_done, u + 1)
                dve.tensor_tensor(xl[:, :, :], s_bank[:, 0:KC, 0:CAP], xh[:, :, :].bitcast(F32),
                                  ALU.subtract).then_inc(xl_done, 1)

            rows(0)
            dve.wait_ge(bias_in, 16)
            for b in range(B):
                for t in range(NT):
                    dve.tensor_tensor(hid[:, b, t, :], hid[:, b, t, :], bias[:, :], ALU.add).then_inc(bias_added, 1)

            def turn(rnd, q, more, more2):
                for k in range(TOPK):
                    u = 2 * (2 * rnd + q) + k
                    for f in range(FC):
                        dve.wait_ge(gelu_done, FC * u + f + 1 + NH)
                        dve.tensor_copy(hh[:, f, :], h[:, f % 2, :]).then_inc(hh_done, 1)
                        dve.wait_ge(hh_done, FC * u + f + 1)
                        dve.tensor_tensor(hl[:, f, :], h[:, f % 2, :], hh[:, f, :].bitcast(F32),
                                          ALU.subtract).then_inc(hl_done, 1)
                    if more or k == 0:
                        rows(u + 1)

            program(turn, dve)

        @block.tensor
        def _(pe):
            pe.sem_inc(w_used, 2)

            def transpose_rows(e, k, u):
                pe.wait_ge(x_in[k], 16 * (e + 1))
                for t in range(CT):
                    for c in range(KC):
                        m = pe.transpose(s_bank[:, c, t * P:(t + 1) * P], xr[k][:, t, c * P:(c + 1) * P], ident[:, :])
                m.then_inc(x_ps, 1)

            transpose_rows(0, 0, 0)

            def turn(rnd, q, more, more2):
                e = 2 * rnd + q
                w1h, w1l = (w[0][q][:, :].rearrange("p (c f) -> p c f", c=KC) for w in (wh, wl))
                w2h, w2l = (w[1][q][:, :].rearrange("p (c d) -> p c d", c=FC) for w in (wh, wl))
                for k in range(TOPK):
                    u = 2 * e + k
                    if k == 0:
                        pe.wait_ge(w_split[0], 2 * e + 2)
                    pe.wait_ge(xl_done, u + 1)
                    for f in range(FC):
                        cols = slice(f * P, (f + 1) * P)
                        pe.wait_ge(gelu_done, FC * u + f + 1)
                        steps = [(w, xx, c) for c in range(KC) for w, xx in ((w1h, xh), (w1h, xl), (w1l, xh))]
                        for i, (w, xx, c) in enumerate(steps):
                            m = pe.matmul(h_banks[f % NH], w[:, c, cols], xx[:, c, :], start=(i == 0),
                                          stop=(i == len(steps) - 1))
                        m.then_inc(h_ps, 1)
                    if k == 0:
                        transpose_rows(e, 1, u + 1)
                        pe.wait_ge(w_split[1], 2 * e + 2)
                    elif more:
                        transpose_rows(e + 1, 0, u + 1)
                    for t in range(CT):
                        rows = slice(t * P, (t + 1) * P)
                        pe.wait_ge(y_sb, CT * u + 1 if t < 2 else CT * u + 2)
                        for f in range(FC):
                            if t == 0:
                                pe.wait_ge(hl_done, FC * u + f + 3)
                            for i, (hx, w) in enumerate(((hh, w2h), (hh, w2l), (hl, w2h))):
                                m = pe.matmul(y_banks[t], hx[:, f, rows], w[:, f, :], start=(f == 0 and i == 0),
                                              stop=(f == FC - 1 and i == 2))
                        m.then_inc(y_ps, 1)
                pe.wait_ge(y_ps, CT * (2 * e + 2))
                pe.sem_inc(w_used, 1)

            program(turn, pe)


def combine(nc, common, slot_out, pos, gate, out):
    hid = common[0]
    sb = common[-1]
    with ExitStack() as own:
        def buf(name, shape, dt=F32):
            return sb(name, shape, dt, own)

        def sem(name):
            return own.enter_context(nc.semaphore(name))

        idx = [buf(f"idx{q}", [P, NT, TOPK], I32) for q in range(2)]
        ya = [buf(f"ya{q}", [P, NT, TOPK, DIM]) for q in range(2)]
        res = [buf(f"res{q}", [P, NT, DIM]) for q in range(2)]

        idx_done = sem("idx_done")
        fetched = [sem(f"fetched{q}") for q in range(2)]
        first_done = sem("first_done")
        res_done = sem("res_done")
        stored = [sem(f"stored{q}") for q in range(2)]
        pool_passed = sem("c_pool_passed")

        block = own.enter_context(nc.Block())

        @block.gpsimd
        def _(pool):
            pool.sem_inc(res_done, 2 * NT)
            with pool.Fori(0, B // 2) as rnd:
                for q in range(2):
                    b = 2 * rnd + q
                    pool.wait_ge(idx_done, b + 1)
                    pool.wait_ge(res_done, NT * b + NT)
                    pool.sem_inc(pool_passed, 1)
                    for t in range(NT):
                        for k in range(TOPK):
                            pool.indirect_dma_start(
                                out=ya[q][:, t, k, :], out_offset=None, in_=slot_out,
                                in_offset=bass.IndirectOffsetOnAxis(ap=idx[q][:, t, k:k + 1], axis=0),
                                bounds_check=SLOTS, oob_is_err=False).then_inc(fetched[q], 16)

        @block.vector
        def _(dve):
            for q in range(2):
                dve.sem_inc(stored[q], 1)
                dve.tensor_copy(idx[q][:, :, :], pos[:, NT * q:NT * q + NT, :]).then_inc(idx_done, 1)

            def turn(rnd, q, more):
                b = 2 * rnd + q
                dve.wait_ge(fetched[q], 16 * NT * TOPK * (rnd + 1))
                if more:
                    dve.tensor_copy(idx[q][:, :, :], pos[:, bass.ds(NT * (b + 2), NT), :]).then_inc(idx_done, 1)
                dve.wait_ge(stored[q], 16 * rnd + 1)
                for t in range(NT):
                    g = gate[:, bass.ds(NT * b + t, 1), :].rearrange("p o k -> p (o k)")
                    dve.scalar_tensor_tensor(out=res[q][:, t, :], in0=ya[q][:, t, 0, :], scalar=g[:, 0:1],
                                             in1=hid[:, b, t, :], op0=ALU.mult, op1=ALU.add).then_inc(first_done, 1)
                for t in range(NT):
                    g = gate[:, bass.ds(NT * b + t, 1), :].rearrange("p o k -> p (o k)")
                    dve.wait_ge(first_done, NT * b + t + 1)
                    dve.scalar_tensor_tensor(out=res[q][:, t, :], in0=ya[q][:, t, 1, :], scalar=g[:, 1:2],
                                             in1=res[q][:, t, :], op0=ALU.mult, op1=ALU.add).then_inc(res_done, 1)

            with dve.Fori(0, B // 2 - 1) as rnd:
                for q in range(2):
                    turn(rnd, q, True)
            for q in range(2):
                turn(B // 2 - 1, q, False)

        @block.sync
        def _(sp):
            with sp.Fori(0, B // 2) as rnd:
                for q in range(2):
                    b = 2 * rnd + q
                    sp.wait_ge(res_done, NT * (b + 3))
                    sp.dma_start(out[b].rearrange("(t p) d -> p t d", p=P), res[q][:, :, :]).then_inc(stored[q], 16)
            for q in range(2):
                sp.wait_ge(stored[q], 16 * (B // 2) + 1)


_INS = ["x", "txt", "L0_tok_ccm", "L0_tok_ccm_bias", "L0_tok_shifts", "L0_tok_slopes", "L0_tok_conv_w",
        "L0_tok_conv_b", "L0_attn_W_DKV", "L0_attn_W_UK", "L0_attn_W_UV", "L0_attn_W_UQ", "L0_attn_W_O",
        "L0_ffn_router_w", "L0_ffn_w1", "L0_ffn_w2", "L0_ffn_bias"]


def kernel(**inputs):
    import concourse.bacc as _bacc
    from concourse.bass_utils import run_bass_kernel_spmd as _run

    nc = _bacc.Bacc("TRN2", target_bir_lowering=False, num_devices=1)
    arrays, args = {}, []
    for name in _INS:
        a = np.ascontiguousarray(inputs[name])
        arrays[f"in_{name}"] = a
        args.append(nc.dram_tensor(f"in_{name}", a.shape, mybir.dt.from_np(a.dtype), kind="ExternalInput").ap())
    out = nc.dram_tensor("out", (B, T, DIM), F32, kind="ExternalOutput").ap()
    build(nc, *args, out)
    return _run(nc, [arrays], core_ids=[0]).results[0]["out"]
```
